# Optimizing a Trainium2 kernel written in Bass

```python
import numpy as np
import jax
import jax.numpy as jnp

def _softmax(x, axis=-1):
    return jax.nn.softmax(x, axis=axis)
def _gelu(x):
    return jax.nn.gelu(x, approximate=True)
def _silu(x):
    return jax.nn.silu(x)
def _sigmoid(x):
    return jax.nn.sigmoid(x)
def _layernorm(x, axis=-1, eps=1e-5):
    m = jnp.mean(x, axis=axis, keepdims=True)
    v = jnp.var(x, axis=axis, keepdims=True)
    return (x - m) / jnp.sqrt(v + eps)
def _scatter_add(tgt, idx, src, axis=0):
    return tgt.at[idx].add(src)
def _segment_sum(src, seg, n):
    return jax.ops.segment_sum(src, seg, n)

kernel_name = 'mk_conv_preact_d4_conv_nhwc192_0a1067'

def setup_inputs(seed: int = 0):
    np.random.seed(seed)
    _w = jnp.asarray
    def _rec_inputs():
        import jax
        import jax.numpy as jnp
        _gk = jax.random.key(seed)
        x = 0.0002141 + 1 * jax.random.normal(jax.random.fold_in(_gk, 1), (4, 32, 32, 192), jnp.float32)
        return x
    x = _rec_inputs()
    def _L0_conv_setup():
        import jax, jax.numpy as jnp
        import numpy as np
        D_MODEL = 192
        D_STATE = 16
        D_CONV = 3
        EXPAND = 2
        D_INNER = EXPAND * D_MODEL
        DT_RANK = (D_MODEL + 15) // 16

        def _ssm_scan(u, W_x, W_dt, b_dt, A_log, D_param):
            x_dbl = u @ W_x
            dt = x_dbl[..., :DT_RANK]
            B_mat = x_dbl[..., DT_RANK:DT_RANK + D_STATE]
            C_mat = x_dbl[..., DT_RANK + D_STATE:]
            dt = jax.nn.softplus(dt @ W_dt + b_dt)
            A = -jnp.exp(A_log)
            log_dA = jnp.einsum('bld,dn->bldn', dt, A)
            dB_u = jnp.einsum('bld,bln->bldn', dt, B_mat) * u[..., None]
            log_decay = jnp.cumsum(log_dA, axis=1)
            decay = jnp.exp(log_decay)
            h = decay * jnp.cumsum(dB_u / (decay + 1e-12), axis=1)
            y = jnp.einsum('bldn,bln->bld', h, C_mat)
            return y + u * D_param
        key = jax.random.key(seed)
        ks = jax.random.split(key, 8)
        B, H, W = (4, 32, 32)
        sc = lambda n: 1.0 / np.sqrt(n)
        x = jax.random.normal(ks[0], (B, H, W, D_MODEL), jnp.float32)
        W_in = jax.random.normal(ks[1], (D_MODEL, 2 * D_INNER), jnp.float32) * sc(D_MODEL)
        conv_w = jax.random.normal(ks[2], (D_INNER, 1, D_CONV, D_CONV), jnp.float32) * sc(D_CONV * D_CONV)
        conv_b = jnp.zeros((D_INNER,), jnp.float32)
        W_x = jax.random.normal(ks[3], (D_INNER, DT_RANK + 2 * D_STATE), jnp.float32) * sc(D_INNER)
        W_dt = jax.random.normal(ks[4], (DT_RANK, D_INNER), jnp.float32) * sc(DT_RANK)
        b_dt = jnp.zeros((D_INNER,), jnp.float32)
        A_log = jnp.log(jnp.tile(jnp.arange(1, D_STATE + 1, dtype=jnp.float32), (D_INNER, 1)))
        D_param = jnp.ones((D_INNER,), jnp.float32)
        W_out = jax.random.normal(ks[5], (D_INNER, D_MODEL), jnp.float32) * sc(D_INNER)
        gamma = jnp.ones((D_INNER,), jnp.float32)
        beta = jnp.zeros((D_INNER,), jnp.float32)
        return {'x': x, 'W_in': W_in, 'conv_w': conv_w, 'conv_b': conv_b, 'W_x': W_x, 'W_dt': W_dt, 'b_dt': b_dt, 'A_log': A_log, 'D_param': D_param, 'W_out': W_out, 'gamma': gamma, 'beta': beta}
    _L0_conv_all = _L0_conv_setup()
    _L0_conv_in = {k: v for k, v in _L0_conv_all.items() if k in ('W_in', 'conv_w', 'conv_b', 'W_x', 'W_dt', 'b_dt', 'A_log', 'D_param', 'W_out', 'gamma', 'beta', )}
    del _L0_conv_all

    def _L1_conv_setup():
        import jax, jax.numpy as jnp
        import numpy as np
        from jax import lax
        B, H, W, C = (32, 56, 56, 192)
        EXP = 4 * C
        EPS = 1e-06
        LAYER_SCALE_INIT = 1e-06
        key = jax.random.key(seed)
        ks = jax.random.split(key, 6)
        x = jax.random.normal(ks[0], (B, H, W, C), dtype=jnp.float32)
        dw_kernel = jax.random.normal(ks[1], (7, 7, 1, C), dtype=jnp.float32) * 0.2
        dw_bias = jnp.zeros((C,), dtype=jnp.float32)
        ln_gamma = jnp.ones((C,), dtype=jnp.float32)
        ln_beta = jnp.zeros((C,), dtype=jnp.float32)
        w0 = jax.random.normal(ks[2], (C, EXP), dtype=jnp.float32) * 0.2
        b0 = jnp.zeros((EXP,), dtype=jnp.float32)
        w1 = jax.random.normal(ks[3], (EXP, C), dtype=jnp.float32) * 0.2
        b1 = jnp.zeros((C,), dtype=jnp.float32)
        gamma = jnp.full((C,), LAYER_SCALE_INIT, dtype=jnp.float32)
        return {'x': x, 'dw_kernel': dw_kernel, 'dw_bias': dw_bias, 'ln_gamma': ln_gamma, 'ln_beta': ln_beta, 'w0': w0, 'b0': b0, 'w1': w1, 'b1': b1, 'gamma': gamma}
    _L1_conv_all = _L1_conv_setup()
    _L1_conv_in = {k: v for k, v in _L1_conv_all.items() if k in ('dw_kernel', 'dw_bias', 'ln_gamma', 'ln_beta', 'w0', 'b0', 'w1', 'b1', 'gamma', )}
    del _L1_conv_all

    def _L2_conv_setup():
        import jax, jax.numpy as jnp
        import numpy as np
        GROUP = 12
        _NEI = np.array([[2, 1], [1, 2], [0, 2], [0, 1], [1, 0], [2, 0]])

        def _d6_tables():
            k = np.arange(GROUP) % 6
            s = np.arange(GROUP) // 6
            sign = np.where(s == 0, 1, -1)
            act = (k[:, None] + sign[:, None] * np.arange(6)[None, :]) % 6
            mk = (k[:, None] + sign[:, None] * k[None, :]) % 6
            ms = s[:, None] ^ s[None, :]
            mult = mk + 6 * ms
            return (act, mult)

        def _expand_kernel_deep(kernel):
            act, mult = _d6_tables()
            C, F = (kernel.shape[2], kernel.shape[3])
            posy = np.empty((GROUP, 7), np.int32)
            posx = np.empty((GROUP, 7), np.int32)
            posy[:, 0] = 1
            posx[:, 0] = 1
            posy[:, 1:] = _NEI[act][:, :, 0]
            posx[:, 1:] = _NEI[act][:, :, 1]
            gg, tt, hh = np.meshgrid(np.arange(GROUP), np.arange(7), np.arange(GROUP), indexing='ij')
            Y, X = (posy[gg, tt], posx[gg, tt])
            H2 = mult[gg, hh]
            Ke = jnp.zeros((3, 3, GROUP, C, GROUP, F), kernel.dtype)
            Ke = Ke.at[Y, X, H2, :, gg, :].set(kernel[tt, hh])
            return Ke.reshape(3, 3, GROUP * C, GROUP * F)
        key = jax.random.key(seed)
        k1, k2 = jax.random.split(key)
        B, H, W, C, F = (16, 96, 96, 16, 16)
        x = jax.random.normal(k1, (B, H, W, GROUP * C), dtype=jnp.float32)
        kernel = jax.random.normal(k2, (7, GROUP, C, F), dtype=jnp.float32) * 0.05
        return {'x': x, 'kernel': kernel}
    _L2_conv_all = _L2_conv_setup()
    _L2_conv_in = {k: v for k, v in _L2_conv_all.items() if k in ('kernel', )}
    del _L2_conv_all

    def _L3_conv_setup():
        import jax, jax.numpy as jnp
        import numpy as np
        D_MODEL = 192
        D_STATE = 64
        D_CONV = 3
        EXPAND = 2
        HEADDIM = 128
        NGROUPS = 1
        CHUNK = 256
        D_INNER = EXPAND * D_MODEL
        NHEADS = D_INNER // HEADDIM
        CONV_DIM = D_INNER + 2 * NGROUPS * D_STATE
        D_IN_PROJ = 2 * D_INNER + 2 * NGROUPS * D_STATE + NHEADS
        BATCH, HIMG, WIMG = (4, 64, 64)

        def _segsum(a):
            T = a.shape[-1]
            cs = jnp.cumsum(a, axis=-1)
            d = cs[..., :, None] - cs[..., None, :]
            mask = jnp.tril(jnp.ones((T, T), bool))
            return jnp.where(mask, d, -jnp.inf)

        def _ssd(X, dA, Bm, Cm, chunk):
            b, l, h, p = X.shape
            g, n = (Bm.shape[2], Bm.shape[3])
            nc = l // chunk
            Xc = X.reshape(b, nc, chunk, h, p)
            Ac = dA.reshape(b, nc, chunk, h).transpose(0, 3, 1, 2)
            rep = h // g
            Bh = jnp.repeat(Bm.reshape(b, nc, chunk, g, n), rep, axis=3)
            Ch = jnp.repeat(Cm.reshape(b, nc, chunk, g, n), rep, axis=3)
            A_cum = jnp.cumsum(Ac, axis=-1)
            Lmat = jnp.exp(_segsum(Ac))
            Y_diag = jnp.einsum('bclhn,bcshn,bhcls,bcshp->bclhp', Ch, Bh, Lmat, Xc)
            decay_states = jnp.exp(A_cum[..., -1:] - A_cum)
            states = jnp.einsum('bclhn,bhcl,bclhp->bchpn', Bh, decay_states, Xc)
            A_last = jnp.pad(A_cum[..., -1], ((0, 0), (0, 0), (1, 0)))
            decay_chunk = jnp.exp(_segsum(A_last))
            states_cat = jnp.concatenate([jnp.zeros_like(states[:, :1]), states], axis=1)
            prev = jnp.einsum('bhzc,bchpn->bzhpn', decay_chunk, states_cat)[:, :-1]
            Y_off = jnp.einsum('bclhn,bchpn,bhcl->bclhp', Ch, prev, jnp.exp(A_cum))
            return (Y_diag + Y_off).reshape(b, l, h, p)

        def _forward(x, in_proj_w, conv_w, conv_b, dt_bias, A_log, Ds, norm_w, out_proj_w):
            B, H, W, _ = x.shape
            L = H * W
            zxbcdt = x @ in_proj_w.T
            z = zxbcdt[..., :D_INNER]
            xBC = zxbcdt[..., D_INNER:D_INNER + CONV_DIM]
            dt = zxbcdt[..., D_INNER + CONV_DIM:]
            xBC = xBC.transpose(0, 3, 1, 2)
            pad = (D_CONV - 1) // 2
            xBC = jax.lax.conv_general_dilated(xBC, conv_w, (1, 1), [(pad, pad), (pad, pad)], feature_group_count=CONV_DIM)
            xBC = xBC + conv_b[None, :, None, None]
            xBC = xBC * jax.nn.sigmoid(xBC)
            dts = jax.nn.softplus(dt + dt_bias).reshape(B, L, NHEADS)
            x_hw = xBC.reshape(B, CONV_DIM, L)
            x_wh = xBC.transpose(0, 1, 3, 2).reshape(B, CONV_DIM, L)
            xBC_hwwh = jnp.stack([x_hw, x_wh], axis=1)
            xBCs = jnp.concatenate([xBC_hwwh, jnp.flip(xBC_hwwh, axis=-1)], axis=1)
            xs = xBCs[:, :, :D_INNER].reshape(B, 4 * D_INNER, L).transpose(0, 2, 1)
            Bs = xBCs[:, :, D_INNER:D_INNER + NGROUPS * D_STATE].transpose(0, 3, 1, 2).reshape(B, L, 4 * NGROUPS * D_STATE)
            Cs = xBCs[:, :, D_INNER + NGROUPS * D_STATE:].transpose(0, 3, 1, 2).reshape(B, L, 4 * NGROUPS * D_STATE)
            heads = 4 * NHEADS
            Xh = xs.reshape(B, L, heads, HEADDIM)
            dts_full = jnp.tile(dts, (1, 1, 4))
            As = -jnp.exp(A_log)
            Bg = Bs.reshape(B, L, NGROUPS, 4 * D_STATE)
            Cg = Cs.reshape(B, L, NGROUPS, 4 * D_STATE)
            out_y = _ssd(Xh * dts_full[..., None], dts_full * As[None, None, :], Bg, Cg, CHUNK)
            out_y = out_y + Ds[None, None, :, None] * Xh
            out_y = out_y.reshape(B, L, 4, D_INNER).transpose(0, 2, 3, 1)
            inv_y = jnp.flip(out_y[:, 2:4], axis=-1)
            wh_y = out_y[:, 1].reshape(B, D_INNER, W, H).transpose(0, 1, 3, 2).reshape(B, D_INNER, L)
            invwh_y = inv_y[:, 1].reshape(B, D_INNER, W, H).transpose(0, 1, 3, 2).reshape(B, D_INNER, L)
            y = out_y[:, 0] + inv_y[:, 0] + wh_y + invwh_y
            y = y.transpose(0, 2, 1).reshape(B, H, W, D_INNER)
            y = y * jax.nn.silu(z)
            y = y * jax.lax.rsqrt(jnp.mean(y * y, axis=-1, keepdims=True) + 1e-05) * norm_w
            return y @ out_proj_w.T
        key = jax.random.key(seed)
        ks = jax.random.split(key, 8)
        x = jax.random.normal(ks[0], (BATCH, HIMG, WIMG, D_MODEL), jnp.float32)
        in_proj_w = jax.random.normal(ks[1], (D_IN_PROJ, D_MODEL), jnp.float32) * D_MODEL ** (-0.5)
        conv_w = jax.random.normal(ks[2], (CONV_DIM, 1, D_CONV, D_CONV), jnp.float32) * (1.0 / D_CONV)
        conv_b = jax.random.normal(ks[3], (CONV_DIM,), jnp.float32) * 0.01
        dt = jnp.exp(jax.random.uniform(ks[4], (NHEADS,)) * (np.log(0.1) - np.log(0.001)) + np.log(0.001))
        dt_bias = (dt + jnp.log(-jnp.expm1(-dt))).astype(jnp.float32)
        A = jax.random.uniform(ks[5], (NHEADS,), minval=1.0, maxval=16.0)
        A_log = jnp.tile(jnp.log(A), 4).astype(jnp.float32)
        Ds = jnp.ones((4 * NHEADS,), jnp.float32)
        norm_w = jnp.ones((D_INNER,), jnp.float32)
        out_proj_w = jax.random.normal(ks[6], (D_MODEL, D_INNER), jnp.float32) * D_INNER ** (-0.5)
        return dict(x=x, in_proj_w=in_proj_w, conv_w=conv_w, conv_b=conv_b, dt_bias=dt_bias, A_log=A_log, Ds=Ds, norm_w=norm_w, out_proj_w=out_proj_w)
    _L3_conv_all = _L3_conv_setup()
    _L3_conv_in = {k: v for k, v in _L3_conv_all.items() if k in ('in_proj_w', 'conv_w', 'conv_b', 'dt_bias', 'A_log', 'Ds', 'norm_w', 'out_proj_w', )}
    del _L3_conv_all

    return {
        "x": x,
        "L0_conv_W_in": _L0_conv_in["W_in"],
        "L0_conv_conv_w": _L0_conv_in["conv_w"],
        "L0_conv_conv_b": _L0_conv_in["conv_b"],
        "L0_conv_W_x": _L0_conv_in["W_x"],
        "L0_conv_W_dt": _L0_conv_in["W_dt"],
        "L0_conv_b_dt": _L0_conv_in["b_dt"],
        "L0_conv_A_log": _L0_conv_in["A_log"],
        "L0_conv_D_param": _L0_conv_in["D_param"],
        "L0_conv_W_out": _L0_conv_in["W_out"],
        "L0_conv_gamma": _L0_conv_in["gamma"],
        "L0_conv_beta": _L0_conv_in["beta"],
        "L1_conv_dw_kernel": _L1_conv_in["dw_kernel"],
        "L1_conv_dw_bias": _L1_conv_in["dw_bias"],
        "L1_conv_ln_gamma": _L1_conv_in["ln_gamma"],
        "L1_conv_ln_beta": _L1_conv_in["ln_beta"],
        "L1_conv_w0": _L1_conv_in["w0"],
        "L1_conv_b0": _L1_conv_in["b0"],
        "L1_conv_w1": _L1_conv_in["w1"],
        "L1_conv_b1": _L1_conv_in["b1"],
        "L1_conv_gamma": _L1_conv_in["gamma"],
        "L2_conv_kernel": _L2_conv_in["kernel"],
        "L3_conv_in_proj_w": _L3_conv_in["in_proj_w"],
        "L3_conv_conv_w": _L3_conv_in["conv_w"],
        "L3_conv_conv_b": _L3_conv_in["conv_b"],
        "L3_conv_dt_bias": _L3_conv_in["dt_bias"],
        "L3_conv_A_log": _L3_conv_in["A_log"],
        "L3_conv_Ds": _L3_conv_in["Ds"],
        "L3_conv_norm_w": _L3_conv_in["norm_w"],
        "L3_conv_out_proj_w": _L3_conv_in["out_proj_w"],
    }

def reference(x, L0_conv_W_in, L0_conv_conv_w, L0_conv_conv_b, L0_conv_W_x, L0_conv_W_dt, L0_conv_b_dt, L0_conv_A_log, L0_conv_D_param, L0_conv_W_out, L0_conv_gamma, L0_conv_beta, L1_conv_dw_kernel, L1_conv_dw_bias, L1_conv_ln_gamma, L1_conv_ln_beta, L1_conv_w0, L1_conv_b0, L1_conv_w1, L1_conv_b1, L1_conv_gamma, L2_conv_kernel, L3_conv_in_proj_w, L3_conv_conv_w, L3_conv_conv_b, L3_conv_dt_bias, L3_conv_A_log, L3_conv_Ds, L3_conv_norm_w, L3_conv_out_proj_w):
    import jax
    import jax.numpy as jnp
    def _L0_conv_ref(x, W_in, conv_w, conv_b, W_x, W_dt, b_dt, A_log, D_param, W_out, gamma, beta):
        import jax, jax.numpy as jnp
        import numpy as np
        D_MODEL = 192
        D_STATE = 16
        D_CONV = 3
        EXPAND = 2
        D_INNER = EXPAND * D_MODEL
        DT_RANK = (D_MODEL + 15) // 16

        def _ssm_scan(u, W_x, W_dt, b_dt, A_log, D_param):
            x_dbl = u @ W_x
            dt = x_dbl[..., :DT_RANK]
            B_mat = x_dbl[..., DT_RANK:DT_RANK + D_STATE]
            C_mat = x_dbl[..., DT_RANK + D_STATE:]
            dt = jax.nn.softplus(dt @ W_dt + b_dt)
            A = -jnp.exp(A_log)
            log_dA = jnp.einsum('bld,dn->bldn', dt, A)
            dB_u = jnp.einsum('bld,bln->bldn', dt, B_mat) * u[..., None]
            log_decay = jnp.cumsum(log_dA, axis=1)
            decay = jnp.exp(log_decay)
            h = decay * jnp.cumsum(dB_u / (decay + 1e-12), axis=1)
            y = jnp.einsum('bldn,bln->bld', h, C_mat)
            return y + u * D_param
        B, H, W, C = x.shape
        xz = x @ W_in
        x_val, z = (xz[..., :D_INNER], xz[..., D_INNER:])
        xc = jnp.transpose(x_val, (0, 3, 1, 2))
        xc = jax.lax.conv_general_dilated(xc, conv_w, window_strides=(1, 1), padding='SAME', feature_group_count=D_INNER, dimension_numbers=('NCHW', 'OIHW', 'NCHW'))
        xc = xc + conv_b[None, :, None, None]
        xc = jax.nn.silu(xc)
        xv = jnp.transpose(xc, (0, 2, 3, 1))
        scan = lambda u: _ssm_scan(u, W_x, W_dt, b_dt, A_log, D_param)
        s1 = xv.reshape(B, H * W, D_INNER)
        s2 = s1[:, ::-1]
        s3 = jnp.transpose(xv, (0, 2, 1, 3)).reshape(B, W * H, D_INNER)
        s4 = s3[:, ::-1]
        y1 = scan(s1)
        y2 = scan(s2)[:, ::-1]
        y3 = scan(s3)
        y4 = scan(s4)[:, ::-1]
        y3 = jnp.transpose(y3.reshape(B, W, H, D_INNER), (0, 2, 1, 3)).reshape(B, H * W, D_INNER)
        y4 = jnp.transpose(y4.reshape(B, W, H, D_INNER), (0, 2, 1, 3)).reshape(B, H * W, D_INNER)
        y = y1 + y2 + y3 + y4
        mu = jnp.mean(y, axis=-1, keepdims=True)
        var = jnp.mean(jnp.square(y - mu), axis=-1, keepdims=True)
        y = (y - mu) * jax.lax.rsqrt(var + 1e-05) * gamma + beta
        y = y.reshape(B, H, W, D_INNER) * jax.nn.silu(z)
        return y @ W_out

    def _L1_conv_ref(x, dw_kernel, dw_bias, ln_gamma, ln_beta, w0, b0, w1, b1, gamma):
        import jax, jax.numpy as jnp
        import numpy as np
        from jax import lax
        B, H, W, C = (32, 56, 56, 192)
        EXP = 4 * C
        EPS = 1e-06
        LAYER_SCALE_INIT = 1e-06
        c = dw_kernel.shape[-1]
        y = lax.conv_general_dilated(x, dw_kernel, window_strides=(1, 1), padding='SAME', dimension_numbers=('NHWC', 'HWIO', 'NHWC'), feature_group_count=c) + dw_bias
        mu = jnp.mean(y, axis=-1, keepdims=True)
        var = jnp.mean(jnp.square(y - mu), axis=-1, keepdims=True)
        y = (y - mu) * lax.rsqrt(var + EPS) * ln_gamma + ln_beta
        y = jnp.einsum('bhwc,cd->bhwd', y, w0) + b0
        y = jax.nn.gelu(y, approximate=False)
        y = jnp.einsum('bhwd,dc->bhwc', y, w1) + b1
        return y * gamma

    def _L2_conv_ref(x, kernel):
        import jax, jax.numpy as jnp
        import numpy as np
        GROUP = 12
        _NEI = np.array([[2, 1], [1, 2], [0, 2], [0, 1], [1, 0], [2, 0]])

        def _d6_tables():
            k = np.arange(GROUP) % 6
            s = np.arange(GROUP) // 6
            sign = np.where(s == 0, 1, -1)
            act = (k[:, None] + sign[:, None] * np.arange(6)[None, :]) % 6
            mk = (k[:, None] + sign[:, None] * k[None, :]) % 6
            ms = s[:, None] ^ s[None, :]
            mult = mk + 6 * ms
            return (act, mult)

        def _expand_kernel_deep(kernel):
            act, mult = _d6_tables()
            C, F = (kernel.shape[2], kernel.shape[3])
            posy = np.empty((GROUP, 7), np.int32)
            posx = np.empty((GROUP, 7), np.int32)
            posy[:, 0] = 1
            posx[:, 0] = 1
            posy[:, 1:] = _NEI[act][:, :, 0]
            posx[:, 1:] = _NEI[act][:, :, 1]
            gg, tt, hh = np.meshgrid(np.arange(GROUP), np.arange(7), np.arange(GROUP), indexing='ij')
            Y, X = (posy[gg, tt], posx[gg, tt])
            H2 = mult[gg, hh]
            Ke = jnp.zeros((3, 3, GROUP, C, GROUP, F), kernel.dtype)
            Ke = Ke.at[Y, X, H2, :, gg, :].set(kernel[tt, hh])
            return Ke.reshape(3, 3, GROUP * C, GROUP * F)
        Ke = _expand_kernel_deep(kernel)
        out = jax.lax.conv_general_dilated(x, Ke, window_strides=(1, 1), padding='SAME', dimension_numbers=('NHWC', 'HWIO', 'NHWC'))
        return out

    def _L3_conv_ref(x, in_proj_w, conv_w, conv_b, dt_bias, A_log, Ds, norm_w, out_proj_w):
        import jax, jax.numpy as jnp
        import numpy as np
        D_MODEL = 192
        D_STATE = 64
        D_CONV = 3
        EXPAND = 2
        HEADDIM = 128
        NGROUPS = 1
        CHUNK = 256
        D_INNER = EXPAND * D_MODEL
        NHEADS = D_INNER // HEADDIM
        CONV_DIM = D_INNER + 2 * NGROUPS * D_STATE
        D_IN_PROJ = 2 * D_INNER + 2 * NGROUPS * D_STATE + NHEADS
        BATCH, HIMG, WIMG = (4, 64, 64)

        def _segsum(a):
            T = a.shape[-1]
            cs = jnp.cumsum(a, axis=-1)
            d = cs[..., :, None] - cs[..., None, :]
            mask = jnp.tril(jnp.ones((T, T), bool))
            return jnp.where(mask, d, -jnp.inf)

        def _ssd(X, dA, Bm, Cm, chunk):
            b, l, h, p = X.shape
            g, n = (Bm.shape[2], Bm.shape[3])
            nc = l // chunk
            Xc = X.reshape(b, nc, chunk, h, p)
            Ac = dA.reshape(b, nc, chunk, h).transpose(0, 3, 1, 2)
            rep = h // g
            Bh = jnp.repeat(Bm.reshape(b, nc, chunk, g, n), rep, axis=3)
            Ch = jnp.repeat(Cm.reshape(b, nc, chunk, g, n), rep, axis=3)
            A_cum = jnp.cumsum(Ac, axis=-1)
            Lmat = jnp.exp(_segsum(Ac))
            Y_diag = jnp.einsum('bclhn,bcshn,bhcls,bcshp->bclhp', Ch, Bh, Lmat, Xc)
            decay_states = jnp.exp(A_cum[..., -1:] - A_cum)
            states = jnp.einsum('bclhn,bhcl,bclhp->bchpn', Bh, decay_states, Xc)
            A_last = jnp.pad(A_cum[..., -1], ((0, 0), (0, 0), (1, 0)))
            decay_chunk = jnp.exp(_segsum(A_last))
            states_cat = jnp.concatenate([jnp.zeros_like(states[:, :1]), states], axis=1)
            prev = jnp.einsum('bhzc,bchpn->bzhpn', decay_chunk, states_cat)[:, :-1]
            Y_off = jnp.einsum('bclhn,bchpn,bhcl->bclhp', Ch, prev, jnp.exp(A_cum))
            return (Y_diag + Y_off).reshape(b, l, h, p)

        def _forward(x, in_proj_w, conv_w, conv_b, dt_bias, A_log, Ds, norm_w, out_proj_w):
            B, H, W, _ = x.shape
            L = H * W
            zxbcdt = x @ in_proj_w.T
            z = zxbcdt[..., :D_INNER]
            xBC = zxbcdt[..., D_INNER:D_INNER + CONV_DIM]
            dt = zxbcdt[..., D_INNER + CONV_DIM:]
            xBC = xBC.transpose(0, 3, 1, 2)
            pad = (D_CONV - 1) // 2
            xBC = jax.lax.conv_general_dilated(xBC, conv_w, (1, 1), [(pad, pad), (pad, pad)], feature_group_count=CONV_DIM)
            xBC = xBC + conv_b[None, :, None, None]
            xBC = xBC * jax.nn.sigmoid(xBC)
            dts = jax.nn.softplus(dt + dt_bias).reshape(B, L, NHEADS)
            x_hw = xBC.reshape(B, CONV_DIM, L)
            x_wh = xBC.transpose(0, 1, 3, 2).reshape(B, CONV_DIM, L)
            xBC_hwwh = jnp.stack([x_hw, x_wh], axis=1)
            xBCs = jnp.concatenate([xBC_hwwh, jnp.flip(xBC_hwwh, axis=-1)], axis=1)
            xs = xBCs[:, :, :D_INNER].reshape(B, 4 * D_INNER, L).transpose(0, 2, 1)
            Bs = xBCs[:, :, D_INNER:D_INNER + NGROUPS * D_STATE].transpose(0, 3, 1, 2).reshape(B, L, 4 * NGROUPS * D_STATE)
            Cs = xBCs[:, :, D_INNER + NGROUPS * D_STATE:].transpose(0, 3, 1, 2).reshape(B, L, 4 * NGROUPS * D_STATE)
            heads = 4 * NHEADS
            Xh = xs.reshape(B, L, heads, HEADDIM)
            dts_full = jnp.tile(dts, (1, 1, 4))
            As = -jnp.exp(A_log)
            Bg = Bs.reshape(B, L, NGROUPS, 4 * D_STATE)
            Cg = Cs.reshape(B, L, NGROUPS, 4 * D_STATE)
            out_y = _ssd(Xh * dts_full[..., None], dts_full * As[None, None, :], Bg, Cg, CHUNK)
            out_y = out_y + Ds[None, None, :, None] * Xh
            out_y = out_y.reshape(B, L, 4, D_INNER).transpose(0, 2, 3, 1)
            inv_y = jnp.flip(out_y[:, 2:4], axis=-1)
            wh_y = out_y[:, 1].reshape(B, D_INNER, W, H).transpose(0, 1, 3, 2).reshape(B, D_INNER, L)
            invwh_y = inv_y[:, 1].reshape(B, D_INNER, W, H).transpose(0, 1, 3, 2).reshape(B, D_INNER, L)
            y = out_y[:, 0] + inv_y[:, 0] + wh_y + invwh_y
            y = y.transpose(0, 2, 1).reshape(B, H, W, D_INNER)
            y = y * jax.nn.silu(z)
            y = y * jax.lax.rsqrt(jnp.mean(y * y, axis=-1, keepdims=True) + 1e-05) * norm_w
            return y @ out_proj_w.T
        return _forward(x, in_proj_w, conv_w, conv_b, dt_bias, A_log, Ds, norm_w, out_proj_w)

    def _gn(v, G=32, eps=1e-5):
        B_, H_, W_, C_ = v.shape
        g = v.reshape(B_, H_, W_, G, C_ // G)
        m = jnp.mean(g, axis=(1, 2, 4), keepdims=True)
        s = jnp.var(g, axis=(1, 2, 4), keepdims=True)
        return ((g - m) / jnp.sqrt(s + eps)).reshape(v.shape)

    def _ln_c(v, eps=1e-6):
        m = jnp.mean(v, axis=-1, keepdims=True)
        s = jnp.var(v, axis=-1, keepdims=True)
        return (v - m) / jnp.sqrt(s + eps)

    def _ln_t(v, eps=1e-5):
        m = jnp.mean(v, axis=-1, keepdims=True)
        s = jnp.var(v, axis=-1, keepdims=True)
        return (v - m) / jnp.sqrt(s + eps)

    def _to_tokens(v):
        B_, H_, W_, C_ = v.shape
        return v.reshape(B_, H_ * W_, C_)
    def _from_tokens(t, like):
        return t.reshape(like.shape)

    x = x + _L0_conv_ref(_gn(x), L0_conv_W_in, L0_conv_conv_w, L0_conv_conv_b, L0_conv_W_x, L0_conv_W_dt, L0_conv_b_dt, L0_conv_A_log, L0_conv_D_param, L0_conv_W_out, L0_conv_gamma, L0_conv_beta)
    x = x + _L1_conv_ref(_gn(x), L1_conv_dw_kernel, L1_conv_dw_bias, L1_conv_ln_gamma, L1_conv_ln_beta, L1_conv_w0, L1_conv_b0, L1_conv_w1, L1_conv_b1, L1_conv_gamma)
    x = x + _L2_conv_ref(_gn(x), L2_conv_kernel)
    x = x + _L3_conv_ref(_gn(x), L3_conv_in_proj_w, L3_conv_conv_w, L3_conv_conv_b, L3_conv_dt_bias, L3_conv_A_log, L3_conv_Ds, L3_conv_norm_w, L3_conv_out_proj_w)
    return x


_drawn_inputs = setup_inputs


def setup_inputs(seed=0):
    import zlib

    import numpy as np

    out = dict(_drawn_inputs(seed))
    spreads = {'L0_conv_conv_b': (0.0, 0.1),
     'L0_conv_b_dt': (0.0, 0.8),
     'L0_conv_D_param': (1.0, 0.2),
     'L0_conv_gamma': (1.0, 0.2),
     'L0_conv_beta': (0.0, 0.1),
     'L1_conv_dw_bias': (0.0, 2.0),
     'L1_conv_ln_gamma': (1.0, 0.6),
     'L1_conv_ln_beta': (0.0, 2.0),
     'L1_conv_b0': (0.0, 2.0),
     'L1_conv_b1': (0.0, 2.0),
     'L1_conv_gamma': (9.999999974752427e-07, 0.6),
     'L3_conv_Ds': (1.0, 0.6),
     'L3_conv_norm_w': (1.0, 0.2)}
    factors = {'L0_conv_W_x': 6.13,
     'L0_conv_W_dt': 8.0,
     'L0_conv_A_log': 8.0,
     'L1_conv_dw_kernel': 64.0,
     'L1_conv_w0': 64.0,
     'L1_conv_w1': 64.0,
     'L3_conv_conv_b': 8.0,
     'L3_conv_A_log': 22.248}
    for name, (base, spread) in spreads.items():
        noise = np.random.default_rng([zlib.crc32(name.encode()), seed]).standard_normal(out[name].shape)
        drawn = base * np.exp(spread * noise) if base else spread * noise
        out[name] = jnp.asarray(drawn.astype(out[name].dtype))
    for name, factor in factors.items():
        out[name] = (out[name] * factor).astype(out[name].dtype)
    return out
```

```python
from contextlib import ExitStack

import concourse.bass as bass
from concourse import mybir

F32 = mybir.dt.float32
BF16 = mybir.dt.bfloat16
U32 = mybir.dt.uint32
ALU = mybir.AluOpType
ACT = mybir.ActivationFunctionType
AX_X = mybir.AxisListType.X

NB, SIDE, C = 4, 32, 192
T = SIDE * SIDE
HALF = 512
CP = 96
CB = C // CP
DI, DB = 384, 3
NS = 16
RANK = 12
MLP, MB = 768, 6
K1 = 7
P3, P7 = SIDE + 2, SIDE + K1 - 1
HD, ND = 3, 4
SB = T // 128
GUARD = 27.631021115928547
TAPS2 = [(y, x) for y in range(3) for x in range(3) if (y, x) not in ((0, 0), (2, 2))]
TRI = [sum(T - 128 * i for i in range(s)) for s in range(SB + 1)]
LAYERS = 4


class Steps:

    def __init__(self, eng, sem, per_image, image):
        self.eng, self.sem, self.per, self.image, self.n = eng, sem, per_image, image, 0

    def done(self, ins):
        ins.then_inc(self.sem, 1)
        self.n += 1
        self.eng.wait_ge(self.sem, self.image * self.per + self.n)

    def end(self):
        assert self.n == self.per, (self.sem, self.n)


ACT_STEPS, DVE_STEPS, STAGES = 4, 238, 9


def build(nc, x, win, conv0, small0, alog0, wx, wdt, wout, dw1, small1, w0, b0, w1, ke,
          win3, conv3, small3, wz3, wout3, ident, group, tri, onehot, out):
    with ExitStack() as ctx:
        def sb(name, shape, dt=F32):
            return ctx.enter_context(nc.sbuf_tensor(name, shape, dt))

        def sem(name):
            return ctx.enter_context(nc.semaphore(name))

        WIN = sb("WIN", [CP, CB, 2 * DI])
        CONV0 = sb("CONV0", [128, DB, 9])
        SMALL0 = sb("SMALL0", [128, 5, DB])
        D4 = sb("D4", [128, DB])
        A0 = sb("A0", [128, DB * NS])
        WX = sb("WX", [128, DB, RANK + 2 * NS])
        WDT = sb("WDT", [RANK, DI])
        WOUT = sb("WOUT", [128, DB, C])
        IDENT = sb("IDENT", [128, 128])
        GROUP = sb("GROUP", [CP, CP])
        TRIM = sb("TRIM", [128, 128])
        ONES = sb("ONES", [128, 128])
        ONEHOT = sb("ONEHOT", [3 * 2 * NS, 2 * NS, 128], BF16)
        GCOL = sb("GCOL", [128, 1])
        EPS5 = sb("EPS5", [128, 1])
        EPS6 = sb("EPS6", [128, 1])
        SMALL3 = sb("SMALL3", [128, 5 + HD + 12 + 12 + DB])
        CONV3 = sb("CONV3", [128, 5, 9])
        A3 = sb("A3", [128, 12])
        DSUM = sb("DSUM", [128, HD])
        SMALL1 = sb("SMALL1", [CP, 5, CB])
        DW1 = sb("DW1", [CP, CB, K1 * K1])
        B0 = sb("B0", [128, MB])
        X = sb("X", [CP, CB, T])
        XN = sb("XN", [CP, CB, T])
        ST = sb("ST", [CP, CB, 2, 6])
        MV = sb("MV", [CP, CB, 2])
        GS = sb("GS", [CP, CB, 2])
        GM = sb("GM", [CP, CB, 2])
        GV = sb("GV", [CP, CB, 2])
        ARENA = sb("ARENA", [128, 42600])

        def area(at, n, p=128):
            return ARENA[0:p, at:at + n]

        DTU = area(0, 3 * T).rearrange("p (d t) -> p d t", d=DB)
        DTUX = area(0, 4 * T).rearrange("p (d t) -> p d t", d=DB + 1)
        U = area(3072, 3 * T).rearrange("p (d t) -> p d t", d=DB)
        DT = area(6144, 3 * T).rearrange("p (d t) -> p d t", d=DB)
        S = area(9216, 12 * T).rearrange("p (d k t) -> p d k t", d=DB, k=4)
        DEC = area(21504, 8 * T).rearrange("p (s o t) -> p s o t", s=4, o=2)
        RING = area(29696, 8 * T).rearrange("p (s t) -> p s t", s=8)
        NUM = area(37888, 2 * T).rearrange("p (s t) -> p s t", s=2)
        CM = area(39936, T)
        CS = area(40960, T)
        BCS = area(41984, T // 2, 96).bitcast(BF16)
        PADX = area(9216, DB * P3 * P3).rearrange("p (d h w) -> p d h w", d=DB, h=P3)
        SPA = [area(21504 + i * 3072, 3072) for i in range(5)]
        DTR = area(37888, T, RANK)
        BCF = area(38912, T, 2 * NS)
        BCH = area(39936, T // 2, 2 * NS).bitcast(BF16)
        Y0 = DTU
        SQ0 = area(9216, 3 * T)
        Z0 = area(12288, 3 * T).rearrange("p (d t) -> p d t", d=DB)
        R0 = area(15360, T)
        W0 = area(33400, CB * MLP, CP).rearrange("p (c n) -> p c n", c=CB)
        W1 = area(34936, MB * C).rearrange("p (m n) -> p m n", m=MB)
        KE = area(36088, CB * 7 * C, CP).rearrange("p (c k n) -> p c k n", c=CB, k=7)
        WIN3 = area(38776, CB * 1024, CP).rearrange("p (c n) -> p c n", c=CB)
        WZ3 = area(40824, CB * DI, CP).rearrange("p (c n) -> p c n", c=CB)
        WOUT3 = area(41592, DB * C).rearrange("p (d n) -> p d n", d=DB)
        PAD1 = area(0, CB * P7 * P7, CP).rearrange("p (c h w) -> p c h w", c=CB, h=P7)
        Y1 = area(2888, CB * T, CP).rearrange("p (c t) -> p c t", c=CB)
        SQ1 = area(4936, CB * T, CP)
        R1 = area(6984, T, CP)
        G1 = area(8008, MB * T).rearrange("p (m t) -> p m t", m=MB)
        O1 = area(4936, CB * T, CP).rearrange("p (c t) -> p c t", c=CB)
        PAD2 = area(0, CB * P3 * P3, CP).rearrange("p (c h w) -> p c h w", c=CB, h=P3)
        XC = area(0, 3 * T).rearrange("p (d t) -> p d t", d=DB)
        BCAT = area(3072, 2 * T).rearrange("p (c t) -> p c t", c=2)
        CCAT = area(5120, 2 * T).rearrange("p (c t) -> p c t", c=2)
        GT = area(7168, TRI[SB])
        DIFF = area(11776, TRI[SB])
        EE = area(16384, 2 * TRI[SB]).rearrange("p (s n) -> p s n", s=2)
        XT = area(25600, 2 * T).rearrange("p (s t) -> p s t", s=2)
        YACC = area(27648, 3 * T).rearrange("p (d t) -> p d t", d=DB)
        XJ = area(30720, ND * T).rearrange("p (k t) -> p k t", k=ND)
        DTS = area(34816, HD * SB)
        CUMS = area(34840, HD * SB)
        CUM = area(34864, 3 * T).rearrange("p (d t) -> p d t", d=DB)
        PAD3 = area(16384, 5 * P3 * P3).rearrange("p (d h w) -> p d h w", d=5, h=P3)
        SPB = [area(a, 3072) for a in (7168, 10240, 13312, 27648, 22164)]
        BC3 = area(25600, 2 * T).rearrange("p (c t) -> p c t", c=2)
        SQ3 = area(16384, 3 * T)
        Z3 = area(19456, 3 * T).rearrange("p (d t) -> p d t", d=DB)
        R3 = area(22528, T)

        PS = ctx.enter_context(nc.psum_tensor("PS", [128, 8, HALF], F32))

        def banks(first, n=2, p=128):
            return PS[0:p, first:first + n, :].rearrange("p a n -> p (a n)")

        def inner(pad, k, size=P3):
            o = k // 2
            return pad[:, o:o + SIDE, o:o + SIDE]

        def grid(ap):
            return ap.rearrange("p (h w) -> p h w", h=SIDE)

        def turned(ap):
            return ap.rearrange("p (h w) -> p w h", h=SIDE)

        def sequence(ap, k):
            v = (grid, turned)[k % 2](ap)
            return v[:, ::-1, ::-1] if k >= 2 else v

        weights_in = sem("weights_in")
        x_in = sem("x_in")
        late_weights_in = sem("late_weights_in")
        out_written = sem("out_written")
        consts_ready = sem("consts_ready")
        a_exp_done = sem("a_exp_done")
        stage_done = sem("stage_done")
        settled = sem("settled")
        act_steps = sem("act_steps")
        dve_steps = sem("dve_steps")
        gn_stats = sem("gn_stats")
        gn_sums = sem("gn_sums")
        gn_var = sem("gn_var")
        gn_std = sem("gn_std")
        std_ready = [sem(f"std_ready{i}") for i in range(3)]
        xn_ready = [sem(f"xn_ready{i}") for i in range(4)]
        pads_clear = sem("pads_clear")
        xval_ready = sem("xval_ready")
        pad_filled = sem("pad_filled")
        conv_done = sem("conv_done")
        u_ready = sem("u_ready")
        dtr_ready = sem("dtr_ready")
        bc_ready = sem("bc_ready")
        dtr_copied = sem("dtr_copied")
        bc_split = sem("bc_split")
        dtp_ready = sem("dtp_ready")
        softplus_logs = sem("softplus_logs")
        s_ready = sem("s_ready")
        decay_ready = sem("decay_ready")
        decay_free = sem("decay_free")
        weight_ready = sem("weight_ready")
        ring_free = sem("ring_free")
        b_row = sem("b_row")
        num_ready = sem("num_ready")
        drive_ready = sem("drive_ready")
        num_free = sem("num_free")
        h_ready = sem("h_ready")
        hsum_ready = sem("hsum_ready")
        c_row = sem("c_row")
        c_copied = sem("c_copied")
        ch_ready = sem("ch_ready")
        ch_added = sem("ch_added")
        y_out = sem("y_out")
        y_ready = sem("y_ready")
        mean_sum = [sem(f"mean_sum{i}") for i in range(2)]
        centered = [sem(f"centered{i}") for i in range(2)]
        squares = [sem(f"squares{i}") for i in range(3)]
        square_sum = [sem(f"square_sum{i}") for i in range(3)]
        z_ready = [sem(f"z_ready{i}") for i in range(2)]
        z_act = [sem(f"z_act{i}") for i in range(2)]
        gated = [sem(f"gated{i}") for i in range(2)]
        layer_out = [sem(f"layer_out{i}") for i in range(4)]
        ln1_ready = sem("ln1_ready")
        hidden_ready = sem("hidden_ready")
        gelu_done = sem("gelu_done")
        dt3_ready = sem("dt3_ready")
        dt3_read = sem("dt3_read")
        xbc_ready = sem("xbc_ready")
        softplus_logs3 = sem("softplus_logs3")
        pad3_filled = sem("pad3_filled")
        conv3_done = sem("conv3_done")
        xbc_act = sem("xbc_act")
        g_ready = sem("g_ready")
        g_kept = sem("g_kept")
        diff_ready = sem("diff_ready")
        diff_used = sem("diff_used")
        xj_ready = sem("xj_ready")
        xj_used = sem("xj_used")
        xt_ps = sem("xt_ps")
        xt_ready = sem("xt_ready")
        e_ready = sem("e_ready")
        m_ready = sem("m_ready")
        y3_ready = sem("y3_ready")
        yacc_added = sem("yacc_added")
        x_final = sem("x_final")

        WEIGHTS = [(WIN, win), (CONV0, conv0), (SMALL0, small0), (A0, alog0), (WX, wx), (WDT, wdt), (WOUT, wout),
                   (IDENT, ident), (GROUP, group), (TRIM, tri), (ONEHOT, onehot), (SMALL3, small3), (CONV3, conv3),
                   (SMALL1, small1), (DW1, dw1), (B0, b0)]
        LATE = [(W0, w0), (W1, w1), (KE, ke), (WIN3, win3), (WZ3, wz3), (WOUT3, wout3)]

        def whole(ap):
            return ap[tuple(slice(None) for _ in ap.shape)]

        def settle(eng):
            eng.sem_inc(settled, 1)

        def stage_end(eng, b, n):
            settle(eng)
            eng.drain().then_inc(stage_done, 1)
            eng.wait_ge(stage_done, b * (5 * STAGES) + 5 * n)
            settle(eng)

        block = ctx.enter_context(nc.Block())

        @block.sync
        def _(sp):
            for to, of in WEIGHTS:
                sp.dma_start(whole(to), whole(of)).then_inc(weights_in, 16)
            with sp.Fori(0, NB) as b:
                sp.dma_start(X[:, :, :], x[bass.ds(b, 1)].rearrange("o p c t -> (o p) c t")).then_inc(x_in, 16)
                stage_end(sp, b, 1)
                stage_end(sp, b, 2)
                for to, of in LATE:
                    sp.dma_start(to, whole(of)).then_inc(late_weights_in, 16)
                for n in range(3, STAGES):
                    stage_end(sp, b, n)
                sp.wait_ge(x_final, b + 1)
                sp.dma_start(out[bass.ds(b, 1)].rearrange("o p c t -> (o p) c t"), X[:, :, :]).then_inc(out_written, 16)
                sp.wait_ge(out_written, b * 16 + 16)
                settle(sp)
                stage_end(sp, b, STAGES)

        @block.gpsimd
        def _(pool):
            nc.gpsimd.memset(ONES[:, :], 1.0).then_inc(consts_ready, 1)
            nc.gpsimd.memset(GCOL[:, :], GUARD).then_inc(consts_ready, 1)
            nc.gpsimd.memset(EPS5[:, :], 1e-5).then_inc(consts_ready, 1)
            nc.gpsimd.memset(EPS6[:, :], 1e-6).then_inc(consts_ready, 1)
            with pool.Fori(0, NB) as b:
                nc.gpsimd.memset(PADX[:, :, :, :], 0.0).then_inc(pads_clear, 1)
                stage_end(pool, b, 1)
                with pool.Fori(0, DB) as d:
                    u0 = b * (DB * NS) + d * NS
                    for n in range(NS):
                        for k in range(4):
                            if k == 0:
                                pool.wait_ge(num_ready, u0 + b + (n + 1))
                            pool.wait_ge(weight_ready, u0 * 4 + (4 * n + k + 1))
                            slot = RING[:, (4 * n + k) % 8, :]
                            num = NUM[:, n % 2, :]
                            if k < 2:
                                ins = nc.gpsimd.tensor_tensor(slot, slot, num, ALU.mult)
                            else:
                                v = slot.rearrange("p (w h) -> p w h", w=SIDE)
                                ins = nc.gpsimd.tensor_tensor(v, v, turned(num), ALU.mult)
                            ins.then_inc(drive_ready, 1)
                stage_end(pool, b, 2)
                stage_end(pool, b, 3)
                nc.gpsimd.memset(PAD1[:, :, :, :], 0.0).then_inc(pads_clear, 1)
                stage_end(pool, b, 4)
                nc.gpsimd.memset(PAD2[:, :, :, :], 0.0).then_inc(pads_clear, 1)
                stage_end(pool, b, 5)
                nc.gpsimd.memset(PAD3[:, :, :, :], 0.0).then_inc(pads_clear, 1)
                stage_end(pool, b, 6)
                stage_end(pool, b, 7)
                with pool.Fori(0, HD) as j:
                    pool.wait_ge(xj_used, b * HD + j + 1)
                    settle(pool)
                    xc = XC[:, bass.ds(j, 1), :].rearrange("p o t -> p (o t)")
                    nc.gpsimd.tensor_copy(XJ[:, 0, :], xc).then_inc(xj_ready, 1)
                    pool.wait_ge(xj_ready, (b * HD + j) * ND + 1)
                    settle(pool)
                    for k in range(1, ND):
                        nc.gpsimd.tensor_copy(XJ[:, k, :].rearrange("p (a c) -> p a c", a=SIDE),
                                              sequence(XJ[:, 0, :], k)).then_inc(xj_ready, 1)
                stage_end(pool, b, 8)
                stage_end(pool, b, STAGES)

        @block.scalar
        def _(act):
            act.wait_ge(weights_in, 16 * len(WEIGHTS))
            act.wait_ge(consts_ready, 4)
            nc.scalar.activation(A0[:, :], A0[:, :], ACT.Exp).then_inc(a_exp_done, 1)
            nc.scalar.activation(A3[:, :], SMALL3[:, 8:20], ACT.Exp).then_inc(a_exp_done, 1)
            with act.Fori(0, NB) as b:
                st = Steps(act, act_steps, ACT_STEPS, b)

                def softplus(psum, biases, scratch, read, done):
                    t1, t2, t3 = scratch[:3]
                    for i in range(3):
                        bias = biases[:, i:i + 1]
                        nc.scalar.activation(t3[:, i * T:(i + 1) * T], psum[i], ACT.Relu, bias=bias)
                        last = nc.scalar.activation(t1[:, i * T:(i + 1) * T], psum[i], ACT.Abs, bias=bias)
                    st.done(last)
                    if read is not None:
                        act.sem_inc(read, 1)
                    st.done(nc.scalar.activation(t1, t1, ACT.Exp, scale=-1.0))
                    nc.scalar.activation(t2, t1, ACT.Ln, bias=1.0).then_inc(done, 1)

                def group_std(layer):
                    act.wait_ge(gn_var, b * 4 + (layer + 1))
                    nc.scalar.activation(GV[:, :, 0], GV[:, :, 0], ACT.Sqrt, bias=EPS5[0:CP, 0:1]).then_inc(gn_std, 1)

                def layer_std(i, to, sums, n, eps):
                    act.wait_ge(square_sum[i], b + 1)
                    nc.scalar.activation(to, sums, ACT.Sqrt, bias=eps, scale=1.0 / n).then_inc(std_ready[i], 1)

                group_std(0)
                for i in range(DB):
                    act.wait_ge(xval_ready, b * DB + (i + 1))
                    if i == 0:
                        act.wait_ge(pads_clear, b * 4 + 1)
                    nc.scalar.activation(inner(PADX[:, i], 3), grid(banks(2 * i)), ACT.Copy).then_inc(pad_filled, 1)
                for i in range(DB):
                    act.wait_ge(conv_done, b * DB + (i + 1))
                    nc.scalar.activation(U[:, i, :], U[:, i, :], ACT.Silu, bias=SMALL0[:, 0, i:i + 1]).then_inc(u_ready, 1)
                act.wait_ge(dtr_ready, b + 1)
                nc.scalar.activation(DTR, banks(6, 2, RANK), ACT.Copy).then_inc(dtr_copied, 1)
                act.wait_ge(dtp_ready, b + 1)
                softplus([banks(2), banks(4), banks(6)], SMALL0[:, 1, :], SPA, None, softplus_logs)
                stage_end(act, b, 1)
                with act.Fori(0, DB) as d:
                    u0 = b * (DB * NS) + d * NS
                    dt = DT[:, bass.ds(d, 1), :].rearrange("p o t -> p (o t)")
                    for n in range(NS):
                        if n % 2 == 0:
                            for m in (n, n + 1):
                                a = A0[:, bass.ds(d * NS + m, 1)]
                                act.wait_ge(decay_free, u0 + (m + 1))
                                settle(act)
                                nc.scalar.activation(DEC[:, m % 4, 0, :], dt, ACT.Exp, scale=a)
                                nc.scalar.activation(DEC[:, m % 4, 1, :].rearrange("p (w h) -> p w h", w=SIDE),
                                                     turned(dt), ACT.Exp, scale=a).then_inc(decay_ready, 1)
                        for k in range(4):
                            s = S[:, bass.ds(d, 1), k, :].rearrange("p o t -> p (o t)")
                            act.wait_ge(ring_free, u0 * 4 + (4 * n + k + 1))
                            settle(act)
                            nc.scalar.activation(RING[:, (4 * n + k) % 8, :], s, ACT.Sigmoid, bias=GCOL[:, 0:1],
                                                 scale=A0[:, bass.ds(d * NS + n, 1)]).then_inc(weight_ready, 1)
                        if n >= 1:
                            act.wait_ge(c_row, u0 + n)
                            act.wait_ge(ch_ready, u0 + n)
                            nc.scalar.activation(CS, banks(6), ACT.Copy).then_inc(c_copied, 1)
                    act.wait_ge(c_row, u0 + NS)
                    act.wait_ge(ch_ready, u0 + NS)
                    nc.scalar.activation(CS, banks(6), ACT.Copy).then_inc(c_copied, 1)
                stage_end(act, b, 2)
                act.wait_ge(centered[0], b + 1)
                nc.scalar.activation(SQ0, Y0.rearrange("p d t -> p (d t)"), ACT.Square).then_inc(squares[0], 1)
                for i in range(DB):
                    act.wait_ge(z_ready[0], b * DB + (i + 1))
                    nc.scalar.activation(Z0[:, i, :], banks((4, 6, 0)[i]), ACT.Silu).then_inc(z_act[0], 1)
                layer_std(0, R0, banks(2), DI, EPS5[:, 0:1])
                stage_end(act, b, 3)
                group_std(1)
                act.wait_ge(centered[1], b + 1)
                nc.scalar.activation(SQ1, Y1.rearrange("p c t -> p (c t)"), ACT.Square).then_inc(squares[1], 1)
                layer_std(1, R1, banks(2, 2, CP), C, EPS6[0:CP, 0:1])
                for m in range(MB):
                    act.wait_ge(hidden_ready, b * MB + (m + 1))
                    nc.scalar.activation(G1[:, m, :], banks(4 + 2 * (m % 2)), ACT.Gelu, bias=B0[:, m:m + 1]).then_inc(gelu_done, 1)
                stage_end(act, b, 4)
                group_std(2)
                stage_end(act, b, 5)
                group_std(3)
                act.wait_ge(dt3_ready, b + 1)
                softplus([banks(0), banks(2), banks(4)], SMALL3[:, 5:8], SPB, dt3_read, softplus_logs3)
                act.wait_ge(pads_clear, b * 4 + 4)
                for i in range(5):
                    act.wait_ge(xbc_ready, b * 5 + (i + 1))
                    nc.scalar.activation(inner(PAD3[:, i], 3), grid(banks((6, 0, 2, 4, 6)[i])), ACT.Copy).then_inc(pad3_filled, 1)
                for i in range(3):
                    act.wait_ge(conv3_done, b * 5 + (i + 1))
                    nc.scalar.activation(XC[:, i, :], XC[:, i, :], ACT.Silu, bias=SMALL3[:, i:i + 1]).then_inc(xbc_act, 1)
                for i, cat in enumerate((BCAT, CCAT)):
                    act.wait_ge(conv3_done, b * 5 + (i + 4))
                    for k in range(ND):
                        p = slice(64 * (k % 2), 64 * (k % 2) + 64)
                        nc.scalar.activation(cat[p, k // 2, :].rearrange("p (a c) -> p a c", a=SIDE),
                                             sequence(BC3[p, i, :], k), ACT.Silu,
                                             bias=SMALL3[p, 3 + i:4 + i]).then_inc(xbc_act, 1)
                stage_end(act, b, 6)
                for s in range(SB):
                    act.wait_ge(g_ready, b * SB + (s + 1))
                    nc.scalar.activation(GT[:, TRI[s]:TRI[s + 1]], banks(2 * (s % 4))[:, 128 * s:T], ACT.Copy).then_inc(g_kept, 1)
                stage_end(act, b, 7)
                with act.Fori(0, HD) as j:
                    for k in range(ND):
                        h = b * 12 + j * 4
                        if k == 0:
                            act.wait_ge(diff_ready, b * HD + j + 1)
                        act.wait_ge(y3_ready, h + (k + 1))
                        settle(act)
                        ins = nc.scalar.activation(EE[:, k % 2, :], DIFF, ACT.Exp, scale=A3[:, bass.ds(j + 3 * k, 1)])
                        ins.then_inc(e_ready, 1)
                stage_end(act, b, 8)
                for i in range(DB):
                    act.wait_ge(z_ready[1], b * DB + (i + 1))
                    nc.scalar.activation(Z3[:, i, :], banks((4, 6, 0)[i]), ACT.Silu).then_inc(z_act[1], 1)
                act.wait_ge(gated[1], b * 2 + 1)
                nc.scalar.activation(SQ3, YACC.rearrange("p d t -> p (d t)"), ACT.Square).then_inc(squares[2], 1)
                layer_std(2, R3, banks(2), DI, EPS5[:, 0:1])
                stage_end(act, b, STAGES)
                st.end()

        @block.vector
        def _(dve):
            dve.wait_ge(a_exp_done, 2)
            dve.wait_ge(weights_in, 16 * len(WEIGHTS))
            nc.vector.tensor_scalar(A0[:, :], A0[:, :], -1.0, None, ALU.mult).then_inc(consts_ready, 1)
            nc.vector.tensor_scalar(A3[:, :], A3[:, :], -1.0, None, ALU.mult).then_inc(consts_ready, 1)
            nc.vector.tensor_scalar(D4[:, :], SMALL0[:, 2, :], 4.0, None, ALU.mult).then_inc(consts_ready, 1)
            nc.vector.tensor_reduce(DSUM[:, :], SMALL3[:, 20:32].rearrange("p (k j) -> p j k", k=ND), AX_X,
                                    ALU.add).then_inc(consts_ready, 1)
            dve.wait_ge(consts_ready, 8)
            with dve.Fori(0, NB) as b:
                st = Steps(dve, dve_steps, DVE_STEPS, b)
                v = nc.vector

                def group_norm(layer, to):
                    for c in range(CB):
                        for h in range(2):
                            ins = v.bn_stats(ST[:, c, h, :], X[:, c, h * HALF:(h + 1) * HALF])
                    st.done(ins)
                    settle(dve)
                    for c in range(CB):
                        ins = v.bn_aggr(MV[:, c, :], ST[:, c].rearrange("p h s -> p (h s)"))
                    st.done(ins)
                    st.done(v.tensor_tensor(GS[:, :, 1], MV[:, :, 0], MV[:, :, 0], ALU.mult))
                    v.tensor_copy(GS[:, :, 0], MV[:, :, 0])
                    v.tensor_tensor(GS[:, :, 1], GS[:, :, 1], MV[:, :, 1], ALU.add).then_inc(gn_stats, 1)
                    dve.wait_ge(gn_sums, b * 4 + (layer + 1))
                    st.done(v.tensor_copy(GM[:, :, :].rearrange("p c s -> p (c s)"), banks(0, 1, CP)[:, 0:2 * CB]))
                    st.done(v.tensor_tensor(GV[:, :, 0], GM[:, :, 0], GM[:, :, 0], ALU.mult))
                    v.tensor_tensor(GV[:, :, 0], GM[:, :, 1], GV[:, :, 0], ALU.subtract).then_inc(gn_var, 1)
                    dve.wait_ge(gn_std, b * 4 + (layer + 1))
                    st.done(v.reciprocal(GV[:, :, 0], GV[:, :, 0]))
                    for c in range(CB):
                        ins = v.tensor_scalar(to[c], grid(X[:, c, :]), GM[:, c, 0:1], GV[:, c, 0:1],
                                              ALU.subtract, ALU.mult)
                        if c == CB - 1:
                            ins.then_inc(xn_ready[layer], 1)

                def conv(to, pad, w, k, bias, sem_done):
                    for t in range(k * k):
                        view = pad[:, t // k:t // k + SIDE, t % k:t % k + SIDE]
                        if t == 0:
                            st.done(v.tensor_scalar(grid(to), view, w[:, 0:1], bias, ALU.mult, ALU.add)
                                    if bias is not None else v.tensor_scalar(grid(to), view, w[:, 0:1], None, ALU.mult))
                            continue
                        ins = v.scalar_tensor_tensor(grid(to), view, w[:, t:t + 1], grid(to), ALU.mult, ALU.add)
                        if t == k * k - 1 and sem_done is not None:
                            ins.then_inc(sem_done, 1)
                        else:
                            st.done(ins)

                def softplus(scratch, to):
                    e, log, top, t, mask = scratch
                    st.done(v.tensor_scalar(t, e, -0.25, 1.0 / 3.0, ALU.mult, ALU.add))
                    st.done(v.tensor_tensor(t, t, e, ALU.mult))
                    st.done(v.scalar_tensor_tensor(t, t, -0.5, e, ALU.add, ALU.mult))
                    st.done(v.scalar_tensor_tensor(t, t, 1.0, e, ALU.add, ALU.mult))
                    st.done(v.tensor_scalar(mask, e, 2.0 ** -6, None, ALU.is_lt))
                    settle(dve)
                    st.done(v.copy_predicated(log, mask.bitcast(U32), t))
                    st.done(v.tensor_tensor(to, log, top, ALU.add))

                def reciprocal_std(i, to):
                    dve.wait_ge(std_ready[i], b + 1)
                    st.done(v.reciprocal(to, to))

                dve.wait_ge(x_in, b * 16 + 16)
                group_norm(0, [grid(XN[:, c, :]) for c in range(CB)])
                for i in range(DB):
                    dve.wait_ge(pad_filled, b * DB + (i + 1))
                    conv(U[:, i, :], PADX[:, i], CONV0[:, i, :], 3, None, conv_done)
                dve.wait_ge(bc_ready, b + 1)
                st.done(v.tensor_copy(BCF, banks(0, 2, 2 * NS)))
                for part in range(3):
                    st.done(v.tensor_copy(BCH, BCF))
                    ins = v.tensor_copy(BCS[32 * part:32 * part + 32, :], BCH)
                    if part == 2:
                        ins.then_inc(bc_split, 1)
                    else:
                        st.done(v.tensor_tensor(BCF, BCF, BCH, ALU.subtract))
                dve.wait_ge(softplus_logs, b + 1)
                softplus(SPA, DT.rearrange("p d t -> p (d t)"))
                v.tensor_tensor(DTU.rearrange("p d t -> p (d t)"), DT.rearrange("p d t -> p (d t)"),
                                U.rearrange("p d t -> p (d t)"), ALU.mult)
                for i in range(DB):
                    st.done(v.tensor_copy(SPA[0][:, i * T:(i + 1) * T].rearrange("p (w h) -> p w h", w=SIDE),
                                          turned(DT[:, i, :])))
                for i in range(DB):
                    for k in range(4):
                        src = DT[:, i, :] if k < 2 else SPA[0][:, i * T:(i + 1) * T]
                        to = S[:, i, k, :]
                        if k % 2:
                            src, to = src[:, ::-1], to[:, ::-1]
                        v.tensor_tensor_scan(to, src, src, 0.0, ALU.add, ALU.max)
                stage_end(dve, b, 1)

                def numerator(n, dtu, wait):
                    dve.wait_ge(b_row, wait)
                    v.tensor_tensor(NUM[:, n % 2, :], dtu.rearrange("p o t -> p (o t)"), banks(4), ALU.mult).then_inc(num_ready, 1)

                numerator(0, DTUX[:, 0:1, :], b * (DB * NS + 1) + 1)
                with dve.Fori(0, DB) as d:
                    u0 = b * (DB * NS) + d * NS

                    def weigh(n):
                        dve.wait_ge(hsum_ready, u0 + (n + 1))
                        dve.wait_ge(c_copied, u0 + (n + 1))
                        dve.wait_ge(ch_added, u0 + (n + 1))
                        v.tensor_tensor(CM, banks(0), CS, ALU.mult).then_inc(ch_ready, 1)

                    for n in range(NS):
                        for k in range(4):
                            if k == 0:
                                dve.wait_ge(decay_ready, u0 + (n + 1))
                            dve.wait_ge(drive_ready, u0 * 4 + (4 * n + k + 1))
                            a, w = DEC[:, n % 4, k // 2, :], RING[:, (4 * n + k) % 8, :]
                            if k % 2:
                                a, w = a[:, ::-1], w[:, ::-1]
                            ins = v.tensor_tensor_scan(w, a, w, 0.0, ALU.mult, ALU.add)
                            ins.then_inc(h_ready, 1)
                            if k == 0 and n >= 1:
                                weigh(n - 1)
                            if k == 1:
                                nxt = DTUX[:, bass.ds(d, 1), :] if n < NS - 1 else DTUX[:, bass.ds(d + 1, 1), :]
                                numerator(n + 1, nxt, u0 + b + (n + 2))
                        dve.wait_ge(h_ready, u0 * 4 + (4 * n + 4))
                        dve.sem_inc(decay_free, 1)
                    weigh(NS - 1)
                    dve.wait_ge(y_out, b * DB + d + 1)
                    yd = Y0[:, bass.ds(d, 1), :].rearrange("p o t -> p (o t)")
                    ud = U[:, bass.ds(d, 1), :].rearrange("p o t -> p (o t)")
                    v.scalar_tensor_tensor(yd, ud, D4[:, bass.ds(d, 1)], banks(2), ALU.mult, ALU.add).then_inc(y_ready, 1)
                stage_end(dve, b, 2)
                dve.wait_ge(mean_sum[0], b + 1)
                for i in range(DB):
                    ins = v.scalar_tensor_tensor(Y0[:, i, :], banks(0), -1.0 / DI, Y0[:, i, :], ALU.mult, ALU.add)
                ins.then_inc(centered[0], 1)
                dve.wait_ge(centered[0], b + 1)
                reciprocal_std(0, R0)
                for i in range(DB):
                    st.done(v.scalar_tensor_tensor(Y0[:, i, :], Y0[:, i, :], SMALL0[:, 3, i:i + 1], R0, ALU.mult, ALU.mult))
                for i in range(DB):
                    dve.wait_ge(z_act[0], b * DB + (i + 1))
                    ins = v.scalar_tensor_tensor(Y0[:, i, :], Y0[:, i, :], SMALL0[:, 4, i:i + 1], Z0[:, i, :], ALU.add, ALU.mult)
                ins.then_inc(gated[0], 1)

                def residual(layer, first=2):
                    dve.wait_ge(layer_out[layer], b + 1)
                    for c in range(CB):
                        ins = v.tensor_tensor(X[:, c, :], X[:, c, :], banks(first + 2 * c, 2, CP), ALU.add)
                        if c == CB - 1 and layer < 3:
                            st.done(ins)
                    return ins

                residual(0)
                stage_end(dve, b, 3)
                dve.wait_ge(pads_clear, b * 4 + 2)
                group_norm(1, [inner(PAD1[:, c], K1) for c in range(CB)])
                dve.wait_ge(xn_ready[1], b + 1)
                for c in range(CB):
                    conv(Y1[:, c, :], PAD1[:, c], DW1[:, c, :], K1, SMALL1[:, 0, c:c + 1], None)
                dve.sem_inc(ln1_ready, 1)
                dve.wait_ge(mean_sum[1], b + 1)
                for c in range(CB):
                    ins = v.scalar_tensor_tensor(Y1[:, c, :], banks(0, 2, CP), -1.0 / C, Y1[:, c, :], ALU.mult, ALU.add)
                ins.then_inc(centered[1], 1)
                dve.wait_ge(centered[1], b + 1)
                reciprocal_std(1, R1)
                for c in range(CB):
                    st.done(v.scalar_tensor_tensor(Y1[:, c, :], Y1[:, c, :], SMALL1[:, 1, c:c + 1], R1, ALU.mult, ALU.mult))
                for c in range(CB):
                    ins = v.tensor_scalar(Y1[:, c, :], Y1[:, c, :], SMALL1[:, 2, c:c + 1], None, ALU.add)
                ins.then_inc(ln1_ready, 1)
                dve.wait_ge(layer_out[1], b + 1)
                for c in range(CB):
                    st.done(v.tensor_scalar(O1[:, c, :], banks(2 * c, 2, CP), SMALL1[:, 3, c:c + 1], SMALL1[:, 4, c:c + 1],
                                            ALU.add, ALU.mult))
                    st.done(v.tensor_tensor(X[:, c, :], X[:, c, :], O1[:, c, :], ALU.add))
                stage_end(dve, b, 4)
                dve.wait_ge(pads_clear, b * 4 + 3)
                group_norm(2, [inner(PAD2[:, c], 3) for c in range(CB)])
                residual(2)
                stage_end(dve, b, 5)
                group_norm(3, [grid(XN[:, c, :]) for c in range(CB)])
                dve.wait_ge(softplus_logs3, b + 1)
                softplus(SPB, SPB[1])
                for j in range(HD):
                    st.done(v.tensor_tensor_scan(CUM[:, j, :], SPB[1][:, j * T:(j + 1) * T], SPB[1][:, j * T:(j + 1) * T],
                                                 0.0, ALU.add, ALU.max))
                for j in range(HD):
                    for of, to in ((SPB[1][:, j * T:(j + 1) * T], DTS), (CUM[:, j, :], CUMS)):
                        diag = SPB[0][:, 0:T].rearrange("p (s q) -> p s q", s=SB)
                        st.done(v.tensor_tensor(diag, of.rearrange("p (s q) -> p s q", s=SB),
                                                IDENT[:, :].unsqueeze(1).to_broadcast([128, SB, 128]), ALU.mult))
                        st.done(v.tensor_reduce(to[:, j * SB:(j + 1) * SB], diag, AX_X, ALU.add))
                for i in range(5):
                    dve.wait_ge(pad3_filled, b * 5 + (i + 1))
                    to = XC[:, i, :] if i < 3 else BC3[:, i - 3, :]
                    conv(to, PAD3[:, i], CONV3[:, i, :], 3, None, conv3_done)
                stage_end(dve, b, 6)
                for s in range(SB):
                    dve.wait_ge(g_kept, b * SB + (s + 1))
                    diag = GT[:, TRI[s]:TRI[s] + 128]
                    v.tensor_tensor(diag, diag, TRIM[:, :], ALU.mult)
                stage_end(dve, b, 7)
                with dve.Fori(0, HD) as j:
                    dve.wait_ge(diff_used, b * HD + j + 1)
                    for s in range(SB):
                        cum = CUM[:, bass.ds(j, 1), 128 * s:T].rearrange("p o t -> p (o t)")
                        ins = v.tensor_scalar(DIFF[:, TRI[s]:TRI[s + 1]], cum, CUMS[:, bass.ds(j * SB + s, 1)], 0.0,
                                              ALU.subtract, ALU.max)
                    ins.then_inc(diff_ready, 1)

                    def collect(k):
                        dve.wait_ge(y3_ready, b * 12 + j * 4 + (k + 3))
                        ya = YACC[:, bass.ds(j, 1), :].rearrange("p o t -> p (o t)")
                        xc = XC[:, bass.ds(j, 1), :].rearrange("p o t -> p (o t)")
                        y = banks(2 * (k % 2)).rearrange("p (a c) -> p a c", a=SIDE)
                        if k >= 2:
                            y = y[:, ::-1, ::-1]
                        if k == 0:
                            ins = v.scalar_tensor_tensor(grid(ya), grid(xc), DSUM[:, bass.ds(j, 1)], y, ALU.mult, ALU.add)
                        else:
                            dve.wait_ge(yacc_added, b * 12 + j * 4 + (k + 1))
                            to = (grid, turned)[k % 2](ya)
                            ins = v.tensor_tensor(to, to, y, ALU.add)
                        ins.then_inc(yacc_added, 1)

                    for k in range(ND):
                        h = b * 12 + j * 4
                        dve.wait_ge(xt_ps, h + (k + 1))
                        dve.wait_ge(y3_ready, h + (k + 1))
                        v.tensor_tensor(XT[:, k % 2, :].rearrange("p (s q) -> p s q", s=SB),
                                        banks(4 + 2 * (k % 2)).rearrange("p (s q) -> p s q", s=SB),
                                        DTS[:, bass.ds(j * SB, SB)].unsqueeze(2).to_broadcast([128, SB, 128]),
                                        ALU.mult).then_inc(xt_ready, 1)
                        dve.wait_ge(e_ready, h + (k + 1))
                        v.tensor_tensor(EE[:, k % 2, :], EE[:, k % 2, :], GT, ALU.mult).then_inc(m_ready, 1)
                        if k >= 1:
                            collect(k - 1)
                        if k == ND - 1:
                            dve.sem_inc(diff_used, 1)
                    collect(ND - 1)
                stage_end(dve, b, 8)
                for i in range(DB):
                    dve.wait_ge(z_act[1], b * DB + (i + 1))
                    ins = v.tensor_tensor(YACC[:, i, :], YACC[:, i, :], Z3[:, i, :], ALU.mult)
                ins.then_inc(gated[1], 1)
                dve.wait_ge(gated[1], b * 2 + 1)
                reciprocal_std(2, R3)
                for i in range(DB):
                    ins = v.scalar_tensor_tensor(YACC[:, i, :], YACC[:, i, :], SMALL3[:, 32 + i:33 + i], R3, ALU.mult, ALU.mult)
                ins.then_inc(gated[1], 1)
                residual(3).then_inc(x_final, 1)
                stage_end(dve, b, STAGES)
                st.end()

        @block.tensor
        def _(pe):
            pe.wait_ge(weights_in, 16 * len(WEIGHTS))
            pe.wait_ge(consts_ready, 8)
            pe.drain().then_inc(decay_free, 4)
            pe.drain().then_inc(ring_free, 8)
            pe.drain().then_inc(ch_ready, 1)
            pe.drain().then_inc(ch_added, 1)
            pe.drain().then_inc(xj_used, 1)
            pe.drain().then_inc(y3_ready, 2)
            pe.drain().then_inc(diff_used, 1)
            pe.drain().then_inc(y_ready, 1)
            pe.drain().then_inc(yacc_added, 1)
            with pe.Fori(0, NB) as b:
                def mm(to, w, x, start=True, stop=True):
                    return nc.tensor.matmul(to, w, x, start=start, stop=stop)

                def project(first, p, w, x, kb):
                    for h in range(2):
                        for i in range(kb):
                            ins = mm(PS[0:p, first + h, :], w(i), x(i, h), i == 0, i == kb - 1)
                    return ins

                def cols(ap, h):
                    return ap[:, h * HALF:(h + 1) * HALF]

                def group_sums(layer):
                    pe.wait_ge(gn_stats, b * 4 + (layer + 1))
                    mm(PS[0:CP, 0, 0:2 * CB], GROUP[:, :], GS[:, :, :].rearrange("p c s -> p (c s)")).then_inc(gn_sums, 1)

                def sums(first, p, of, kb):
                    return project(first, p, lambda i: ONES[0:p, 0:p], lambda i, h: cols(of(i), h), kb)

                group_sums(0)
                pe.wait_ge(xn_ready[0], b + 1)
                for d in range(DB):
                    project(2 * d, 128, lambda i: WIN[:, i, 128 * d:128 * d + 128],
                            lambda i, h: cols(XN[:, i, :], h), CB).then_inc(xval_ready, 1)
                pe.wait_ge(u_ready, b * DB + DB)
                project(6, RANK, lambda i: WX[:, i, 0:RANK], lambda i, h: cols(U[:, i, :], h), DB).then_inc(dtr_ready, 1)
                project(0, 2 * NS, lambda i: WX[:, i, RANK:RANK + 2 * NS], lambda i, h: cols(U[:, i, :], h), DB).then_inc(bc_ready, 1)
                pe.wait_ge(dtr_copied, b + 1)
                for d in range(DB):
                    ins = project(2 + 2 * d, 128, lambda i: WDT[:, 128 * d:128 * d + 128], lambda i, h: cols(DTR, h), 1)
                ins.then_inc(dtp_ready, 1)
                pe.wait_ge(bc_split, b + 1)
                stage_end(pe, b, 1)

                def row(first, r):
                    return project(first, 128, lambda i: ONEHOT[:, r, :], lambda i, h: cols(BCS, h), 1)

                row(4, 0).then_inc(b_row, 1)
                with pe.Fori(0, DB) as d:
                    u0 = b * (DB * NS) + d * NS

                    def add_product(n):
                        pe.wait_ge(ch_ready, u0 + (n + 2))
                        if n == 0:
                            pe.wait_ge(y_ready, b * DB + d + 1)
                        for h in range(2):
                            ins = mm(PS[:, 2 + h, :], IDENT[:, :], cols(CM, h), n == 0, n == NS - 1)
                        ins.then_inc(ch_added, 1)
                        return ins

                    for n in range(NS):
                        pe.wait_ge(num_ready, u0 + b + (n + 1))
                        row(4, (n + 1) % NS).then_inc(b_row, 1)
                        if n >= 1:
                            pe.wait_ge(c_copied, u0 + n)
                        row(6, NS + n).then_inc(c_row, 1)
                        if n >= 1:
                            add_product(n - 1)
                        for k in range(4):
                            pe.wait_ge(h_ready, u0 * 4 + (4 * n + k + 1))
                            state = RING[:, (4 * n + k) % 8, :]
                            for h in range(2):
                                if k < 2:
                                    src = cols(state, h)
                                else:
                                    src = state.rearrange("p (w h) -> p h w", w=SIDE)[:, 16 * h:16 * h + 16, :]
                                ins = mm(PS[:, h, :], IDENT[:, :], src, k == 0, k == 3)
                            ins.then_inc(ring_free, 1)
                        pe.wait_ge(ring_free, u0 * 4 + (4 * n + 12))
                        pe.sem_inc(hsum_ready, 1)
                    add_product(NS - 1)
                    pe.wait_ge(ch_added, u0 + (NS + 1))
                    pe.sem_inc(y_out, 1)
                stage_end(pe, b, 2)
                sums(0, 128, lambda i: Y0[:, i, :], DB).then_inc(mean_sum[0], 1)
                for d in range(DB):
                    if d == 2:
                        pe.wait_ge(centered[0], b + 1)
                    project((4, 6, 0)[d], 128, lambda i: WIN[:, i, DI + 128 * d:DI + 128 * d + 128],
                            lambda i, h: cols(XN[:, i, :], h), CB).then_inc(z_ready[0], 1)
                pe.wait_ge(squares[0], b + 1)
                sums(2, 128, lambda i: SQ0[:, i * T:(i + 1) * T], DB).then_inc(square_sum[0], 1)

                def project_out(first, w, of, kb):
                    for c in range(CB):
                        ins = project(first + 2 * c, CP, lambda i: w[:, i, CP * c:CP * c + CP], lambda i, h: cols(of(i), h), kb)
                    return ins

                pe.wait_ge(gated[0], b + 1)
                project_out(2, WOUT, lambda i: Y0[:, i, :], DB).then_inc(layer_out[0], 1)
                stage_end(pe, b, 3)
                pe.wait_ge(late_weights_in, b * (16 * len(LATE)) + 16 * len(LATE))
                group_sums(1)
                pe.wait_ge(ln1_ready, b * 2 + 1)
                sums(0, CP, lambda i: Y1[:, i, :], CB).then_inc(mean_sum[1], 1)
                pe.wait_ge(squares[1], b + 1)
                sums(2, CP, lambda i: SQ1[:, i * T:(i + 1) * T], CB).then_inc(square_sum[1], 1)
                pe.wait_ge(ln1_ready, b * 2 + 2)
                for m in range(MB):
                    if m >= 2:
                        pe.wait_ge(gelu_done, b * MB + (m - 1))
                    project(4 + 2 * (m % 2), 128, lambda i: W0[:, i, 128 * m:128 * m + 128],
                            lambda i, h: cols(Y1[:, i, :], h), CB).then_inc(hidden_ready, 1)
                pe.wait_ge(gelu_done, b * MB + MB)
                project_out(0, W1, lambda i: G1[:, i, :], MB).then_inc(layer_out[1], 1)
                stage_end(pe, b, 4)
                group_sums(2)
                pe.wait_ge(xn_ready[2], b + 1)
                for c in range(CB):
                    for h in range(2):
                        for i in range(CB):
                            for t, (y, xx) in enumerate(TAPS2):
                                ins = mm(PS[0:CP, 2 + 2 * c + h, :], KE[:, i, t, CP * c:CP * c + CP],
                                         PAD2[:, i, 16 * h + y:16 * h + y + 16, xx:xx + SIDE],
                                         i == 0 and t == 0, i == CB - 1 and t == len(TAPS2) - 1)
                ins.then_inc(layer_out[2], 1)
                stage_end(pe, b, 5)
                group_sums(3)
                pe.wait_ge(xn_ready[3], b + 1)

                def in3(first, blk):
                    return project(first, 128, lambda i: WIN3[:, i, 128 * blk:128 * blk + 128],
                                   lambda i, h: cols(XN[:, i, :], h), CB)

                for j in range(HD):
                    ins = in3(2 * j, 5 + j)
                ins.then_inc(dt3_ready, 1)
                in3(6, 0).then_inc(xbc_ready, 1)
                pe.wait_ge(dt3_read, b + 1)
                for i in range(1, 5):
                    if i == 4:
                        pe.wait_ge(pad3_filled, b * 5 + 1)
                    in3((6, 0, 2, 4, 6)[i], i).then_inc(xbc_ready, 1)
                pe.wait_ge(xbc_act, b * 11 + 11)
                stage_end(pe, b, 6)
                for s in range(SB):
                    if s >= 4:
                        pe.wait_ge(g_kept, b * SB + (s - 3))
                    for h in range(2):
                        lo, hi = max(HALF * h, 128 * s), HALF * (h + 1)
                        if lo >= hi:
                            continue
                        for c in range(2):
                            ins = mm(PS[:, 2 * (s % 4) + h, lo - HALF * h:HALF], BCAT[:, c, 128 * s:128 * s + 128],
                                     CCAT[:, c, lo:hi], c == 0, c == 1)
                    ins.then_inc(g_ready, 1)
                stage_end(pe, b, 7)
                with pe.Fori(0, HD) as j:
                    def outputs(k):
                        h0 = b * 12 + j * 4
                        pe.wait_ge(m_ready, h0 + (k + 1))
                        pe.wait_ge(xt_ready, h0 + (k + 1))
                        if k >= 2:
                            pe.wait_ge(yacc_added, h0 + k)
                        for h in range(2):
                            for s in range(4 * h + 4):
                                lo = max(HALF * h, 128 * s)
                                at = TRI[s] + lo - 128 * s
                                ins = mm(PS[:, 2 * (k % 2) + h, lo - HALF * h:HALF], XT[:, k % 2, 128 * s:128 * s + 128],
                                         EE[:, k % 2, at:at + HALF * (h + 1) - lo], s == 0, s == 4 * h + 3)
                        ins.then_inc(y3_ready, 1)

                    pe.wait_ge(xj_ready, (b * HD + j) * ND + ND)
                    pe.wait_ge(yacc_added, b * 12 + j * 4 + 1)
                    for k in range(ND):
                        if k >= 2:
                            pe.wait_ge(xt_ready, b * 12 + j * 4 + (k - 1))
                        for s in range(SB):
                            src = XJ[:, k, 128 * s:128 * s + 128]
                            ins = nc.tensor.transpose(banks(4 + 2 * (k % 2))[:, 128 * s:128 * s + 128], src, IDENT[:, :])
                        ins.then_inc(xt_ps, 1)
                        if k == ND - 1:
                            pe.wait_ge(xt_ps, b * 12 + j * 4 + 4)
                            pe.sem_inc(xj_used, 1)
                        if k >= 1:
                            outputs(k - 1)
                    outputs(ND - 1)
                stage_end(pe, b, 8)
                for d in range(DB):
                    project((4, 6, 0)[d], 128, lambda i: WZ3[:, i, 128 * d:128 * d + 128],
                            lambda i, h: cols(XN[:, i, :], h), CB).then_inc(z_ready[1], 1)
                pe.wait_ge(squares[2], b + 1)
                sums(2, 128, lambda i: SQ3[:, i * T:(i + 1) * T], DB).then_inc(square_sum[2], 1)
                pe.wait_ge(gated[1], b * 2 + 2)
                project_out(2, WOUT3, lambda i: YACC[:, i, :], DB).then_inc(layer_out[3], 1)
                stage_end(pe, b, STAGES)


def kernel(**inputs):
    import ml_dtypes
    import numpy as np
    import concourse.bacc as bacc
    from concourse import mybir as mb
    from concourse.bass_utils import run_bass_kernel_spmd as run

    a = {k: np.asarray(v) for k, v in inputs.items()}

    def cols(v, p):
        return np.ascontiguousarray(v.reshape(-1, p).T)

    def rows(w, p):
        return w.reshape(-1, p, w.shape[1]).transpose(1, 0, 2)

    def on_all(v):
        return np.broadcast_to(v.reshape(1, -1), (128, v.size))

    h = {}
    h["x"] = a["x"].reshape(NB, T, CB, CP).transpose(0, 3, 2, 1)
    h["win"] = rows(a["L0_conv_W_in"], CP)
    h["conv0"] = rows(a["L0_conv_conv_w"].reshape(DI, 9), 128)
    h["small0"] = np.stack([cols(a["L0_conv_" + n], 128) for n in ("conv_b", "b_dt", "D_param", "gamma", "beta")], 1)
    h["alog0"] = rows(a["L0_conv_A_log"], 128).reshape(128, DB * NS)
    h["wx"] = rows(a["L0_conv_W_x"], 128)
    h["wdt"] = a["L0_conv_W_dt"]
    h["wout"] = rows(a["L0_conv_W_out"], 128)
    h["dw1"] = rows(a["L1_conv_dw_kernel"].reshape(K1 * K1, C).T, CP)
    h["small1"] = np.stack([cols(a["L1_conv_" + n], CP) for n in ("dw_bias", "ln_gamma", "ln_beta", "b1", "gamma")], 1)
    h["w0"] = rows(a["L1_conv_w0"], CP)
    h["b0"] = cols(a["L1_conv_b0"], 128)
    h["w1"] = rows(a["L1_conv_w1"], 128)
    k2 = a["L2_conv_kernel"]
    grp = 12
    near = np.array([[2, 1], [1, 2], [0, 2], [0, 1], [1, 0], [2, 0]])
    k6, s6 = np.arange(grp) % 6, np.arange(grp) // 6
    sign = np.where(s6 == 0, 1, -1)
    act = (k6[:, None] + sign[:, None] * np.arange(6)[None, :]) % 6
    mult = (k6[:, None] + sign[:, None] * k6[None, :]) % 6 + 6 * (s6[:, None] ^ s6[None, :])
    py, px = np.ones((grp, 7), int), np.ones((grp, 7), int)
    py[:, 1:], px[:, 1:] = near[act][:, :, 0], near[act][:, :, 1]
    gg, tt, hh = np.meshgrid(np.arange(grp), np.arange(7), np.arange(grp), indexing="ij")
    full = np.zeros((3, 3, grp, 16, grp, 16), k2.dtype)
    full[py[gg, tt], px[gg, tt], mult[gg, hh], :, gg, :] = k2[tt, hh]
    full = full.reshape(3, 3, C, C)
    h["ke"] = np.stack([full[y, x].reshape(CB, CP, C) for y, x in TAPS2], 0).transpose(2, 1, 0, 3)
    w3 = a["L3_conv_in_proj_w"].T
    xs, bs, cs, dts = w3[:, DI:2 * DI], w3[:, 2 * DI:2 * DI + 64], w3[:, 2 * DI + 64:2 * DI + 128], w3[:, 2 * DI + 128:]
    h["win3"] = rows(np.concatenate([xs, bs, bs, cs, cs, np.repeat(dts, 128, axis=1)], 1), CP)
    h["wz3"] = rows(w3[:, :DI], CP)

    def doubled(v):
        return np.concatenate([v[:DI], v[DI:DI + 64], v[DI:DI + 64], v[DI + 64:], v[DI + 64:]], 0)

    h["conv3"] = rows(doubled(a["L3_conv_conv_w"].reshape(DI + 128, 9)), 128)
    h["small3"] = np.concatenate([cols(doubled(a["L3_conv_conv_b"]), 128), on_all(a["L3_conv_dt_bias"]), on_all(a["L3_conv_A_log"]),
                                  on_all(a["L3_conv_Ds"]), cols(a["L3_conv_norm_w"], 128)], 1)
    h["wout3"] = rows(a["L3_conv_out_proj_w"].T, 128)
    h["ident"] = np.eye(128, dtype=np.float32)
    h["group"] = (np.kron(np.eye(CP // 6), np.ones((6, 6))) / 6).astype(np.float32)
    h["tri"] = np.triu(np.ones((128, 128), np.float32))
    pick = np.tile(np.eye(2 * NS, dtype=np.float32), (3, 1))
    h["onehot"] = np.repeat(pick[:, :, None], 128, 2).astype(ml_dtypes.bfloat16)

    nc = bacc.Bacc("TRN2", target_bir_lowering=False, num_devices=1)
    arrays, args = {}, []
    for name in ("x", "win", "conv0", "small0", "alog0", "wx", "wdt", "wout", "dw1", "small1", "w0", "b0", "w1", "ke",
                 "win3", "conv3", "small3", "wz3", "wout3", "ident", "group", "tri", "onehot"):
        v = np.ascontiguousarray(h[name])
        arrays[f"in_{name}"] = v
        args.append(nc.dram_tensor(f"in_{name}", v.shape, mb.dt.from_np(v.dtype), kind="ExternalInput").ap())
    args.append(nc.dram_tensor("out_x", (NB, CP, CB, T), F32, kind="ExternalOutput").ap())
    build(nc, *args)
    r = run(nc, [arrays], core_ids=[0])
    got = r.results[0]["out_x"]
    return got.transpose(0, 3, 2, 1).reshape(NB, SIDE, SIDE, C)
```

```python
from contextlib import ExitStack

import concourse.bass as bass
from concourse import mybir

F32 = mybir.dt.float32
BF16 = mybir.dt.bfloat16
U32 = mybir.dt.uint32
ALU = mybir.AluOpType
ACT = mybir.ActivationFunctionType
AX_X = mybir.AxisListType.X

NB, SIDE, C = 4, 32, 192
T = SIDE * SIDE
HALF = 512
CP = 96
CB = C // CP
DI, DB = 384, 3
NS = 16
RANK = 12
MLP, MB = 768, 6
K1 = 7
P3, P7 = SIDE + 2, SIDE + K1 - 1
HD, ND = 3, 4
SB = T // 128
BANK3 = (2, 4, 6, 2, 4)
GUARD = 27.631021115928547
TAPS2 = [(y, x) for y in range(3) for x in range(3) if (y, x) not in ((0, 0), (2, 2))]
TRI = [sum(T - 128 * i for i in range(s)) for s in range(SB + 1)]
ORDER = (0, 1, 3, 2)
TAPS_DVE, TAPS_PE, TAPS_POOL = range(23), range(23, 38), range(38, 49)
SHARE = 4
DRIVES = 3 * NS + NS // SHARE
PRODUCTS = 8 + 2 * (len(TAPS_POOL) - 1) + 8


def drives(n):
    return 3 * n + (n + SHARE - 1) // SHARE


class Steps:

    def __init__(self, eng, sem, per_image, image):
        self.eng, self.sem, self.per, self.image, self.n = eng, sem, per_image, image, 0

    def done(self, ins):
        ins.then_inc(self.sem, 1)
        self.n += 1
        self.eng.wait_ge(self.sem, self.image * self.per + self.n)

    def end(self):
        assert self.n == self.per, (self.sem, self.n)


ACT_STEPS, DVE_STEPS, STAGES = 7, 125, 9


def build(nc, x, win, conv0, small0, alog0, wx, wdt, wout, dw1, small1, w0, b0, w1, ke,
          win3, conv3, small3, wz3, wout3, wdt3, ident, group, tri, onehot, out, c_rows):
    with ExitStack() as ctx:
        def sb(name, shape, dt=F32):
            return ctx.enter_context(nc.sbuf_tensor(name, shape, dt))

        def sem(name):
            return ctx.enter_context(nc.semaphore(name))

        WIN = sb("WIN", [CP, CB, 2 * DI])
        CONV0 = sb("CONV0", [128, DB, 9])
        SMALL0 = sb("SMALL0", [128, 5, DB])
        D4 = sb("D4", [128, DB])
        A0 = sb("A0", [128, DB * NS])
        IDENT = sb("IDENT", [128, 128])
        GROUP = sb("GROUP", [CP, CP])
        TRIM = sb("TRIM", [128, 128])
        ONES = sb("ONES", [128, 128])
        ONEHOT = sb("ONEHOT", [3 * 2 * NS, NS, 128], BF16)
        GCOL = sb("GCOL", [128, 1])
        MHALF = sb("MHALF", [128, 1])
        EPS5 = sb("EPS5", [128, 1])
        EPS6 = sb("EPS6", [128, 1])
        SMALL3 = sb("SMALL3", [128, 5 + HD + 12 + 12 + DB])
        CONV3 = sb("CONV3", [128, 5, 9])
        A3 = sb("A3", [128, 12])
        DSUM = sb("DSUM", [128, HD])
        SMALL1 = sb("SMALL1", [CP, 5, CB])
        DW1 = sb("DW1", [CP, CB, K1 * K1])
        B0 = sb("B0", [128, MB])
        STREAM = sb("STREAM", [128, 4 * T])
        X = STREAM[0:CP, 0:2 * T].rearrange("p (c t) -> p c t", c=CB)
        XN = STREAM[0:CP, 2 * T:4 * T].rearrange("p (c t) -> p c t", c=CB)
        WEIGHT = STREAM[:, :].rearrange("p (s k t) -> p s k t", s=2, k=2)
        ST = sb("ST", [CP, CB, 2, 6])
        MV = sb("MV", [CP, CB, 2])
        GS = sb("GS", [CP, CB, 2])
        GM = sb("GM", [CP, CB, 2])
        GV = sb("GV", [CP, CB, 2])
        ARENA = sb("ARENA", [128, 45568])

        def area(at, n, p=128):
            return ARENA[0:p, at:at + n]

        DTU = area(0, 3 * T).rearrange("p (d t) -> p d t", d=DB)
        DTUX = area(0, 4 * T).rearrange("p (d t) -> p d t", d=DB + 1)
        U = area(3072, 3 * T).rearrange("p (d t) -> p d t", d=DB)
        DT = area(6144, 3 * T).rearrange("p (d t) -> p d t", d=DB)
        S = area(9216, 12 * T).rearrange("p (d k t) -> p d k t", d=DB, k=4)
        DEC = area(21504, 8 * T).rearrange("p (s o t) -> p s o t", s=4, o=2)
        RING = area(29696, 8 * T).rearrange("p (s t) -> p s t", s=8)
        NUM = area(37888, 2 * T).rearrange("p (s t) -> p s t", s=2)
        CM = area(39936, T)
        CS = (area(40960, T), area(44544, T))
        BCS = area(41984, T // 2, 96).bitcast(BF16)
        CM2 = area(42496, T)
        YD = area(43520, T)
        WDT = area(43520, DI, RANK)
        WX = area(43904, DB * (RANK + 2 * NS)).rearrange("p (d n) -> p d n", d=DB)
        WOUT = area(42512, DB * C).rearrange("p (d n) -> p d n", d=DB)
        DIAG0 = area(12800, 9 * 128).rearrange("p (d k q) -> p d k q", d=1, k=9)
        PROD0 = area(15104, 2 * T).rearrange("p (s t) -> p s t", s=2)
        PADX = area(9216, DB * P3 * P3).rearrange("p (d h w) -> p d h w", d=DB, h=P3)
        SPA = [area(21504 + i * 3072, 3072) for i in range(5)]
        DTR = area(37888, T, RANK)
        BCF = area(38912, T, 2 * NS)
        BCH = area(39936, T // 2, 2 * NS).bitcast(BF16)
        Y0 = DTU
        SQ0 = area(9216, 3 * T)
        Z0 = area(12288, 3 * T).rearrange("p (d t) -> p d t", d=DB)
        R0 = area(15360, T)
        W0 = area(33400, CB * MLP, CP).rearrange("p (c n) -> p c n", c=CB)
        W1 = area(34936, MB * C).rearrange("p (m n) -> p m n", m=MB)
        KE = area(36088, CB * 7 * C, CP).rearrange("p (c k n) -> p c k n", c=CB, k=7)
        WIN3 = area(38776, CB * 640, CP).rearrange("p (c n) -> p c n", c=CB)
        WZ3 = area(40824, CB * DI, CP).rearrange("p (c n) -> p c n", c=CB)
        WDT3 = area(42504, CB * HD, CP).rearrange("p (c n) -> p c n", c=CB)
        WOUT3 = area(41592, DB * C).rearrange("p (d n) -> p d n", d=DB)
        PAD1 = area(0, CB * P7 * P7, CP).rearrange("p (c h w) -> p c h w", c=CB, h=P7)
        Y1 = area(2888, CB * T, CP).rearrange("p (c t) -> p c t", c=CB)
        SQ1 = area(4936, CB * T, CP)
        R1 = area(6984, T, CP)
        G1 = area(8008, MB * T).rearrange("p (m t) -> p m t", m=MB)
        O1 = area(4936, CB * T, CP).rearrange("p (c t) -> p c t", c=CB)
        PROD1 = area(19264, 2 * T, CP).rearrange("p (s t) -> p s t", s=2)
        YP1 = area(21312, CB * T, CP).rearrange("p (c t) -> p c t", c=CB)
        DIAG1 = area(16384, CB * len(TAPS_PE) * CP, CP).rearrange("p (c k q) -> p c k q", c=CB, q=CP)
        PAD2 = area(0, CB * P3 * P3, CP).rearrange("p (c h w) -> p c h w", c=CB, h=P3)
        XC = area(0, 3 * T).rearrange("p (d t) -> p d t", d=DB)
        BCAT = area(3072, 2 * T).rearrange("p (c t) -> p c t", c=2)
        CCAT = area(5120, 2 * T).rearrange("p (c t) -> p c t", c=2)
        GT = area(7168, TRI[SB])
        DIFF = area(11776, TRI[SB])
        EE = area(16384, 2 * TRI[SB]).rearrange("p (s n) -> p s n", s=2)
        XT = area(25600, 2 * T).rearrange("p (s t) -> p s t", s=2)
        YACC = area(27648, 3 * T).rearrange("p (d t) -> p d t", d=DB)
        XJ = area(30720, ND * T).rearrange("p (k t) -> p k t", k=ND)
        DTS = area(34816, HD * SB)
        CUMS = area(34840, (HD + 1) * SB)
        CUM = area(34864, 3 * T).rearrange("p (d t) -> p d t", d=DB)
        CUMX = area(34864, 4 * T).rearrange("p (d t) -> p d t", d=DB + 1)
        PAD3 = area(16384, 5 * P3 * P3).rearrange("p (d h w) -> p d h w", d=5, h=P3)
        DIAG3 = area(10240, 2 * 9 * 128).rearrange("p (d k q) -> p d k q", d=2, k=9)
        PROD3 = area(13696, 2 * T).rearrange("p (s t) -> p s t", s=2)
        SPREAD = area(7168, 3 * T).rearrange("p (j t) -> p j t", j=HD)
        SPB = [area(22200 + 32 * i, HD * SB) for i in range(6)]
        SQ3 = area(16384, 3 * T)
        Z3 = area(19456, 3 * T).rearrange("p (d t) -> p d t", d=DB)
        R3 = area(22528, T)

        PS = ctx.enter_context(nc.psum_tensor("PS", [128, 8, HALF], F32))

        def banks(first, n=2, p=128):
            return PS[0:p, first:first + n, :].rearrange("p a n -> p (a n)")

        def inner(pad, k, size=P3):
            o = k // 2
            return pad[:, o:o + SIDE, o:o + SIDE]

        def grid(ap):
            return ap.rearrange("p (h w) -> p h w", h=SIDE)

        def turned(ap):
            return ap.rearrange("p (h w) -> p w h", h=SIDE)

        def sequence(ap, k):
            v = (grid, turned)[k % 2](ap)
            return v[:, ::-1, ::-1] if k >= 2 else v

        weights_in = sem("weights_in")
        x_in = sem("x_in")
        step_weights_in = sem("step_weights_in")
        wout_in = sem("wout_in")
        late_weights_in = sem("late_weights_in")
        out_written = sem("out_written")
        consts_ready = sem("consts_ready")
        a_exp_done = sem("a_exp_done")
        stage_done = sem("stage_done")
        settled = sem("settled")
        act_steps = sem("act_steps")
        dve_steps = sem("dve_steps")
        gn_stats = sem("gn_stats")
        gn_sums = sem("gn_sums")
        gn_var = sem("gn_var")
        gn_std = sem("gn_std")
        std_ready = [sem(f"std_ready{i}") for i in range(3)]
        xn_ready = [sem(f"xn_ready{i}") for i in range(4)]
        xn_again = sem("xn_again")
        pads_clear = sem("pads_clear")
        xval_ready = sem("xval_ready")
        pad_filled = sem("pad_filled")
        conv_done = sem("conv_done")
        u_ready = sem("u_ready")
        dtr_ready = sem("dtr_ready")
        bc_ready = sem("bc_ready")
        dtr_copied = sem("dtr_copied")
        bc_split = sem("bc_split")
        dtp_ready = sem("dtp_ready")
        softplus_exps = sem("softplus_exps")
        softplus_logs = sem("softplus_logs")
        softplus_exps3 = sem("softplus_exps3")
        dt_ready = sem("dt_ready")
        dt_turned = sem("dt_turned")
        s_ready = sem("s_ready")
        decay_ready = sem("decay_ready")
        decay_free = sem("decay_free")
        weight_ready = sem("weight_ready")
        ring_free = sem("ring_free")
        b_row = sem("b_row")
        num_ready = sem("num_ready")
        drive_ready = sem("drive_ready")
        drive3_ready = sem("drive3_ready")
        h_ready = sem("h_ready")
        hsum_ready = sem("hsum_ready")
        c_row = [sem(f"c_row{i}") for i in range(2)]
        bc_kept = sem("bc_kept")
        c_stored = sem("c_stored")
        ch_ready = sem("ch_ready")
        skips_ready = sem("skips_ready")
        ch_added = sem("ch_added")
        y_ready = sem("y_ready")
        mean_sum = [sem(f"mean_sum{i}") for i in range(2)]
        centered = [sem(f"centered{i}") for i in range(2)]
        squares = [sem(f"squares{i}") for i in range(3)]
        square_sum = [sem(f"square_sum{i}") for i in range(3)]
        z_ready = [sem(f"z_ready{i}") for i in range(2)]
        z_act = [sem(f"z_act{i}") for i in range(2)]
        gated = [sem(f"gated{i}") for i in range(2)]
        layer_out = [sem(f"layer_out{i}") for i in range(4)]
        ln1_ready = sem("ln1_ready")
        hidden_ready = sem("hidden_ready")
        gelu_done = sem("gelu_done")
        dt3_ready = sem("dt3_ready")
        xbc_ready = sem("xbc_ready")
        softplus_logs3 = sem("softplus_logs3")
        pad3_filled = sem("pad3_filled")
        conv3_done = sem("conv3_done")
        prod_first = sem("prod_first")
        prod_ready = sem("prod_ready")
        prod_used = sem("prod_used")
        pool_conv_done = [sem(f"pool_conv_done{i}") for i in range(3)]
        products_merged = sem("products_merged")
        diags_ready = [sem(f"diags_ready{i}") for i in range(3)]
        pe_conv_done = [sem(f"pe_conv_done{i}") for i in range(3)]
        spread_ready = sem("spread_ready")
        row_ready = sem("row_ready")
        cum_ready = sem("cum_ready")
        dtv_ready = sem("dtv_ready")
        xbc_act = sem("xbc_act")
        g_ready = sem("g_ready")
        g_kept = sem("g_kept")
        diff_ready = sem("diff_ready")
        xj_ready = sem("xj_ready")
        xj_used = sem("xj_used")
        xt_ps = sem("xt_ps")
        xt_ready = sem("xt_ready")
        e_ready = sem("e_ready")
        m_ready = sem("m_ready")
        y3_ready = sem("y3_ready")
        yacc_added = sem("yacc_added")
        x_final = sem("x_final")

        WEIGHTS = [(WIN, win), (CONV0, conv0), (SMALL0, small0), (A0, alog0), 
                   (IDENT, ident), (GROUP, group), (TRIM, tri), (ONEHOT, onehot), (SMALL3, small3), (CONV3, conv3),
                   (SMALL1, small1), (DW1, dw1), (B0, b0)]
        LATE = [(W0, w0), (W1, w1), (KE, ke), (WIN3, win3), (WZ3, wz3), (WOUT3, wout3), (WDT3, wdt3)]

        def whole(ap):
            return ap[tuple(slice(None) for _ in ap.shape)]

        def settle(eng):
            eng.sem_inc(settled, 1)

        def stage_end(eng, b, n):
            settle(eng)
            eng.drain().then_inc(stage_done, 1)
            eng.wait_ge(stage_done, b * (5 * STAGES) + 5 * n)
            settle(eng)

        block = ctx.enter_context(nc.Block())

        @block.sync
        def _(sp):
            for to, of in WEIGHTS:
                sp.dma_start(whole(to), whole(of)).then_inc(weights_in, 16)
            with sp.Fori(0, NB) as b:
                sp.dma_start(X[:, :, :], x[bass.ds(b, 1)].rearrange("o p c t -> (o p) c t")).then_inc(x_in, 16)
                sp.dma_start(WX, whole(wx)).then_inc(step_weights_in, 16)
                sp.dma_start(WDT, whole(wdt)).then_inc(step_weights_in, 16)
                sp.wait_ge(bc_kept, b + 1)
                settle(sp)
                sp.dma_start(c_rows[:, :], BCF[NS:2 * NS, :]).then_inc(c_stored, 16)
                sp.wait_ge(c_stored, b * 16 + 16)
                settle(sp)
                stage_end(sp, b, 1)
                with sp.Fori(0, DB) as d:
                    for n in range(NS):
                        sp.wait_ge(ch_ready, b * (DB * NS) + d * NS + (n + 1))
                        settle(sp)
                        sp.dma_start(CS[n % 2], c_rows[n:n + 1, :].to_broadcast([128, T])).then_inc(c_row[n % 2], 16)
                stage_end(sp, b, 2)
                sp.dma_start(X[:, :, :], x[bass.ds(b, 1)].rearrange("o p c t -> (o p) c t")).then_inc(x_in, 16)
                sp.dma_start(WOUT, whole(wout)).then_inc(wout_in, 16)
                for to, of in LATE:
                    sp.dma_start(to, whole(of)).then_inc(late_weights_in, 16)
                for n in range(3, STAGES):
                    stage_end(sp, b, n)
                sp.wait_ge(x_final, b + 1)
                sp.dma_start(out[bass.ds(b, 1)].rearrange("o p c t -> (o p) c t"), X[:, :, :]).then_inc(out_written, 16)
                sp.wait_ge(out_written, b * 16 + 16)
                settle(sp)
                stage_end(sp, b, STAGES)

        @block.gpsimd
        def _(pool):
            nc.gpsimd.memset(ONES[:, :], 1.0).then_inc(consts_ready, 1)
            nc.gpsimd.memset(GCOL[:, :], GUARD).then_inc(consts_ready, 1)
            nc.gpsimd.memset(MHALF[:, :], -0.5).then_inc(consts_ready, 1)
            nc.gpsimd.memset(EPS5[:, :], 1e-5).then_inc(consts_ready, 1)
            nc.gpsimd.memset(EPS6[:, :], 1e-6).then_inc(consts_ready, 1)

            def diagonals(to, w, blocks, taps, p):
                for d in range(blocks):
                    for i, t in enumerate(taps):
                        ins = nc.gpsimd.tensor_scalar(to[:, d, i, :], IDENT[0:p, 0:p], w(d, t), None, ALU.mult)
                return ins

            pool.wait_ge(weights_in, 16 * len(WEIGHTS))
            with pool.Fori(0, NB) as b:
                nc.gpsimd.memset(PADX[:, :, :, :], 0.0).then_inc(pads_clear, 1)
                diagonals(DIAG0, lambda d, t: CONV0[:, 1, t:t + 1], 1, range(9), 128).then_inc(diags_ready[0], 1)

                def add_products(to, slots, first, base, n, done):
                    pool.wait_ge(prod_first, b * 4 + first)
                    for i in range(base, base + n):
                        pool.wait_ge(prod_ready, b * PRODUCTS + (i + 1))
                        if i > base:
                            pool.wait_ge(prod_used, b * PRODUCTS + (i + 2))
                        nc.gpsimd.tensor_tensor(to, to, slots[:, i % 2, :], ALU.add).then_inc(prod_used, 1)
                    pool.wait_ge(prod_used, b * PRODUCTS + (base + n + 2))
                    pool.sem_inc(done, 1)

                add_products(U[:, 2, :], PROD0, 1, 0, 8, pool_conv_done[0])
                pool.wait_ge(dt_ready, b + 1)
                pool.wait_ge(u_ready, b * DB + DB)
                nc.gpsimd.tensor_tensor(DTU.rearrange("p d t -> p (d t)"), DT.rearrange("p d t -> p (d t)"),
                                        U.rearrange("p d t -> p (d t)"), ALU.mult)
                stage_end(pool, b, 1)
                with pool.Fori(0, DB) as d:
                    u0 = b * (DB * NS) + d * NS
                    for n in range(NS):
                        for k in (ORDER if n % SHARE == 0 else range(3)):
                            if k == 0:
                                pool.wait_ge(num_ready, u0 + b + (n + 1))
                                pool.wait_ge(weight_ready, u0 * 2 + (2 * n + 1))
                            if k == (3 if n % SHARE == 0 else 2):
                                pool.wait_ge(weight_ready, u0 * 2 + (2 * n + 2))
                            slot, num = RING[:, (4 * n + k) % 8, :], NUM[:, n % 2, :]
                            if k < 2:
                                pool.wait_ge(ring_free, u0 * 4 + (4 * n + ORDER.index(k) + 1))
                                ins = nc.gpsimd.tensor_tensor(slot, WEIGHT[:, n % 2, k, :], num, ALU.mult)
                            else:
                                ins = nc.gpsimd.tensor_tensor(grid(slot), grid(slot), turned(num), ALU.mult)
                            ins.then_inc(drive_ready, 1)
                stage_end(pool, b, 2)
                diagonals(DIAG1, lambda d, t: DW1[:, d, t:t + 1], CB, TAPS_PE, CP).then_inc(diags_ready[1], 1)
                stage_end(pool, b, 3)
                nc.gpsimd.memset(PAD1[:, :, :, :], 0.0).then_inc(pads_clear, 1)
                for c in range(CB):
                    m = len(TAPS_POOL) - 1
                    add_products(YP1[:, c, :], PROD1, 2 + c, 8 + m * c, m, pool_conv_done[1])
                stage_end(pool, b, 4)
                nc.gpsimd.memset(PAD2[:, :, :, :], 0.0).then_inc(pads_clear, 1)
                diagonals(DIAG3, lambda d, t: CONV3[:, d + 3, t:t + 1], 2, range(9), 128).then_inc(diags_ready[2], 1)
                nc.gpsimd.memset(PAD3[:, :, :, :], 0.0).then_inc(pads_clear, 1)
                stage_end(pool, b, 5)
                add_products(XC[:, 2, :], PROD3, 4, PRODUCTS - 8, 8, pool_conv_done[2])
                stage_end(pool, b, 6)
                stage_end(pool, b, 7)
                with pool.Fori(0, HD) as j:
                    pool.wait_ge(xj_used, b * HD + j + 1)
                    settle(pool)
                    xc = XC[:, bass.ds(j, 1), :].rearrange("p o t -> p (o t)")
                    nc.gpsimd.tensor_copy(XJ[:, 0, :], xc).then_inc(xj_ready, 1)
                    pool.wait_ge(xj_ready, (b * HD + j) * ND + 1)
                    settle(pool)
                    for k in range(1, ND):
                        nc.gpsimd.tensor_copy(XJ[:, k, :].rearrange("p (a c) -> p a c", a=SIDE),
                                              sequence(XJ[:, 0, :], k)).then_inc(xj_ready, 1)
                stage_end(pool, b, 8)
                stage_end(pool, b, STAGES)

        @block.scalar
        def _(act):
            act.wait_ge(weights_in, 16 * len(WEIGHTS))
            act.wait_ge(consts_ready, 5)
            nc.scalar.activation(A0[:, :], A0[:, :], ACT.Exp).then_inc(a_exp_done, 1)
            nc.scalar.activation(A3[:, :], SMALL3[:, 8:20], ACT.Exp).then_inc(a_exp_done, 1)
            with act.Fori(0, NB) as b:
                st = Steps(act, act_steps, ACT_STEPS, b)

                def softplus(values, biases, scratch, exps_done, done):
                    t1, t2, t3, t4 = scratch[:4]
                    n = values[0].shape[-1]

                    def each(to, func):
                        for i, value in enumerate(values):
                            bias = {} if biases is None else {"bias": biases[:, i:i + 1]}
                            ins = nc.scalar.activation(to[:, i * n:(i + 1) * n], value, func, **bias)
                        return ins

                    st.done(each(t1, ACT.Abs))
                    st.done(nc.scalar.activation(t1, t1, ACT.Exp, scale=-1.0))
                    nc.scalar.activation(t4, t1, ACT.Identity, bias=MHALF[:, 0:1], scale=1.0 / 3.0).then_inc(exps_done, 1)
                    each(t3, ACT.Relu)
                    nc.scalar.activation(t2, t1, ACT.Ln, bias=1.0).then_inc(done, 1)

                def group_std(layer):
                    act.wait_ge(gn_var, b * 4 + (layer + 1))
                    nc.scalar.activation(GV[:, :, 0], GV[:, :, 0], ACT.Sqrt, bias=EPS5[0:CP, 0:1]).then_inc(gn_std, 1)

                def layer_std(i, to, sums, n, eps):
                    act.wait_ge(square_sum[i], b + 1)
                    st.done(nc.scalar.activation(to, sums, ACT.Ln, bias=eps, scale=1.0 / n))
                    nc.scalar.activation(to, to, ACT.Exp, scale=-0.5).then_inc(std_ready[i], 1)

                def products(to, slots, pad, w, taps, k, base):
                    for i, t in enumerate(taps):
                        view = pad[:, t // k:t // k + SIDE, t % k:t % k + SIDE]
                        if i == 0:
                            nc.scalar.activation(grid(to), view, ACT.Copy, scale=w[:, t:t + 1]).then_inc(prod_first, 1)
                            continue
                        n = base + i - 1
                        act.wait_ge(prod_used, b * PRODUCTS + (n + 1))
                        nc.scalar.activation(grid(slots[:, n % 2, :]), view, ACT.Copy, scale=w[:, t:t + 1]).then_inc(prod_ready, 1)

                group_std(0)
                for i in range(DB):
                    act.wait_ge(xval_ready, b * DB + (i + 1))
                    if i == 0:
                        act.wait_ge(pads_clear, b * 4 + 1)
                    nc.scalar.activation(inner(PADX[:, i], 3), grid(banks(2 * i)), ACT.Copy).then_inc(pad_filled, 1)
                act.wait_ge(pad_filled, b * DB + DB)
                products(U[:, 2, :], PROD0, PADX[:, 2], CONV0[:, 2, :], range(9), 3, 0)
                for i in range(DB):
                    act.wait_ge((conv_done, pe_conv_done[0], pool_conv_done[0])[i], b + 1)
                    src = banks(6) if i == 1 else U[:, i, :]
                    nc.scalar.activation(U[:, i, :], src, ACT.Silu, bias=SMALL0[:, 0, i:i + 1]).then_inc(u_ready, 1)
                act.wait_ge(dtr_ready, b + 1)
                nc.scalar.activation(DTR, banks(6, 2, RANK), ACT.Copy).then_inc(dtr_copied, 1)
                act.wait_ge(dtp_ready, b + 1)
                softplus([banks(2), banks(4), banks(6)], SMALL0[:, 1, :], SPA, softplus_exps, softplus_logs)
                act.wait_ge(dt_ready, b + 1)
                for i in range(DB):
                    nc.scalar.activation(SPA[0][:, i * T:(i + 1) * T].rearrange("p (w h) -> p w h", w=SIDE),
                                         turned(DT[:, i, :]), ACT.Copy).then_inc(dt_turned, 1)
                stage_end(act, b, 1)
                with act.Fori(0, DB) as d:
                    u0 = b * (DB * NS) + d * NS
                    dt = DT[:, bass.ds(d, 1), :].rearrange("p o t -> p (o t)")

                    for n in range(NS):
                        if n % 2 == 0:
                            for m in (n, n + 1):
                                a = A0[:, bass.ds(d * NS + m, 1)]
                                act.wait_ge(decay_free, u0 + (m + 1))
                                settle(act)
                                nc.scalar.activation(DEC[:, m % 4, 0, :], dt, ACT.Exp, scale=a)
                                nc.scalar.activation(DEC[:, m % 4, 1, :].rearrange("p (w h) -> p w h", w=SIDE),
                                                     turned(dt), ACT.Exp, scale=a).then_inc(decay_ready, 1)
                        for k in (0, 2):
                            s = S[:, bass.ds(d, 1), k:k + 2, :].rearrange("p o k t -> p (o k t)")
                            if k == 0:
                                act.wait_ge(drive_ready, (b * DB + d) * DRIVES + (drives(n - 2) + 8))
                                to = WEIGHT[:, n % 2, :, :]
                            else:
                                act.wait_ge(ring_free, u0 * 4 + (4 * n + 4))
                                to = RING[:, (4 * n + 2) % 8:(4 * n + 2) % 8 + 2, :]
                            settle(act)
                            nc.scalar.activation(to.rearrange("p k t -> p (k t)"), s, ACT.Sigmoid,
                                                 bias=GCOL[:, 0:1], scale=A0[:, bass.ds(d * NS + n, 1)]).then_inc(weight_ready, 1)
                        if n == 1:
                            act.wait_ge(y_ready, b * DB + d + 1)
                            settle(act)
                            ud = U[:, bass.ds(d, 1), :].rearrange("p o t -> p (o t)")
                            nc.scalar.activation(YD, ud, ACT.Copy, scale=D4[:, bass.ds(d, 1)]).then_inc(skips_ready, 1)
                stage_end(act, b, 2)
                act.wait_ge(centered[0], b + 1)
                nc.scalar.activation(SQ0, Y0.rearrange("p d t -> p (d t)"), ACT.Square).then_inc(squares[0], 1)
                for i in range(DB):
                    act.wait_ge(z_ready[0], b * DB + (i + 1))
                    nc.scalar.activation(Z0[:, i, :], banks((4, 6, 0)[i]), ACT.Silu).then_inc(z_act[0], 1)
                layer_std(0, R0, banks(2), DI, EPS5[:, 0:1])
                stage_end(act, b, 3)
                group_std(1)
                act.wait_ge(xn_ready[1], b + 1)
                for c in range(CB):
                    products(YP1[:, c, :], PROD1, PAD1[:, c], DW1[:, c, :], TAPS_POOL, K1, 8 + (len(TAPS_POOL) - 1) * c)
                act.wait_ge(centered[1], b + 1)
                nc.scalar.activation(SQ1, Y1.rearrange("p c t -> p (c t)"), ACT.Square).then_inc(squares[1], 1)
                layer_std(1, R1, banks(2, 2, CP), C, EPS6[0:CP, 0:1])
                for m in range(MB):
                    act.wait_ge(hidden_ready, b * MB + (m + 1))
                    nc.scalar.activation(G1[:, m, :], banks(4 + 2 * (m % 2)), ACT.Gelu, bias=B0[:, m:m + 1]).then_inc(gelu_done, 1)
                stage_end(act, b, 4)
                group_std(2)
                stage_end(act, b, 5)
                group_std(3)
                act.wait_ge(dtv_ready, b + 1)
                softplus([SPB[5]], None, SPB, softplus_exps3, softplus_logs3)
                act.wait_ge(pads_clear, b * 4 + 4)
                for i in range(5):
                    act.wait_ge(xbc_ready, b * 5 + (i + 1))
                    nc.scalar.activation(inner(PAD3[:, i], 3), grid(banks(BANK3[i])), ACT.Copy).then_inc(pad3_filled, 1)
                act.wait_ge(pad3_filled, b * 5 + 5)
                products(XC[:, 2, :], PROD3, PAD3[:, 2], CONV3[:, 2, :], range(9), 3, PRODUCTS - 8)
                for i in range(3):
                    act.wait_ge((conv3_done, conv3_done, pool_conv_done[2])[i], (b * 2 + 1, b * 2 + 2, b + 1)[i])
                    nc.scalar.activation(XC[:, i, :], XC[:, i, :], ACT.Silu, bias=SMALL3[:, i:i + 1]).then_inc(xbc_act, 1)
                for i, cat in enumerate((BCAT, CCAT)):
                    act.wait_ge(pe_conv_done[2], b * 2 + (i + 1))
                    for k in range(ND):
                        p = slice(64 * (k % 2), 64 * (k % 2) + 64)
                        nc.scalar.activation(cat[p, k // 2, :].rearrange("p (a c) -> p a c", a=SIDE),
                                             sequence(banks(BANK3[3 + i])[p, :], k), ACT.Silu,
                                             bias=SMALL3[p, 3 + i:4 + i]).then_inc(xbc_act, 1)
                stage_end(act, b, 6)
                for s in range(SB):
                    act.wait_ge(g_ready, b * SB + (s + 1))
                    nc.scalar.activation(GT[:, TRI[s]:TRI[s + 1]], banks(2 * (s % 4))[:, 128 * s:T], ACT.Copy).then_inc(g_kept, 1)
                stage_end(act, b, 7)
                with act.Fori(0, HD) as j:
                    for k in range(ND):
                        h = b * 12 + j * 4
                        if k == 0:
                            act.wait_ge(diff_ready, b * (HD + 1) + j + 1)
                        act.wait_ge(y3_ready, h + (k + 1))
                        settle(act)
                        ins = nc.scalar.activation(EE[:, k % 2, :], DIFF, ACT.Exp, scale=A3[:, bass.ds(j + 3 * k, 1)])
                        ins.then_inc(e_ready, 1)
                stage_end(act, b, 8)
                for i in range(DB):
                    act.wait_ge(z_ready[1], b * DB + (i + 1))
                    nc.scalar.activation(Z3[:, i, :], banks((4, 6, 0)[i]), ACT.Silu).then_inc(z_act[1], 1)
                act.wait_ge(gated[1], b * 2 + 1)
                nc.scalar.activation(SQ3, YACC.rearrange("p d t -> p (d t)"), ACT.Square).then_inc(squares[2], 1)
                layer_std(2, R3, banks(2), DI, EPS5[:, 0:1])
                stage_end(act, b, STAGES)
                st.end()

        @block.vector
        def _(dve):
            dve.wait_ge(a_exp_done, 2)
            dve.wait_ge(weights_in, 16 * len(WEIGHTS))
            nc.vector.tensor_scalar(A0[:, :], A0[:, :], -1.0, None, ALU.mult).then_inc(consts_ready, 1)
            nc.vector.tensor_scalar(A3[:, :], A3[:, :], -1.0, None, ALU.mult).then_inc(consts_ready, 1)
            nc.vector.tensor_scalar(D4[:, :], SMALL0[:, 2, :], 4.0, None, ALU.mult).then_inc(consts_ready, 1)
            nc.vector.tensor_reduce(DSUM[:, :], SMALL3[:, 20:32].rearrange("p (k j) -> p j k", k=ND), AX_X,
                                    ALU.add).then_inc(consts_ready, 1)
            dve.wait_ge(consts_ready, 9)
            with dve.Fori(0, NB) as b:
                st = Steps(dve, dve_steps, DVE_STEPS, b)
                v = nc.vector

                def group_norm(layer, to):
                    for c in range(CB):
                        for h in range(2):
                            ins = v.bn_stats(ST[:, c, h, :], X[:, c, h * HALF:(h + 1) * HALF])
                    st.done(ins)
                    settle(dve)
                    for c in range(CB):
                        ins = v.bn_aggr(MV[:, c, :], ST[:, c].rearrange("p h s -> p (h s)"))
                    st.done(ins)
                    st.done(v.tensor_tensor(GS[:, :, 1], MV[:, :, 0], MV[:, :, 0], ALU.mult))
                    v.tensor_copy(GS[:, :, 0], MV[:, :, 0])
                    v.tensor_tensor(GS[:, :, 1], GS[:, :, 1], MV[:, :, 1], ALU.add).then_inc(gn_stats, 1)
                    dve.wait_ge(gn_sums, b * 4 + (layer + 1))
                    st.done(v.tensor_copy(GM[:, :, :].rearrange("p c s -> p (c s)"), banks(0, 1, CP)[:, 0:2 * CB]))
                    st.done(v.tensor_tensor(GV[:, :, 0], GM[:, :, 0], GM[:, :, 0], ALU.mult))
                    v.tensor_tensor(GV[:, :, 0], GM[:, :, 1], GV[:, :, 0], ALU.subtract).then_inc(gn_var, 1)
                    dve.wait_ge(gn_std, b * 4 + (layer + 1))
                    st.done(v.reciprocal(GV[:, :, 0], GV[:, :, 0]))
                    for c in range(CB):
                        ins = v.tensor_scalar(to[c], grid(X[:, c, :]), GM[:, c, 0:1], GV[:, c, 0:1],
                                              ALU.subtract, ALU.mult)
                        if c == CB - 1:
                            ins.then_inc(xn_ready[layer], 1)

                def conv(to, pad, w, k, bias, sem_done, taps=None):
                    taps = taps or k * k
                    for t in range(taps):
                        view = pad[:, t // k:t // k + SIDE, t % k:t % k + SIDE]
                        if t == 0:
                            st.done(v.tensor_scalar(grid(to), view, w[:, 0:1], bias, ALU.mult, ALU.add)
                                    if bias is not None else v.tensor_scalar(grid(to), view, w[:, 0:1], None, ALU.mult))
                            continue
                        ins = v.scalar_tensor_tensor(grid(to), view, w[:, t:t + 1], grid(to), ALU.mult, ALU.add)
                        if t == taps - 1 and sem_done is not None:
                            ins.then_inc(sem_done, 1)
                        else:
                            st.done(ins)

                def softplus(scratch, to, exps, logs):
                    e, log, top, t, mask = scratch[:5]
                    dve.wait_ge(exps, b + 1)
                    v.tensor_scalar(mask, e, 2.0 ** -8, None, ALU.is_lt)
                    st.done(v.tensor_tensor(t, t, e, ALU.mult))
                    st.done(v.scalar_tensor_tensor(t, t, 1.0, e, ALU.add, ALU.mult))
                    dve.wait_ge(logs, b + 1)
                    settle(dve)
                    st.done(v.copy_predicated(log, mask.bitcast(U32), t))
                    return v.tensor_tensor(to, log, top, ALU.add)

                dve.wait_ge(x_in, b * 32 + 16)
                group_norm(0, [grid(XN[:, c, :]) for c in range(CB)])
                dve.wait_ge(pad_filled, b * DB + 1)
                conv(U[:, 0, :], PADX[:, 0], CONV0[:, 0, :], 3, None, conv_done)
                dve.wait_ge(bc_ready, b + 1)
                v.tensor_copy(BCF, banks(0, 2, 2 * NS)).then_inc(bc_kept, 1)
                dve.wait_ge(bc_kept, b + 1)
                settle(dve)
                for part in range(3):
                    st.done(v.tensor_copy(BCH, BCF))
                    ins = v.tensor_copy(BCS[32 * part:32 * part + 32, :], BCH)
                    if part == 2:
                        ins.then_inc(bc_split, 1)
                    else:
                        if part == 0:
                            dve.wait_ge(c_stored, b * 16 + 16)
                        st.done(v.tensor_tensor(BCF, BCF, BCH, ALU.subtract))
                softplus(SPA, DT.rearrange("p d t -> p (d t)"), softplus_exps, softplus_logs).then_inc(dt_ready, 1)
                dve.wait_ge(dt_ready, b + 1)
                for k in range(4):
                    for i in range(DB):
                        if k == 2:
                            dve.wait_ge(dt_turned, b * DB + (i + 1))
                        src = DT[:, i, :] if k < 2 else SPA[0][:, i * T:(i + 1) * T]
                        to = S[:, i, k, :]
                        if k % 2:
                            src, to = src[:, ::-1], to[:, ::-1]
                        v.tensor_tensor_scan(to, src, src, 0.0, ALU.add, ALU.max)
                stage_end(dve, b, 1)

                def numerator(n, dtu, wait):
                    dve.wait_ge(b_row, wait)
                    v.tensor_tensor(NUM[:, n % 2, :], dtu.rearrange("p o t -> p (o t)"), banks(4), ALU.mult).then_inc(num_ready, 1)

                numerator(0, DTUX[:, 0:1, :], b * (DB * NS + 2) + 1)
                with dve.Fori(0, DB) as d:
                    u0 = b * (DB * NS) + d * NS

                    def weigh(n):
                        dve.wait_ge(hsum_ready, u0 + (n + 1))
                        dve.wait_ge(c_row[n % 2], b * (DB * NS * 8) + d * (NS * 8) + (n // 2 * 16 + 16))
                        if n % 2 == 0 and n > 0:
                            dve.wait_ge(ch_added, (b * DB + d) * (NS // 2 - 1) + n // 2)
                        v.tensor_tensor((CM, CM2)[n % 2], banks(2 * (n % 2)), CS[n % 2], ALU.mult).then_inc(ch_ready, 1)

                    def merge(n):
                        dve.wait_ge(ch_ready, u0 + (n + 3))
                        v.tensor_tensor(CM, CM, CM2, ALU.add).then_inc(products_merged, 1)

                    for n in range(NS):
                        nxt = DTUX[:, bass.ds(d, 1), :] if n < NS - 1 else DTUX[:, bass.ds(d + 1, 1), :]
                        numerator(n + 1, nxt, u0 + 2 * b + (n + 2))
                        for k in ORDER:
                            if k == 0:
                                dve.wait_ge(decay_ready, u0 + (n + 1))
                            if k == 3 and n % SHARE:
                                dve.wait_ge(drive3_ready, (b * DB + d) * (4 * NS - DRIVES) + (4 * n - drives(n) + 1))
                            else:
                                made = ORDER.index(k) if n % SHARE == 0 else k
                                dve.wait_ge(drive_ready, (b * DB + d) * DRIVES + (drives(n) + made + 7))
                            a, w = DEC[:, n % 4, k // 2, :], RING[:, (4 * n + k) % 8, :]
                            if k % 2:
                                a, w = a[:, ::-1], w[:, ::-1]
                            ins = v.tensor_tensor_scan(w, a, w, 0.0, ALU.mult, ALU.add)
                            ins.then_inc(h_ready, 1)
                            if k == 1 and n >= 1:
                                weigh(n - 1)
                            if k == 0 and n % SHARE:
                                dve.wait_ge(weight_ready, u0 * 2 + (2 * n + 2))
                                dve.wait_ge(num_ready, u0 + b + (n + 1))
                                slot = grid(RING[:, (4 * n + 3) % 8, :])
                                v.tensor_tensor(slot, slot, turned(NUM[:, n % 2, :]), ALU.mult).then_inc(drive3_ready, 1)
                            if k == 3 and n >= 2 and n % 2 == 0:
                                merge(n - 1)
                        dve.wait_ge(h_ready, u0 * 4 + (4 * n + 4))
                        dve.sem_inc(decay_free, 1)
                    weigh(NS - 1)
                    merge(NS - 1)
                    dve.wait_ge(products_merged, (b * DB + d) * (NS // 2) + NS // 2)
                    dve.wait_ge(ch_added, (b * DB + d) * (NS // 2 - 1) + (NS // 2 - 1))
                    settle(dve)
                    yd = Y0[:, bass.ds(d, 1), :].rearrange("p o t -> p (o t)")
                    v.tensor_tensor(yd, banks(6), CM, ALU.add).then_inc(y_ready, 1)
                stage_end(dve, b, 2)
                dve.wait_ge(x_in, b * 32 + 32)
                for c in range(CB):
                    ins = v.tensor_scalar(XN[:, c, :], X[:, c, :], GM[:, c, 0:1], GV[:, c, 0:1], ALU.subtract, ALU.mult)
                ins.then_inc(xn_again, 1)
                dve.wait_ge(mean_sum[0], b + 1)
                for i in range(DB):
                    ins = v.scalar_tensor_tensor(Y0[:, i, :], banks(0), -1.0 / DI, Y0[:, i, :], ALU.mult, ALU.add)
                ins.then_inc(centered[0], 1)
                dve.wait_ge(centered[0], b + 1)
                dve.wait_ge(std_ready[0], b + 1)
                for i in range(DB):
                    st.done(v.scalar_tensor_tensor(Y0[:, i, :], Y0[:, i, :], SMALL0[:, 3, i:i + 1], R0, ALU.mult, ALU.mult))
                for i in range(DB):
                    dve.wait_ge(z_act[0], b * DB + (i + 1))
                    ins = v.scalar_tensor_tensor(Y0[:, i, :], Y0[:, i, :], SMALL0[:, 4, i:i + 1], Z0[:, i, :], ALU.add, ALU.mult)
                ins.then_inc(gated[0], 1)

                def residual(layer, first=2):
                    dve.wait_ge(layer_out[layer], b + 1)
                    for c in range(CB):
                        ins = v.tensor_tensor(X[:, c, :], X[:, c, :], banks(first + 2 * c, 2, CP), ALU.add)
                        if c == CB - 1 and layer < 3:
                            st.done(ins)
                    return ins

                residual(0)
                stage_end(dve, b, 3)
                dve.wait_ge(pads_clear, b * 4 + 2)
                group_norm(1, [inner(PAD1[:, c], K1) for c in range(CB)])
                dve.wait_ge(xn_ready[1], b + 1)
                for c in range(CB):
                    conv(Y1[:, c, :], PAD1[:, c], DW1[:, c, :], K1, SMALL1[:, 0, c:c + 1], None, len(TAPS_DVE))
                dve.wait_ge(pool_conv_done[1], b * CB + CB)
                for c in range(CB):
                    st.done(v.tensor_tensor(Y1[:, c, :], Y1[:, c, :], YP1[:, c, :], ALU.add))
                dve.wait_ge(pe_conv_done[1], b + 1)
                for c in range(CB):
                    ins = v.tensor_tensor(Y1[:, c, :], Y1[:, c, :], banks(4 + 2 * c, 2, CP), ALU.add)
                ins.then_inc(ln1_ready, 1)
                dve.wait_ge(ln1_ready, b * 2 + 1)
                dve.wait_ge(mean_sum[1], b + 1)
                for c in range(CB):
                    ins = v.scalar_tensor_tensor(Y1[:, c, :], banks(0, 2, CP), -1.0 / C, Y1[:, c, :], ALU.mult, ALU.add)
                ins.then_inc(centered[1], 1)
                dve.wait_ge(centered[1], b + 1)
                dve.wait_ge(std_ready[1], b + 1)
                for c in range(CB):
                    st.done(v.scalar_tensor_tensor(Y1[:, c, :], Y1[:, c, :], SMALL1[:, 1, c:c + 1], R1, ALU.mult, ALU.mult))
                for c in range(CB):
                    ins = v.tensor_scalar(Y1[:, c, :], Y1[:, c, :], SMALL1[:, 2, c:c + 1], None, ALU.add)
                ins.then_inc(ln1_ready, 1)
                dve.wait_ge(layer_out[1], b + 1)
                for c in range(CB):
                    st.done(v.tensor_scalar(O1[:, c, :], banks(2 * c, 2, CP), SMALL1[:, 3, c:c + 1], SMALL1[:, 4, c:c + 1],
                                            ALU.add, ALU.mult))
                    st.done(v.tensor_tensor(X[:, c, :], X[:, c, :], O1[:, c, :], ALU.add))
                stage_end(dve, b, 4)
                dve.wait_ge(pads_clear, b * 4 + 3)
                group_norm(2, [inner(PAD2[:, c], 3) for c in range(CB)])
                residual(2)
                stage_end(dve, b, 5)
                group_norm(3, [grid(XN[:, c, :]) for c in range(CB)])
                dve.wait_ge(dt3_ready, b + 1)
                v.tensor_tensor(SPB[5].rearrange("p (j s) -> p s j", j=HD), banks(0, 1)[:, 0:HD * SB].rearrange("p (s j) -> p s j", j=HD),
                                SMALL3[:, 5:8].unsqueeze(1).to_broadcast([128, SB, HD]), ALU.add).then_inc(dtv_ready, 1)
                st.done(softplus(SPB, DTS, softplus_exps3, softplus_logs3))
                by_block = "p (s q) -> p s q"
                eye = IDENT[:, :].unsqueeze(1).to_broadcast([128, SB, 128])
                for j in range(HD):
                    v.tensor_tensor(SPREAD[:, j, :].rearrange(by_block, s=SB), eye,
                                    DTS[:, j * SB:(j + 1) * SB].unsqueeze(2).to_broadcast([128, SB, 128]),
                                    ALU.mult).then_inc(spread_ready, 1)
                for i in range(2):
                    dve.wait_ge(pad3_filled, b * 5 + (i + 1))
                    conv(XC[:, i, :], PAD3[:, i], CONV3[:, i, :], 3, None, conv3_done)
                for j in range(HD):
                    dve.wait_ge(row_ready, b * HD + (j + 1))
                    v.tensor_tensor_scan(CUM[:, j, :], banks(0), SPREAD[:, j, :], 0.0, ALU.add, ALU.max).then_inc(cum_ready, 1)
                    dve.wait_ge(cum_ready, b * HD + (j + 1))
                    diag = SPREAD[:, j, :].rearrange(by_block, s=SB)
                    st.done(v.tensor_tensor(diag, CUM[:, j, :].rearrange(by_block, s=SB), eye, ALU.mult))
                    st.done(v.tensor_reduce(CUMS[:, j * SB:(j + 1) * SB], diag, AX_X, ALU.add))
                stage_end(dve, b, 6)
                for s in range(SB):
                    dve.wait_ge(g_kept, b * SB + (s + 1))
                    diag = GT[:, TRI[s]:TRI[s] + 128]
                    v.tensor_tensor(diag, diag, TRIM[:, :], ALU.mult)
                stage_end(dve, b, 7)

                def differences(j):
                    for s in range(SB):
                        cum = CUMX[:, bass.ds(j, 1), 128 * s:T].rearrange("p o t -> p (o t)")
                        ins = v.tensor_scalar(DIFF[:, TRI[s]:TRI[s + 1]], cum, CUMS[:, bass.ds(j * SB + s, 1)], 0.0,
                                              ALU.subtract, ALU.max)
                    ins.then_inc(diff_ready, 1)

                differences(0)
                with dve.Fori(0, HD) as j:

                    def collect(k):
                        dve.wait_ge(y3_ready, b * 12 + j * 4 + (k + 3))
                        ya = YACC[:, bass.ds(j, 1), :].rearrange("p o t -> p (o t)")
                        xc = XC[:, bass.ds(j, 1), :].rearrange("p o t -> p (o t)")
                        y = banks(2 * (k % 2)).rearrange("p (a c) -> p a c", a=SIDE)
                        if k >= 2:
                            y = y[:, ::-1, ::-1]
                        if k == 0:
                            ins = v.scalar_tensor_tensor(grid(ya), grid(xc), DSUM[:, bass.ds(j, 1)], y, ALU.mult, ALU.add)
                        else:
                            dve.wait_ge(yacc_added, b * 12 + j * 4 + (k + 2))
                            to = (grid, turned)[k % 2](ya)
                            ins = v.tensor_tensor(to, to, y, ALU.add)
                        ins.then_inc(yacc_added, 1)

                    for k in range(ND):
                        h = b * 12 + j * 4
                        dve.wait_ge(xt_ps, h + (k + 1))
                        dve.wait_ge(y3_ready, h + (k + 1))
                        v.tensor_tensor(XT[:, k % 2, :].rearrange("p (s q) -> p s q", s=SB),
                                        banks(4 + 2 * (k % 2)).rearrange("p (s q) -> p s q", s=SB),
                                        DTS[:, bass.ds(j * SB, SB)].unsqueeze(2).to_broadcast([128, SB, 128]),
                                        ALU.mult).then_inc(xt_ready, 1)
                        dve.wait_ge(e_ready, h + (k + 1))
                        v.tensor_tensor(EE[:, k % 2, :], EE[:, k % 2, :], GT, ALU.mult).then_inc(m_ready, 1)
                        if k == ND - 1:
                            differences(j + 1)
                        if k >= 1:
                            collect(k - 1)
                    collect(ND - 1)
                stage_end(dve, b, 8)
                for i in range(DB):
                    dve.wait_ge(z_act[1], b * DB + (i + 1))
                    ins = v.tensor_tensor(YACC[:, i, :], YACC[:, i, :], Z3[:, i, :], ALU.mult)
                ins.then_inc(gated[1], 1)
                dve.wait_ge(gated[1], b * 2 + 1)
                dve.wait_ge(std_ready[2], b + 1)
                for i in range(DB):
                    ins = v.scalar_tensor_tensor(YACC[:, i, :], YACC[:, i, :], SMALL3[:, 32 + i:33 + i], R3, ALU.mult, ALU.mult)
                ins.then_inc(gated[1], 1)
                residual(3).then_inc(x_final, 1)
                stage_end(dve, b, STAGES)
                st.end()

        @block.tensor
        def _(pe):
            pe.wait_ge(weights_in, 16 * len(WEIGHTS))
            pe.wait_ge(consts_ready, 9)
            pe.drain().then_inc(decay_free, 4)
            pe.drain().then_inc(ring_free, 8)
            pe.drain().then_inc(drive_ready, 6)
            pe.drain().then_inc(ch_ready, 2)
            pe.drain().then_inc(xj_used, 1)
            pe.drain().then_inc(y3_ready, 2)
            pe.drain().then_inc(xt_ready, 2)
            pe.drain().then_inc(prod_used, 2)
            pe.drain().then_inc(y_ready, 1)
            pe.drain().then_inc(yacc_added, 2)
            with pe.Fori(0, NB) as b:
                def mm(to, w, x, start=True, stop=True):
                    return nc.tensor.matmul(to, w, x, start=start, stop=stop)

                def project(first, p, w, x, kb):
                    for h in range(2):
                        for i in range(kb):
                            ins = mm(PS[0:p, first + h, :], w(i), x(i, h), i == 0, i == kb - 1)
                    return ins

                def cols(ap, h):
                    return ap[:, h * HALF:(h + 1) * HALF]

                def group_sums(layer):
                    pe.wait_ge(gn_stats, b * 4 + (layer + 1))
                    mm(PS[0:CP, 0, 0:2 * CB], GROUP[:, :], GS[:, :, :].rearrange("p c s -> p (c s)")).then_inc(gn_sums, 1)

                def sums(first, p, of, kb):
                    return project(first, p, lambda i: ONES[0:p, 0:p], lambda i, h: cols(of(i), h), kb)

                def diagonal_conv(first, p, diag, pad, taps, k):
                    for h in range(2):
                        for i, t in enumerate(taps):
                            view = pad[:, 16 * h + t // k:16 * h + t // k + 16, t % k:t % k + SIDE]
                            ins = mm(PS[0:p, first + h, :], diag[:, i, :], view, i == 0, i == len(taps) - 1)
                    return ins

                group_sums(0)
                pe.wait_ge(xn_ready[0], b + 1)
                for d in range(DB):
                    project(2 * d, 128, lambda i: WIN[:, i, 128 * d:128 * d + 128],
                            lambda i, h: cols(XN[:, i, :], h), CB).then_inc(xval_ready, 1)
                pe.wait_ge(diags_ready[0], b + 1)
                pe.wait_ge(pad_filled, b * DB + 2)
                diagonal_conv(6, 128, DIAG0[:, 0], PADX[:, 1], range(9), 3).then_inc(pe_conv_done[0], 1)
                pe.wait_ge(u_ready, b * DB + DB)
                pe.wait_ge(step_weights_in, b * 32 + 32)
                project(6, RANK, lambda i: WX[:, i, 0:RANK], lambda i, h: cols(U[:, i, :], h), DB).then_inc(dtr_ready, 1)
                project(0, 2 * NS, lambda i: WX[:, i, RANK:RANK + 2 * NS], lambda i, h: cols(U[:, i, :], h), DB).then_inc(bc_ready, 1)
                pe.wait_ge(dtr_copied, b + 1)
                for d in range(DB):
                    ins = project(2 + 2 * d, 128, lambda i: WDT[:, 128 * d:128 * d + 128], lambda i, h: cols(DTR, h), 1)
                ins.then_inc(dtp_ready, 1)
                pe.wait_ge(bc_split, b + 1)
                stage_end(pe, b, 1)

                def row(first, r):
                    return project(first, 128, lambda i: ONEHOT[:, r, :], lambda i, h: cols(BCS, h), 1)

                row(4, 0).then_inc(b_row, 1)
                pe.wait_ge(num_ready, b * (DB * NS + 1) + 1)
                row(4, 1).then_inc(b_row, 1)
                with pe.Fori(0, DB) as d:
                    u0 = b * (DB * NS) + d * NS

                    for n in range(NS):
                        pe.wait_ge(ch_ready, u0 + (n + 1))
                        for i, k in enumerate(ORDER):
                            pe.wait_ge(h_ready, u0 * 4 + (4 * n + i + 1))
                            state = RING[:, (4 * n + k) % 8, :]
                            for h in range(2):
                                if k < 2:
                                    src = cols(state, h)
                                else:
                                    src = state.rearrange("p (w h) -> p h w", w=SIDE)[:, 16 * h:16 * h + 16, :]
                                ins = mm(PS[:, 2 * (n % 2) + h, :], IDENT[:, :], src, i == 0, i == 3)
                            ins.then_inc(ring_free, 1)
                            if i == 0:
                                pe.wait_ge(num_ready, u0 + b + (n + 2))
                                row(4, (n + 2) % NS).then_inc(b_row, 1)
                        if n >= 2 and n % 2 == 0:
                            if n == 2:
                                pe.wait_ge(skips_ready, b * DB + d + 1)
                                for h in range(2):
                                    mm(PS[:, 6 + h, :], IDENT[:, :], cols(YD, h), True, False)
                            pe.wait_ge(products_merged, (b * DB + d) * (NS // 2) + n // 2)
                            for h in range(2):
                                ins = mm(PS[:, 6 + h, :], IDENT[:, :], cols(CM, h), False, n == NS - 2)
                            ins.then_inc(ch_added, 1)
                        pe.wait_ge(ring_free, u0 * 4 + (4 * n + 12))
                        pe.sem_inc(hsum_ready, 1)
                stage_end(pe, b, 2)
                sums(0, 128, lambda i: Y0[:, i, :], DB).then_inc(mean_sum[0], 1)
                pe.wait_ge(xn_again, b + 1)
                for d in range(DB):
                    if d == 2:
                        pe.wait_ge(centered[0], b + 1)
                    project((4, 6, 0)[d], 128, lambda i: WIN[:, i, DI + 128 * d:DI + 128 * d + 128],
                            lambda i, h: cols(XN[:, i, :], h), CB).then_inc(z_ready[0], 1)
                pe.wait_ge(squares[0], b + 1)
                sums(2, 128, lambda i: SQ0[:, i * T:(i + 1) * T], DB).then_inc(square_sum[0], 1)

                def project_out(first, w, of, kb):
                    for c in range(CB):
                        ins = project(first + 2 * c, CP, lambda i: w[:, i, CP * c:CP * c + CP], lambda i, h: cols(of(i), h), kb)
                    return ins

                pe.wait_ge(gated[0], b + 1)
                pe.wait_ge(wout_in, b * 16 + 16)
                project_out(2, WOUT, lambda i: Y0[:, i, :], DB).then_inc(layer_out[0], 1)
                stage_end(pe, b, 3)
                pe.wait_ge(late_weights_in, b * (16 * len(LATE)) + 16 * len(LATE))
                group_sums(1)
                pe.wait_ge(xn_ready[1], b + 1)
                pe.wait_ge(diags_ready[1], b + 1)
                for c in range(CB):
                    ins = diagonal_conv(4 + 2 * c, CP, DIAG1[:, c], PAD1[:, c], TAPS_PE, K1)
                ins.then_inc(pe_conv_done[1], 1)
                pe.wait_ge(ln1_ready, b * 2 + 1)
                sums(0, CP, lambda i: Y1[:, i, :], CB).then_inc(mean_sum[1], 1)
                pe.wait_ge(squares[1], b + 1)
                sums(2, CP, lambda i: SQ1[:, i * T:(i + 1) * T], CB).then_inc(square_sum[1], 1)
                pe.wait_ge(ln1_ready, b * 2 + 2)
                for m in range(MB):
                    if m >= 2:
                        pe.wait_ge(gelu_done, b * MB + (m - 1))
                    project(4 + 2 * (m % 2), 128, lambda i: W0[:, i, 128 * m:128 * m + 128],
                            lambda i, h: cols(Y1[:, i, :], h), CB).then_inc(hidden_ready, 1)
                pe.wait_ge(gelu_done, b * MB + MB)
                project_out(0, W1, lambda i: G1[:, i, :], MB).then_inc(layer_out[1], 1)
                stage_end(pe, b, 4)
                group_sums(2)
                pe.wait_ge(xn_ready[2], b + 1)
                for c in range(CB):
                    for h in range(2):
                        for i in range(CB):
                            for t, (y, xx) in enumerate(TAPS2):
                                ins = mm(PS[0:CP, 2 + 2 * c + h, :], KE[:, i, t, CP * c:CP * c + CP],
                                         PAD2[:, i, 16 * h + y:16 * h + y + 16, xx:xx + SIDE],
                                         i == 0 and t == 0, i == CB - 1 and t == len(TAPS2) - 1)
                ins.then_inc(layer_out[2], 1)
                stage_end(pe, b, 5)
                group_sums(3)
                pe.wait_ge(xn_ready[3], b + 1)

                def in3(first, blk):
                    return project(first, 128, lambda i: WIN3[:, i, 128 * blk:128 * blk + 128],
                                   lambda i, h: cols(XN[:, i, :], h), CB)

                for i in range(SB):
                    for c in range(CB):
                        ins = mm(PS[:, 0, HD * i:HD * i + HD], XN[:, c, 128 * i:128 * i + 128], WDT3[:, c, :], c == 0, c == CB - 1)
                ins.then_inc(dt3_ready, 1)
                for i in range(5):
                    if i >= 3:
                        pe.wait_ge(pad3_filled, b * 5 + (i - 2))
                    in3(BANK3[i], i).then_inc(xbc_ready, 1)

                def spread_row(j):
                    pe.wait_ge(spread_ready, b * HD + (j + 1))
                    if j >= 1:
                        pe.wait_ge(cum_ready, b * HD + j)
                    sums(0, 128, lambda i: SPREAD[:, j, :], 1).then_inc(row_ready, 1)

                pe.wait_ge(diags_ready[2], b + 1)
                spread_row(0)
                pe.wait_ge(pad3_filled, b * 5 + 5)
                for i in (3, 4):
                    diagonal_conv(BANK3[i], 128, DIAG3[:, i - 3], PAD3[:, i], range(9), 3).then_inc(pe_conv_done[2], 1)
                    spread_row(i - 2)
                pe.wait_ge(xbc_act, b * 11 + 11)
                stage_end(pe, b, 6)
                for s in range(SB):
                    if s >= 4:
                        pe.wait_ge(g_kept, b * SB + (s - 3))
                    for h in range(2):
                        lo, hi = max(HALF * h, 128 * s), HALF * (h + 1)
                        if lo >= hi:
                            continue
                        for c in range(2):
                            ins = mm(PS[:, 2 * (s % 4) + h, lo - HALF * h:HALF], BCAT[:, c, 128 * s:128 * s + 128],
                                     CCAT[:, c, lo:hi], c == 0, c == 1)
                    ins.then_inc(g_ready, 1)
                stage_end(pe, b, 7)
                with pe.Fori(0, HD) as j:
                    def outputs(k):
                        h0 = b * 12 + j * 4
                        pe.wait_ge(m_ready, h0 + (k + 1))
                        pe.wait_ge(xt_ready, h0 + (k + 3))
                        pe.wait_ge(yacc_added, h0 + (k + 1))
                        for h in range(2):
                            for s in range(4 * h + 4):
                                lo = max(HALF * h, 128 * s)
                                at = TRI[s] + lo - 128 * s
                                ins = mm(PS[:, 2 * (k % 2) + h, lo - HALF * h:HALF], XT[:, k % 2, 128 * s:128 * s + 128],
                                         EE[:, k % 2, at:at + HALF * (h + 1) - lo], s == 0, s == 4 * h + 3)
                        ins.then_inc(y3_ready, 1)

                    pe.wait_ge(xj_ready, (b * HD + j) * ND + ND)
                    for k in range(ND):
                        pe.wait_ge(xt_ready, b * 12 + j * 4 + (k + 1))
                        for s in range(SB):
                            src = XJ[:, k, 128 * s:128 * s + 128]
                            ins = nc.tensor.transpose(banks(4 + 2 * (k % 2))[:, 128 * s:128 * s + 128], src, IDENT[:, :])
                        ins.then_inc(xt_ps, 1)
                        if k == ND - 1:
                            pe.wait_ge(xt_ps, b * 12 + j * 4 + 4)
                            pe.sem_inc(xj_used, 1)
                        if k >= 1:
                            outputs(k - 1)
                    outputs(ND - 1)
                stage_end(pe, b, 8)
                for d in range(DB):
                    project((4, 6, 0)[d], 128, lambda i: WZ3[:, i, 128 * d:128 * d + 128],
                            lambda i, h: cols(XN[:, i, :], h), CB).then_inc(z_ready[1], 1)
                pe.wait_ge(squares[2], b + 1)
                sums(2, 128, lambda i: SQ3[:, i * T:(i + 1) * T], DB).then_inc(square_sum[2], 1)
                pe.wait_ge(gated[1], b * 2 + 2)
                project_out(2, WOUT3, lambda i: YACC[:, i, :], DB).then_inc(layer_out[3], 1)
                stage_end(pe, b, STAGES)


def kernel(**inputs):
    import ml_dtypes
    import numpy as np
    import concourse.bacc as bacc
    from concourse import mybir as mb
    from concourse.bass_utils import run_bass_kernel_spmd as run

    a = {k: np.asarray(v) for k, v in inputs.items()}

    def cols(v, p):
        return np.ascontiguousarray(v.reshape(-1, p).T)

    def rows(w, p):
        return w.reshape(-1, p, w.shape[1]).transpose(1, 0, 2)

    def on_all(v):
        return np.broadcast_to(v.reshape(1, -1), (128, v.size))

    h = {}
    h["x"] = a["x"].reshape(NB, T, CB, CP).transpose(0, 3, 2, 1)
    h["win"] = rows(a["L0_conv_W_in"], CP)
    h["conv0"] = rows(a["L0_conv_conv_w"].reshape(DI, 9), 128)
    h["small0"] = np.stack([cols(a["L0_conv_" + n], 128) for n in ("conv_b", "b_dt", "D_param", "gamma", "beta")], 1)
    h["alog0"] = rows(a["L0_conv_A_log"], 128).reshape(128, DB * NS)
    h["wx"] = rows(a["L0_conv_W_x"], 128)
    h["wdt"] = a["L0_conv_W_dt"]
    h["wout"] = rows(a["L0_conv_W_out"], 128)
    h["dw1"] = rows(a["L1_conv_dw_kernel"].reshape(K1 * K1, C).T, CP)
    h["small1"] = np.stack([cols(a["L1_conv_" + n], CP) for n in ("dw_bias", "ln_gamma", "ln_beta", "b1", "gamma")], 1)
    h["w0"] = rows(a["L1_conv_w0"], CP)
    h["b0"] = cols(a["L1_conv_b0"], 128)
    h["w1"] = rows(a["L1_conv_w1"], 128)
    k2 = a["L2_conv_kernel"]
    grp = 12
    near = np.array([[2, 1], [1, 2], [0, 2], [0, 1], [1, 0], [2, 0]])
    k6, s6 = np.arange(grp) % 6, np.arange(grp) // 6
    sign = np.where(s6 == 0, 1, -1)
    act = (k6[:, None] + sign[:, None] * np.arange(6)[None, :]) % 6
    mult = (k6[:, None] + sign[:, None] * k6[None, :]) % 6 + 6 * (s6[:, None] ^ s6[None, :])
    py, px = np.ones((grp, 7), int), np.ones((grp, 7), int)
    py[:, 1:], px[:, 1:] = near[act][:, :, 0], near[act][:, :, 1]
    gg, tt, hh = np.meshgrid(np.arange(grp), np.arange(7), np.arange(grp), indexing="ij")
    full = np.zeros((3, 3, grp, 16, grp, 16), k2.dtype)
    full[py[gg, tt], px[gg, tt], mult[gg, hh], :, gg, :] = k2[tt, hh]
    full = full.reshape(3, 3, C, C)
    h["ke"] = np.stack([full[y, x].reshape(CB, CP, C) for y, x in TAPS2], 0).transpose(2, 1, 0, 3)
    w3 = a["L3_conv_in_proj_w"].T
    xs, bs, cs, dts = w3[:, DI:2 * DI], w3[:, 2 * DI:2 * DI + 64], w3[:, 2 * DI + 64:2 * DI + 128], w3[:, 2 * DI + 128:]
    h["win3"] = rows(np.concatenate([xs, bs, bs, cs, cs], 1), CP)
    h["wdt3"] = rows(dts, CP)
    h["wz3"] = rows(w3[:, :DI], CP)

    def doubled(v):
        return np.concatenate([v[:DI], v[DI:DI + 64], v[DI:DI + 64], v[DI + 64:], v[DI + 64:]], 0)

    h["conv3"] = rows(doubled(a["L3_conv_conv_w"].reshape(DI + 128, 9)), 128)
    h["small3"] = np.concatenate([cols(doubled(a["L3_conv_conv_b"]), 128), on_all(a["L3_conv_dt_bias"]), on_all(a["L3_conv_A_log"]),
                                  on_all(a["L3_conv_Ds"]), cols(a["L3_conv_norm_w"], 128)], 1)
    h["wout3"] = rows(a["L3_conv_out_proj_w"].T, 128)
    h["ident"] = np.eye(128, dtype=np.float32)
    h["group"] = (np.kron(np.eye(CP // 6), np.ones((6, 6))) / 6).astype(np.float32)
    h["tri"] = np.triu(np.ones((128, 128), np.float32))
    pick = np.tile(np.eye(2 * NS, NS, dtype=np.float32), (3, 1))
    h["onehot"] = np.repeat(pick[:, :, None], 128, 2).astype(ml_dtypes.bfloat16)

    nc = bacc.Bacc("TRN2", target_bir_lowering=False, num_devices=1)
    arrays, args = {}, []
    for name in ("x", "win", "conv0", "small0", "alog0", "wx", "wdt", "wout", "dw1", "small1", "w0", "b0", "w1", "ke",
                 "win3", "conv3", "small3", "wz3", "wout3", "wdt3", "ident", "group", "tri", "onehot"):
        v = np.ascontiguousarray(h[name])
        arrays[f"in_{name}"] = v
        args.append(nc.dram_tensor(f"in_{name}", v.shape, mb.dt.from_np(v.dtype), kind="ExternalInput").ap())
    args.append(nc.dram_tensor("out_x", (NB, CP, CB, T), F32, kind="ExternalOutput").ap())
    args.append(nc.dram_tensor("c_rows", (NS, T), F32, kind="Internal").ap())
    build(nc, *args)
    r = run(nc, [arrays], core_ids=[0])
    got = r.results[0]["out_x"]
    return got.transpose(0, 3, 2, 1).reshape(NB, SIDE, SIDE, C)
```

```python
from contextlib import ExitStack

import concourse.bass as bass
from concourse import mybir

F32 = mybir.dt.float32
BF16 = mybir.dt.bfloat16
U32 = mybir.dt.uint32
ALU = mybir.AluOpType
ACT = mybir.ActivationFunctionType
AX_X = mybir.AxisListType.X

NB, SIDE, C = 4, 32, 192
T = SIDE * SIDE
HALF = 512
CP = 96
CB = C // CP
DI, DB = 384, 3
NS = 16
RANK = 12
MLP, MB = 768, 6
K1 = 7
P3, P7 = SIDE + 2, SIDE + K1 - 1
HD, ND = 3, 4
SB = T // 128
BANK3 = (2, 4, 6, 2, 4)
GUARD = 27.631021115928547
TAPS2 = [(y, x) for y in range(3) for x in range(3) if (y, x) not in ((0, 0), (2, 2))]
TRI = [sum(T - 128 * i for i in range(s)) for s in range(SB + 1)]
ORDER = (0, 1, 3, 2)
TAPS_DVE, TAPS_PE, TAPS_POOL = range(21), range(21, 37), range(37, 49)
SHARE = 4
DRIVES = 3 * NS + NS // SHARE
TAPS3_DVE, TAPS3_PE = range(4), range(4, 9)
TAPS0_DVE, TAPS0_POOL = range(4), range(4, 9)
FIRST = len(TAPS0_POOL) - 1
PRODUCTS = FIRST + 2 * (len(TAPS_POOL) - 1) + 8


def drives(n):
    return 3 * n + (n + SHARE - 1) // SHARE


class Steps:

    def __init__(self, eng, sem, per_image, image):
        self.eng, self.sem, self.per, self.image, self.n = eng, sem, per_image, image, 0

    def done(self, ins):
        ins.then_inc(self.sem, 1)
        self.n += 1
        self.eng.wait_ge(self.sem, self.image * self.per + self.n)

    def end(self):
        assert self.n == self.per, (self.sem, self.n)


ACT_STEPS, DVE_STEPS, STAGES = 7, 130, 9


def build(nc, x, win, conv0, small0, alog0, wx, wdt, wout, dw1, small1, w0, b0, w1, ke,
          win3, conv3, small3, wz3, wout3, wdt3, ident, group, tri, onehot, out, c_rows):
    with ExitStack() as ctx:
        def sb(name, shape, dt=F32):
            return ctx.enter_context(nc.sbuf_tensor(name, shape, dt))

        def sem(name):
            return ctx.enter_context(nc.semaphore(name))

        WIN = sb("WIN", [CP, CB, 2 * DI])
        CONV0 = sb("CONV0", [128, DB, 9])
        SMALL0 = sb("SMALL0", [128, 5, DB])
        D4 = sb("D4", [128, DB])
        A0 = sb("A0", [128, DB * NS])
        IDENT = sb("IDENT", [128, 128])
        GROUP = sb("GROUP", [CP, CP])
        TRIM = sb("TRIM", [128, 128])
        ONES = sb("ONES", [128, 128])
        ONEHOT = sb("ONEHOT", [3 * 2 * NS, NS, 128], BF16)
        GCOL = sb("GCOL", [128, 1])
        MHALF = sb("MHALF", [128, 1])
        EPS5 = sb("EPS5", [128, 1])
        EPS6 = sb("EPS6", [128, 1])
        SMALL3 = sb("SMALL3", [128, 5 + HD + 12 + 12 + DB])
        CONV3 = sb("CONV3", [128, 5, 9])
        A3 = sb("A3", [128, 12])
        DSUM = sb("DSUM", [128, HD])
        SMALL1 = sb("SMALL1", [CP, 5, CB])
        DW1 = sb("DW1", [CP, CB, K1 * K1])
        B0 = sb("B0", [128, MB])
        STREAM = sb("STREAM", [128, 4 * T])
        X = STREAM[0:CP, 0:2 * T].rearrange("p (c t) -> p c t", c=CB)
        XN = STREAM[0:CP, 2 * T:4 * T].rearrange("p (c t) -> p c t", c=CB)
        WEIGHT = STREAM[:, :].rearrange("p (s k t) -> p s k t", s=2, k=2)
        ST = sb("ST", [CP, CB, 2, 6])
        MV = sb("MV", [CP, CB, 2])
        GS = sb("GS", [CP, CB, 2])
        GM = sb("GM", [CP, CB, 2])
        GV = sb("GV", [CP, CB, 2])
        ARENA = sb("ARENA", [128, 45568])

        def area(at, n, p=128):
            return ARENA[0:p, at:at + n]

        DTU = area(0, 3 * T).rearrange("p (d t) -> p d t", d=DB)
        DTUX = area(0, 4 * T).rearrange("p (d t) -> p d t", d=DB + 1)
        U = area(3072, 3 * T).rearrange("p (d t) -> p d t", d=DB)
        DT = area(6144, 3 * T).rearrange("p (d t) -> p d t", d=DB)
        S = area(9216, 12 * T).rearrange("p (d k t) -> p d k t", d=DB, k=4)
        DEC = area(21504, 8 * T).rearrange("p (s o t) -> p s o t", s=4, o=2)
        RING = area(29696, 8 * T).rearrange("p (s t) -> p s t", s=8)
        NUM = area(37888, 2 * T).rearrange("p (s t) -> p s t", s=2)
        CM = area(39936, T)
        CS = (area(40960, T), area(44544, T))
        BCS = area(41984, T // 2, 96).bitcast(BF16)
        CM2 = area(42496, T)
        YD = area(43520, T)
        WDT = area(43520, DI, RANK)
        WX = area(43904, DB * (RANK + 2 * NS)).rearrange("p (d n) -> p d n", d=DB)
        WOUT = area(42512, DB * C).rearrange("p (d n) -> p d n", d=DB)
        DIAG0 = area(12800, 9 * 128).rearrange("p (d k q) -> p d k q", d=1, k=9)
        PROD0 = area(15104, 2 * T).rearrange("p (s t) -> p s t", s=2)
        PADX = area(9216, DB * P3 * P3).rearrange("p (d h w) -> p d h w", d=DB, h=P3)
        SPA = [area(21504 + i * 3072, 3072) for i in range(5)]
        V2 = area(42496, T)
        DTR = area(37888, T, RANK)
        BCF = area(38912, T, 2 * NS)
        BCH = area(39936, T // 2, 2 * NS).bitcast(BF16)
        Y0 = DTU
        SQ0 = area(9216, 3 * T).rearrange("p (d t) -> p d t", d=DB)
        Z0 = area(12288, 3 * T).rearrange("p (d t) -> p d t", d=DB)
        R0 = area(23360, T)
        W0 = area(33400, CB * MLP, CP).rearrange("p (c n) -> p c n", c=CB)
        W1 = area(34936, MB * C).rearrange("p (m n) -> p m n", m=MB)
        KE = area(36088, CB * 7 * C, CP).rearrange("p (c k n) -> p c k n", c=CB, k=7)
        WIN3 = area(38776, CB * 640, CP).rearrange("p (c n) -> p c n", c=CB)
        WZ3 = area(40824, CB * DI, CP).rearrange("p (c n) -> p c n", c=CB)
        WDT3 = area(42504, CB * HD, CP).rearrange("p (c n) -> p c n", c=CB)
        WOUT3 = area(41592, DB * C).rearrange("p (d n) -> p d n", d=DB)
        PAD1 = area(0, CB * P7 * P7, CP).rearrange("p (c h w) -> p c h w", c=CB, h=P7)
        Y1 = area(2888, CB * T, CP).rearrange("p (c t) -> p c t", c=CB)
        SQ1 = area(4936, CB * T, CP).rearrange("p (c t) -> p c t", c=CB)
        R1 = area(6984, T, CP)
        G1 = area(8008, MB * T).rearrange("p (m t) -> p m t", m=MB)
        O1 = area(4936, CB * T, CP).rearrange("p (c t) -> p c t", c=CB)
        PROD1 = area(19264, 2 * T, CP).rearrange("p (s t) -> p s t", s=2)
        YP1 = area(21312, CB * T, CP).rearrange("p (c t) -> p c t", c=CB)
        DIAG1 = area(16192, CB * len(TAPS_PE) * CP, CP).rearrange("p (c k q) -> p c k q", c=CB, q=CP)
        PAD2 = area(0, CB * P3 * P3, CP).rearrange("p (c h w) -> p c h w", c=CB, h=P3)
        XC = area(0, 3 * T).rearrange("p (d t) -> p d t", d=DB)
        BCAT = area(3072, 2 * T).rearrange("p (c t) -> p c t", c=2)
        CCAT = area(5120, 2 * T).rearrange("p (c t) -> p c t", c=2)
        GT = area(7168, TRI[SB])
        DIFF = area(11776, TRI[SB])
        EE = area(16384, 2 * TRI[SB]).rearrange("p (s n) -> p s n", s=2)
        XT = area(25600, 2 * T).rearrange("p (s t) -> p s t", s=2)
        YACC = area(27648, 3 * T).rearrange("p (d t) -> p d t", d=DB)
        XJ = area(30720, ND * T).rearrange("p (k t) -> p k t", k=ND)
        DTS = area(34816, HD * SB)
        CUMS = area(34840, (HD + 1) * SB)
        CUM = area(34864, 3 * T).rearrange("p (d t) -> p d t", d=DB)
        CUMX = area(34864, 4 * T).rearrange("p (d t) -> p d t", d=DB + 1)
        PAD3 = area(16384, 5 * P3 * P3).rearrange("p (d h w) -> p d h w", d=5, h=P3)
        DIAG3 = area(10240, 2 * 9 * 128).rearrange("p (d k q) -> p d k q", d=2, k=9)
        PROD3 = area(13696, 2 * T).rearrange("p (s t) -> p s t", s=2)
        SPREAD = area(7168, 3 * T).rearrange("p (j t) -> p j t", j=HD)
        SPB = [area(22200 + 32 * i, HD * SB) for i in range(6)]
        C3 = area(22528, T)
        SQ3 = area(16384, 3 * T)
        Z3 = area(19456, 3 * T).rearrange("p (d t) -> p d t", d=DB)
        R3 = area(22528, T)
        O3 = area(23552, CB * T, CP).rearrange("p (c t) -> p c t", c=CB)

        PS = ctx.enter_context(nc.psum_tensor("PS", [128, 8, HALF], F32))

        def banks(first, n=2, p=128):
            return PS[0:p, first:first + n, :].rearrange("p a n -> p (a n)")

        def inner(pad, k, size=P3):
            o = k // 2
            return pad[:, o:o + SIDE, o:o + SIDE]

        def half(ap, h):
            return ap[:, :, h * HALF:(h + 1) * HALF]

        def grid(ap):
            return ap.rearrange("p (h w) -> p h w", h=SIDE)

        def turned(ap):
            return ap.rearrange("p (h w) -> p w h", h=SIDE)

        def sequence(ap, k):
            v = (grid, turned)[k % 2](ap)
            return v[:, ::-1, ::-1] if k >= 2 else v

        weights_in = sem("weights_in")
        x_in = sem("x_in")
        step_weights_in = sem("step_weights_in")
        wout_in = sem("wout_in")
        late_weights_in = sem("late_weights_in")
        out_written = sem("out_written")
        consts_ready = sem("consts_ready")
        a_exp_done = sem("a_exp_done")
        stage_done = sem("stage_done")
        settled = sem("settled")
        act_steps = sem("act_steps")
        dve_steps = sem("dve_steps")
        gn_stats = sem("gn_stats")
        gn_sums = sem("gn_sums")
        gn_var = sem("gn_var")
        gn_std = sem("gn_std")
        std_ready = [sem(f"std_ready{i}") for i in range(3)]
        xn_ready = [sem(f"xn_ready{i}") for i in range(4)]
        xn_again = sem("xn_again")
        pads_clear = sem("pads_clear")
        xval_ready = sem("xval_ready")
        pad_filled = sem("pad_filled")
        conv_done = sem("conv_done")
        u_ready = sem("u_ready")
        dtr_ready = sem("dtr_ready")
        bc_ready = sem("bc_ready")
        dtr_copied = sem("dtr_copied")
        bc_split = sem("bc_split")
        dtp_ready = sem("dtp_ready")
        softplus_exps = sem("softplus_exps")
        softplus_logs = sem("softplus_logs")
        softplus_exps3 = sem("softplus_exps3")
        dt_ready = sem("dt_ready")
        dt_turned = sem("dt_turned")
        s_ready = sem("s_ready")
        decay_ready = sem("decay_ready")
        decay_free = sem("decay_free")
        weight_ready = sem("weight_ready")
        ring_free = sem("ring_free")
        b_row = sem("b_row")
        num_ready = sem("num_ready")
        drive_ready = sem("drive_ready")
        drive3_ready = sem("drive3_ready")
        h_ready = sem("h_ready")
        hsum_ready = sem("hsum_ready")
        c_row = [sem(f"c_row{i}") for i in range(2)]
        bc_kept = sem("bc_kept")
        c_stored = sem("c_stored")
        ch_ready = sem("ch_ready")
        skips_ready = sem("skips_ready")
        ch_added = sem("ch_added")
        y_ready = sem("y_ready")
        mean_sum = [sem(f"mean_sum{i}") for i in range(2)]
        centered = [sem(f"centered{i}") for i in range(2)]
        squares = [sem(f"squares{i}") for i in range(3)]
        square_sum = [sem(f"square_sum{i}") for i in range(3)]
        z_ready = [sem(f"z_ready{i}") for i in range(2)]
        z_act = [sem(f"z_act{i}") for i in range(2)]
        gated = [sem(f"gated{i}") for i in range(2)]
        layer_out = [sem(f"layer_out{i}") for i in range(4)]
        ln1_ready = sem("ln1_ready")
        hidden_ready = sem("hidden_ready")
        gelu_done = sem("gelu_done")
        dt3_ready = sem("dt3_ready")
        xbc_ready = sem("xbc_ready")
        softplus_logs3 = sem("softplus_logs3")
        pad3_filled = sem("pad3_filled")
        conv3_done = sem("conv3_done")
        prod_first = sem("prod_first")
        prod_ready = sem("prod_ready")
        prod_used = sem("prod_used")
        pool_conv_done = [sem(f"pool_conv_done{i}") for i in range(3)]
        products_merged = sem("products_merged")
        diags_ready = [sem(f"diags_ready{i}") for i in range(3)]
        pe_conv_done = [sem(f"pe_conv_done{i}") for i in range(3)]
        spread_ready = sem("spread_ready")
        row_ready = sem("row_ready")
        cum_ready = sem("cum_ready")
        dtv_ready = sem("dtv_ready")
        xbc_act = sem("xbc_act")
        c3_ready = sem("c3_ready")
        g_ready = sem("g_ready")
        g_kept = sem("g_kept")
        diff_ready = sem("diff_ready")
        xj_ready = sem("xj_ready")
        xj_used = sem("xj_used")
        xt_ps = sem("xt_ps")
        xt_ready = sem("xt_ready")
        e_ready = sem("e_ready")
        m_ready = sem("m_ready")
        y3_ready = sem("y3_ready")
        yacc_added = sem("yacc_added")
        x_final = sem("x_final")

        WEIGHTS = [(WIN, win), (CONV0, conv0), (SMALL0, small0), (A0, alog0), 
                   (IDENT, ident), (GROUP, group), (TRIM, tri), (ONEHOT, onehot), (SMALL3, small3), (CONV3, conv3),
                   (SMALL1, small1), (DW1, dw1), (B0, b0)]
        LATE = [(W0, w0), (W1, w1), (KE, ke), (WIN3, win3), (WZ3, wz3), (WOUT3, wout3), (WDT3, wdt3)]

        def whole(ap):
            return ap[tuple(slice(None) for _ in ap.shape)]

        def settle(eng):
            eng.sem_inc(settled, 1)

        def stage_end(eng, b, n):
            settle(eng)
            eng.drain().then_inc(stage_done, 1)
            eng.wait_ge(stage_done, b * (5 * STAGES) + 5 * n)
            settle(eng)

        block = ctx.enter_context(nc.Block())

        @block.sync
        def _(sp):
            for to, of in WEIGHTS:
                sp.dma_start(whole(to), whole(of)).then_inc(weights_in, 16)
            with sp.Fori(0, NB) as b:
                sp.dma_start(X[:, :, :], x[bass.ds(b, 1)].rearrange("o p c t -> (o p) c t")).then_inc(x_in, 16)
                sp.dma_start(WX, whole(wx)).then_inc(step_weights_in, 16)
                sp.dma_start(WDT, whole(wdt)).then_inc(step_weights_in, 16)
                sp.wait_ge(bc_kept, b + 1)
                settle(sp)
                sp.dma_start(c_rows[:, :], BCF[NS:2 * NS, :]).then_inc(c_stored, 16)
                sp.wait_ge(c_stored, b * 16 + 16)
                settle(sp)
                stage_end(sp, b, 1)
                with sp.Fori(0, DB) as d:
                    for n in range(NS):
                        sp.wait_ge(ch_ready, b * (DB * NS) + d * NS + (n + 1))
                        settle(sp)
                        sp.dma_start(CS[n % 2], c_rows[n:n + 1, :].to_broadcast([128, T])).then_inc(c_row[n % 2], 16)
                stage_end(sp, b, 2)
                sp.dma_start(X[:, :, :], x[bass.ds(b, 1)].rearrange("o p c t -> (o p) c t")).then_inc(x_in, 16)
                sp.dma_start(WOUT, whole(wout)).then_inc(wout_in, 16)
                for to, of in LATE:
                    sp.dma_start(to, whole(of)).then_inc(late_weights_in, 16)
                for n in range(3, STAGES):
                    stage_end(sp, b, n)
                sp.wait_ge(x_final, b * CB + CB)
                sp.dma_start(out[bass.ds(b, 1)].rearrange("o p c t -> (o p) c t"), X[:, :, :]).then_inc(out_written, 16)
                sp.wait_ge(out_written, b * 16 + 16)
                settle(sp)
                stage_end(sp, b, STAGES)

        @block.gpsimd
        def _(pool):
            nc.gpsimd.memset(ONES[:, :], 1.0).then_inc(consts_ready, 1)
            nc.gpsimd.memset(GCOL[:, :], GUARD).then_inc(consts_ready, 1)
            nc.gpsimd.memset(MHALF[:, :], -0.5).then_inc(consts_ready, 1)
            nc.gpsimd.memset(EPS5[:, :], 1e-5).then_inc(consts_ready, 1)
            nc.gpsimd.memset(EPS6[:, :], 1e-6).then_inc(consts_ready, 1)

            def diagonals(to, w, blocks, taps, p):
                for d in range(blocks):
                    for i, t in enumerate(taps):
                        ins = nc.gpsimd.tensor_scalar(to[:, d, i, :], IDENT[0:p, 0:p], w(d, t), None, ALU.mult)
                return ins

            pool.wait_ge(weights_in, 16 * len(WEIGHTS))
            with pool.Fori(0, NB) as b:
                nc.gpsimd.memset(PADX[:, :, :, :], 0.0).then_inc(pads_clear, 1)
                diagonals(DIAG0, lambda d, t: CONV0[:, 1, t:t + 1], 1, range(9), 128).then_inc(diags_ready[0], 1)

                def add_products(to, slots, first, base, n, done):
                    pool.wait_ge(prod_first, b * 4 + first)
                    for i in range(base, base + n):
                        pool.wait_ge(prod_ready, b * PRODUCTS + (i + 1))
                        if i > base:
                            pool.wait_ge(prod_used, b * PRODUCTS + (i + 2))
                        nc.gpsimd.tensor_tensor(to, to, slots[:, i % 2, :], ALU.add).then_inc(prod_used, 1)
                    pool.wait_ge(prod_used, b * PRODUCTS + (base + n + 2))
                    pool.sem_inc(done, 1)

                add_products(U[:, 2, :], PROD0, 1, 0, FIRST, pool_conv_done[0])
                pool.wait_ge(dt_ready, b + 1)
                pool.wait_ge(u_ready, b * DB + DB)
                nc.gpsimd.tensor_tensor(DTU.rearrange("p d t -> p (d t)"), DT.rearrange("p d t -> p (d t)"),
                                        U.rearrange("p d t -> p (d t)"), ALU.mult)
                stage_end(pool, b, 1)
                with pool.Fori(0, DB) as d:
                    u0 = b * (DB * NS) + d * NS
                    for n in range(NS):
                        for k in (ORDER if n % SHARE == 0 else range(3)):
                            if k == 0:
                                pool.wait_ge(num_ready, u0 + b + (n + 1))
                                pool.wait_ge(weight_ready, u0 * 2 + (2 * n + 1))
                            if k == (3 if n % SHARE == 0 else 2):
                                pool.wait_ge(weight_ready, u0 * 2 + (2 * n + 2))
                            slot, num = RING[:, (4 * n + k) % 8, :], NUM[:, n % 2, :]
                            if k < 2:
                                pool.wait_ge(ring_free, u0 * 4 + (4 * n + ORDER.index(k) + 1))
                                ins = nc.gpsimd.tensor_tensor(slot, WEIGHT[:, n % 2, k, :], num, ALU.mult)
                            else:
                                ins = nc.gpsimd.tensor_tensor(grid(slot), grid(slot), turned(num), ALU.mult)
                            ins.then_inc(drive_ready, 1)
                stage_end(pool, b, 2)
                diagonals(DIAG1, lambda d, t: DW1[:, d, t:t + 1], CB, TAPS_PE, CP).then_inc(diags_ready[1], 1)
                stage_end(pool, b, 3)
                nc.gpsimd.memset(PAD1[:, :, :, :], 0.0).then_inc(pads_clear, 1)
                for c in range(CB):
                    m = len(TAPS_POOL) - 1
                    add_products(YP1[:, c, :], PROD1, 2 + c, FIRST + m * c, m, pool_conv_done[1])
                stage_end(pool, b, 4)
                nc.gpsimd.memset(PAD2[:, :, :, :], 0.0).then_inc(pads_clear, 1)
                diagonals(DIAG3, lambda d, t: CONV3[:, d + 3, t:t + 1], 2, range(9), 128).then_inc(diags_ready[2], 1)
                nc.gpsimd.memset(PAD3[:, :, :, :], 0.0).then_inc(pads_clear, 1)
                stage_end(pool, b, 5)
                add_products(XC[:, 2, :], PROD3, 4, PRODUCTS - 8, 8, pool_conv_done[2])
                stage_end(pool, b, 6)
                stage_end(pool, b, 7)
                with pool.Fori(0, HD) as j:
                    pool.wait_ge(xj_used, b * HD + j + 1)
                    settle(pool)
                    xc = XC[:, bass.ds(j, 1), :].rearrange("p o t -> p (o t)")
                    nc.gpsimd.tensor_copy(XJ[:, 0, :], xc).then_inc(xj_ready, 1)
                    pool.wait_ge(xj_ready, (b * HD + j) * ND + 1)
                    settle(pool)
                    for k in range(1, ND):
                        nc.gpsimd.tensor_copy(XJ[:, k, :].rearrange("p (a c) -> p a c", a=SIDE),
                                              sequence(XJ[:, 0, :], k)).then_inc(xj_ready, 1)
                stage_end(pool, b, 8)
                stage_end(pool, b, STAGES)

        @block.scalar
        def _(act):
            act.wait_ge(weights_in, 16 * len(WEIGHTS))
            act.wait_ge(consts_ready, 5)
            nc.scalar.activation(A0[:, :], A0[:, :], ACT.Exp).then_inc(a_exp_done, 1)
            nc.scalar.activation(A3[:, :], SMALL3[:, 8:20], ACT.Exp).then_inc(a_exp_done, 1)
            with act.Fori(0, NB) as b:
                st = Steps(act, act_steps, ACT_STEPS, b)

                def softplus(values, biases, scratch, exps_done, done):
                    t1, t2, t3, t4 = scratch[:4]
                    n = values[0].shape[-1]

                    def each(to, func):
                        for i, value in enumerate(values):
                            bias = {} if biases is None else {"bias": biases[:, i:i + 1]}
                            ins = nc.scalar.activation(to[:, i * n:(i + 1) * n], value, func, **bias)
                        return ins

                    st.done(each(t1, ACT.Abs))
                    st.done(nc.scalar.activation(t1, t1, ACT.Exp, scale=-1.0))
                    nc.scalar.activation(t4, t1, ACT.Identity, bias=MHALF[:, 0:1], scale=1.0 / 3.0).then_inc(exps_done, 1)
                    each(t3, ACT.Relu)
                    nc.scalar.activation(t2, t1, ACT.Ln, bias=1.0).then_inc(done, 1)

                def group_std(layer):
                    act.wait_ge(gn_var, b * 4 + (layer + 1))
                    nc.scalar.activation(GV[:, :, 0], GV[:, :, 0], ACT.Sqrt, bias=EPS5[0:CP, 0:1]).then_inc(gn_std, 1)

                def layer_std(i, to, first, n, eps):
                    p = to.shape[0]
                    for h in range(2):
                        act.wait_ge(square_sum[i], b * 2 + (h + 1))
                        ins = nc.scalar.activation(to[:, h * HALF:(h + 1) * HALF], PS[0:p, first + h, :], ACT.Ln,
                                                   bias=eps, scale=1.0 / n)
                    st.done(ins)
                    for h in range(2):
                        th = to[:, h * HALF:(h + 1) * HALF]
                        nc.scalar.activation(th, th, ACT.Exp, scale=-0.5).then_inc(std_ready[i], 1)

                def square(i, to, of):
                    for h in range(2):
                        act.wait_ge(centered[i], b * 2 + (h + 1))
                        nc.scalar.activation(half(to, h), half(of, h), ACT.Square).then_inc(squares[i], 1)

                def products(to, slots, pad, w, taps, k, base):
                    for i, t in enumerate(taps):
                        view = pad[:, t // k:t // k + SIDE, t % k:t % k + SIDE]
                        if i == 0:
                            nc.scalar.activation(grid(to), view, ACT.Copy, scale=w[:, t:t + 1]).then_inc(prod_first, 1)
                            continue
                        n = base + i - 1
                        act.wait_ge(prod_used, b * PRODUCTS + (n + 1))
                        nc.scalar.activation(grid(slots[:, n % 2, :]), view, ACT.Copy, scale=w[:, t:t + 1]).then_inc(prod_ready, 1)

                group_std(0)
                for i in range(DB):
                    act.wait_ge(xval_ready, b * DB + (i + 1))
                    if i == 0:
                        act.wait_ge(pads_clear, b * 4 + 1)
                    nc.scalar.activation(inner(PADX[:, i], 3), grid(banks(2 * i)), ACT.Copy).then_inc(pad_filled, 1)
                act.wait_ge(pad_filled, b * DB + DB)
                products(U[:, 2, :], PROD0, PADX[:, 2], CONV0[:, 2, :], TAPS0_POOL, 3, 0)
                for i in range(DB):
                    act.wait_ge((conv_done, pe_conv_done[0], conv_done)[i], (b * 2 + 1, b + 1, b * 2 + 2)[i])
                    src = banks(6) if i == 1 else U[:, i, :]
                    nc.scalar.activation(U[:, i, :], src, ACT.Silu, bias=SMALL0[:, 0, i:i + 1]).then_inc(u_ready, 1)
                act.wait_ge(dtr_ready, b + 1)
                nc.scalar.activation(DTR, banks(6, 2, RANK), ACT.Copy).then_inc(dtr_copied, 1)
                act.wait_ge(dtp_ready, b + 1)
                softplus([banks(2), banks(4), banks(6)], SMALL0[:, 1, :], SPA, softplus_exps, softplus_logs)
                act.wait_ge(dt_ready, b + 1)
                for i in range(DB):
                    nc.scalar.activation(SPA[0][:, i * T:(i + 1) * T].rearrange("p (w h) -> p w h", w=SIDE),
                                         turned(DT[:, i, :]), ACT.Copy).then_inc(dt_turned, 1)
                stage_end(act, b, 1)
                with act.Fori(0, DB) as d:
                    u0 = b * (DB * NS) + d * NS
                    dt = DT[:, bass.ds(d, 1), :].rearrange("p o t -> p (o t)")

                    for n in range(NS):
                        if n % 2 == 0:
                            for m in (n, n + 1):
                                a = A0[:, bass.ds(d * NS + m, 1)]
                                act.wait_ge(decay_free, u0 + (m + 1))
                                settle(act)
                                nc.scalar.activation(DEC[:, m % 4, 0, :], dt, ACT.Exp, scale=a)
                                nc.scalar.activation(DEC[:, m % 4, 1, :].rearrange("p (w h) -> p w h", w=SIDE),
                                                     turned(dt), ACT.Exp, scale=a).then_inc(decay_ready, 1)
                        for k in (0, 2):
                            s = S[:, bass.ds(d, 1), k:k + 2, :].rearrange("p o k t -> p (o k t)")
                            if k == 0:
                                act.wait_ge(drive_ready, (b * DB + d) * DRIVES + (drives(n - 2) + 8))
                                to = WEIGHT[:, n % 2, :, :]
                            else:
                                act.wait_ge(ring_free, u0 * 4 + (4 * n + 4))
                                to = RING[:, (4 * n + 2) % 8:(4 * n + 2) % 8 + 2, :]
                            settle(act)
                            nc.scalar.activation(to.rearrange("p k t -> p (k t)"), s, ACT.Sigmoid,
                                                 bias=GCOL[:, 0:1], scale=A0[:, bass.ds(d * NS + n, 1)]).then_inc(weight_ready, 1)
                        if n == 4:
                            act.wait_ge(y_ready, b * DB + d + 1)
                            settle(act)
                            ud = U[:, bass.ds(d, 1), :].rearrange("p o t -> p (o t)")
                            nc.scalar.activation(YD, ud, ACT.Copy, scale=D4[:, bass.ds(d, 1)]).then_inc(skips_ready, 1)
                stage_end(act, b, 2)
                square(0, SQ0, Y0)
                layer_std(0, R0, 2, DI, EPS5[:, 0:1])
                for i in range(DB):
                    act.wait_ge(z_ready[0], b * DB + (i + 1))
                    nc.scalar.activation(Z0[:, i, :], banks((4, 6, 0)[i]), ACT.Silu).then_inc(z_act[0], 1)
                stage_end(act, b, 3)
                group_std(1)
                act.wait_ge(xn_ready[1], b + 1)
                for c in range(CB):
                    products(YP1[:, c, :], PROD1, PAD1[:, c], DW1[:, c, :], TAPS_POOL, K1, FIRST + (len(TAPS_POOL) - 1) * c)
                square(1, SQ1, Y1)
                layer_std(1, R1, 2, C, EPS6[0:CP, 0:1])
                for m in range(MB):
                    act.wait_ge(hidden_ready, b * MB + (m + 1))
                    nc.scalar.activation(G1[:, m, :], banks(4 + 2 * (m % 2)), ACT.Gelu, bias=B0[:, m:m + 1]).then_inc(gelu_done, 1)
                stage_end(act, b, 4)
                group_std(2)
                stage_end(act, b, 5)
                group_std(3)
                act.wait_ge(dtv_ready, b + 1)
                softplus([SPB[5]], None, SPB, softplus_exps3, softplus_logs3)
                act.wait_ge(pads_clear, b * 4 + 4)
                for i in range(5):
                    act.wait_ge(xbc_ready, b * 5 + (i + 1))
                    nc.scalar.activation(inner(PAD3[:, i], 3), grid(banks(BANK3[i])), ACT.Copy).then_inc(pad3_filled, 1)
                act.wait_ge(pad3_filled, b * 5 + 5)
                products(XC[:, 2, :], PROD3, PAD3[:, 2], CONV3[:, 2, :], range(9), 3, PRODUCTS - 8)
                for i in range(3):
                    act.wait_ge((conv3_done, conv3_done, pool_conv_done[2])[i], (b * 2 + 1, b * 2 + 2, b + 1)[i])
                    nc.scalar.activation(XC[:, i, :], XC[:, i, :], ACT.Silu, bias=SMALL3[:, i:i + 1]).then_inc(xbc_act, 1)
                for i, cat in enumerate((BCAT, CCAT)):
                    if i == 0:
                        act.wait_ge(pe_conv_done[2], b * 2 + 1)
                    else:
                        act.wait_ge(c3_ready, b + 1)
                    for k in range(ND):
                        p = slice(64 * (k % 2), 64 * (k % 2) + 64)
                        nc.scalar.activation(cat[p, k // 2, :].rearrange("p (a c) -> p a c", a=SIDE),
                                             sequence((banks(BANK3[3]), C3)[i][p, :], k), ACT.Silu,
                                             bias=SMALL3[p, 3 + i:4 + i]).then_inc(xbc_act, 1)
                stage_end(act, b, 6)
                for s in range(SB):
                    act.wait_ge(g_ready, b * SB + (s + 1))
                    nc.scalar.activation(GT[:, TRI[s]:TRI[s + 1]], banks(2 * (s % 4))[:, 128 * s:T], ACT.Copy).then_inc(g_kept, 1)
                stage_end(act, b, 7)
                with act.Fori(0, HD) as j:
                    for k in range(ND):
                        h = b * 12 + j * 4
                        if k == 0:
                            act.wait_ge(diff_ready, b * (HD + 1) + j + 1)
                        act.wait_ge(y3_ready, h + (k + 1))
                        settle(act)
                        ins = nc.scalar.activation(EE[:, k % 2, :], DIFF, ACT.Exp, scale=A3[:, bass.ds(j + 3 * k, 1)])
                        ins.then_inc(e_ready, 1)
                stage_end(act, b, 8)
                for i in range(DB):
                    act.wait_ge(z_ready[1], b * DB + (i + 1))
                    nc.scalar.activation(Z3[:, i, :], banks((4, 6, 0)[i]), ACT.Silu).then_inc(z_act[1], 1)
                for i in range(DB):
                    act.wait_ge(gated[1], b * (2 * DB) + (i + 1))
                    nc.scalar.activation(SQ3[:, i * T:(i + 1) * T], YACC[:, i, :], ACT.Square).then_inc(squares[2], 1)
                layer_std(2, R3, 6, DI, EPS5[:, 0:1])
                stage_end(act, b, STAGES)
                st.end()

        @block.vector
        def _(dve):
            dve.wait_ge(a_exp_done, 2)
            dve.wait_ge(weights_in, 16 * len(WEIGHTS))
            nc.vector.tensor_scalar(A0[:, :], A0[:, :], -1.0, None, ALU.mult).then_inc(consts_ready, 1)
            nc.vector.tensor_scalar(A3[:, :], A3[:, :], -1.0, None, ALU.mult).then_inc(consts_ready, 1)
            nc.vector.tensor_scalar(D4[:, :], SMALL0[:, 2, :], 4.0, None, ALU.mult).then_inc(consts_ready, 1)
            nc.vector.tensor_reduce(DSUM[:, :], SMALL3[:, 20:32].rearrange("p (k j) -> p j k", k=ND), AX_X,
                                    ALU.add).then_inc(consts_ready, 1)
            dve.wait_ge(consts_ready, 9)
            with dve.Fori(0, NB) as b:
                st = Steps(dve, dve_steps, DVE_STEPS, b)
                v = nc.vector

                def group_norm(layer, to):
                    for c in range(CB):
                        for h in range(2):
                            ins = v.bn_stats(ST[:, c, h, :], X[:, c, h * HALF:(h + 1) * HALF])
                    st.done(ins)
                    settle(dve)
                    for c in range(CB):
                        ins = v.bn_aggr(MV[:, c, :], ST[:, c].rearrange("p h s -> p (h s)"))
                    st.done(ins)
                    st.done(v.tensor_tensor(GS[:, :, 1], MV[:, :, 0], MV[:, :, 0], ALU.mult))
                    v.tensor_copy(GS[:, :, 0], MV[:, :, 0])
                    v.tensor_tensor(GS[:, :, 1], GS[:, :, 1], MV[:, :, 1], ALU.add).then_inc(gn_stats, 1)
                    dve.wait_ge(gn_sums, b * 4 + (layer + 1))
                    st.done(v.tensor_copy(GM[:, :, :].rearrange("p c s -> p (c s)"), banks(0, 1, CP)[:, 0:2 * CB]))
                    st.done(v.tensor_tensor(GV[:, :, 0], GM[:, :, 0], GM[:, :, 0], ALU.mult))
                    v.tensor_tensor(GV[:, :, 0], GM[:, :, 1], GV[:, :, 0], ALU.subtract).then_inc(gn_var, 1)
                    dve.wait_ge(gn_std, b * 4 + (layer + 1))
                    st.done(v.reciprocal(GV[:, :, 0], GV[:, :, 0]))
                    for c in range(CB):
                        ins = v.tensor_scalar(to[c], grid(X[:, c, :]), GM[:, c, 0:1], GV[:, c, 0:1],
                                              ALU.subtract, ALU.mult)
                        if c == CB - 1:
                            ins.then_inc(xn_ready[layer], 1)

                def conv(to, pad, w, k, bias, sem_done, taps=None):
                    taps = taps or k * k
                    for t in range(taps):
                        view = pad[:, t // k:t // k + SIDE, t % k:t % k + SIDE]
                        if t == 0:
                            st.done(v.tensor_scalar(grid(to), view, w[:, 0:1], bias, ALU.mult, ALU.add)
                                    if bias is not None else v.tensor_scalar(grid(to), view, w[:, 0:1], None, ALU.mult))
                            continue
                        ins = v.scalar_tensor_tensor(grid(to), view, w[:, t:t + 1], grid(to), ALU.mult, ALU.add)
                        if t == taps - 1 and sem_done is not None:
                            ins.then_inc(sem_done, 1)
                        else:
                            st.done(ins)

                def softplus(scratch, to, exps, logs):
                    e, log, top, t, mask = scratch[:5]
                    dve.wait_ge(exps, b + 1)
                    v.tensor_scalar(mask, e, 2.0 ** -8, None, ALU.is_lt)
                    st.done(v.tensor_tensor(t, t, e, ALU.mult))
                    st.done(v.scalar_tensor_tensor(t, t, 1.0, e, ALU.add, ALU.mult))
                    dve.wait_ge(logs, b + 1)
                    settle(dve)
                    st.done(v.copy_predicated(log, mask.bitcast(U32), t))
                    return v.tensor_tensor(to, log, top, ALU.add)

                dve.wait_ge(x_in, b * 32 + 16)
                group_norm(0, [grid(XN[:, c, :]) for c in range(CB)])
                dve.wait_ge(pad_filled, b * DB + 1)
                conv(U[:, 0, :], PADX[:, 0], CONV0[:, 0, :], 3, None, conv_done)
                dve.wait_ge(pad_filled, b * DB + DB)
                conv(V2, PADX[:, 2], CONV0[:, 2, :], 3, None, None, len(TAPS0_DVE))
                dve.wait_ge(pool_conv_done[0], b + 1)
                v.tensor_tensor(U[:, 2, :], U[:, 2, :], V2, ALU.add).then_inc(conv_done, 1)
                dve.wait_ge(bc_ready, b + 1)
                v.tensor_copy(BCF, banks(0, 2, 2 * NS)).then_inc(bc_kept, 1)
                dve.wait_ge(bc_kept, b + 1)
                settle(dve)
                for part in range(3):
                    st.done(v.tensor_copy(BCH, BCF))
                    ins = v.tensor_copy(BCS[32 * part:32 * part + 32, :], BCH)
                    if part == 2:
                        ins.then_inc(bc_split, 1)
                    else:
                        if part == 0:
                            dve.wait_ge(c_stored, b * 16 + 16)
                        st.done(v.tensor_tensor(BCF, BCF, BCH, ALU.subtract))
                softplus(SPA, DT.rearrange("p d t -> p (d t)"), softplus_exps, softplus_logs).then_inc(dt_ready, 1)
                dve.wait_ge(dt_ready, b + 1)
                for k in range(4):
                    for i in range(DB):
                        if k == 2:
                            dve.wait_ge(dt_turned, b * DB + (i + 1))
                        src = DT[:, i, :] if k < 2 else SPA[0][:, i * T:(i + 1) * T]
                        to = S[:, i, k, :]
                        if k % 2:
                            src, to = src[:, ::-1], to[:, ::-1]
                        v.tensor_tensor_scan(to, src, src, 0.0, ALU.add, ALU.max)
                stage_end(dve, b, 1)

                def numerator(n, dtu, wait):
                    dve.wait_ge(b_row, wait)
                    v.tensor_tensor(NUM[:, n % 2, :], dtu.rearrange("p o t -> p (o t)"), banks(4), ALU.mult).then_inc(num_ready, 1)

                numerator(0, DTUX[:, 0:1, :], b * (DB * NS + 2) + 1)
                with dve.Fori(0, DB) as d:
                    u0 = b * (DB * NS) + d * NS

                    def weigh(n):
                        dve.wait_ge(hsum_ready, u0 + (n + 1))
                        dve.wait_ge(c_row[n % 2], b * (DB * NS * 8) + d * (NS * 8) + (n // 2 * 16 + 16))
                        if n % 2 == 0 and n > 0:
                            dve.wait_ge(ch_added, (b * DB + d) * (NS // 2 - 1) + n // 2)
                        v.tensor_tensor((CM, CM2)[n % 2], banks(2 * (n % 2)), CS[n % 2], ALU.mult).then_inc(ch_ready, 1)

                    def merge(n):
                        dve.wait_ge(ch_ready, u0 + (n + 3))
                        v.tensor_tensor(CM, CM, CM2, ALU.add).then_inc(products_merged, 1)

                    for n in range(NS):
                        nxt = DTUX[:, bass.ds(d, 1), :] if n < NS - 1 else DTUX[:, bass.ds(d + 1, 1), :]
                        numerator(n + 1, nxt, u0 + 2 * b + (n + 2))
                        for k in ORDER:
                            if k == 0:
                                dve.wait_ge(decay_ready, u0 + (n + 1))
                            if k == 3 and n % SHARE:
                                dve.wait_ge(drive3_ready, (b * DB + d) * (4 * NS - DRIVES) + (4 * n - drives(n) + 1))
                            else:
                                made = ORDER.index(k) if n % SHARE == 0 else k
                                dve.wait_ge(drive_ready, (b * DB + d) * DRIVES + (drives(n) + made + 7))
                            a, w = DEC[:, n % 4, k // 2, :], RING[:, (4 * n + k) % 8, :]
                            if k % 2:
                                a, w = a[:, ::-1], w[:, ::-1]
                            ins = v.tensor_tensor_scan(w, a, w, 0.0, ALU.mult, ALU.add)
                            ins.then_inc(h_ready, 1)
                            if k == 1 and n >= 1:
                                weigh(n - 1)
                            if k == 0 and n % SHARE:
                                dve.wait_ge(weight_ready, u0 * 2 + (2 * n + 2))
                                dve.wait_ge(num_ready, u0 + b + (n + 1))
                                slot = grid(RING[:, (4 * n + 3) % 8, :])
                                v.tensor_tensor(slot, slot, turned(NUM[:, n % 2, :]), ALU.mult).then_inc(drive3_ready, 1)
                            if k == 3 and n >= 2 and n % 2 == 0:
                                merge(n - 1)
                        dve.wait_ge(h_ready, u0 * 4 + (4 * n + 4))
                        dve.sem_inc(decay_free, 1)
                    weigh(NS - 1)
                    merge(NS - 1)
                    dve.wait_ge(products_merged, (b * DB + d) * (NS // 2) + NS // 2)
                    dve.wait_ge(ch_added, (b * DB + d) * (NS // 2 - 1) + (NS // 2 - 1))
                    settle(dve)
                    yd = Y0[:, bass.ds(d, 1), :].rearrange("p o t -> p (o t)")
                    v.tensor_tensor(yd, banks(6), CM, ALU.add).then_inc(y_ready, 1)
                stage_end(dve, b, 2)
                def center(i, to, first, n, h):
                    dve.wait_ge(mean_sum[i], b * 2 + (h + 1))
                    for k in range(to.shape[1]):
                        yk = to[:, k, h * HALF:(h + 1) * HALF]
                        ins = v.scalar_tensor_tensor(yk, PS[0:to.shape[0], first + h, :], -1.0 / n, yk, ALU.mult, ALU.add)
                    ins.then_inc(centered[i], 1)

                def normalize(i, to, gamma, r, h):
                    dve.wait_ge(centered[i], b * 2 + (h + 1))
                    dve.wait_ge(std_ready[i], b * 2 + (h + 1))
                    for k in range(to.shape[1]):
                        yk = to[:, k, h * HALF:(h + 1) * HALF]
                        ins = v.scalar_tensor_tensor(yk, yk, gamma[:, k:k + 1], r[:, h * HALF:(h + 1) * HALF], ALU.mult, ALU.mult)
                    st.done(ins)

                center(0, Y0, 0, DI, 0)
                dve.wait_ge(x_in, b * 32 + 32)
                for c in range(CB):
                    ins = v.tensor_scalar(XN[:, c, :], X[:, c, :], GM[:, c, 0:1], GV[:, c, 0:1], ALU.subtract, ALU.mult)
                ins.then_inc(xn_again, 1)
                center(0, Y0, 0, DI, 1)
                for h in range(2):
                    normalize(0, Y0, SMALL0[:, 3, :], R0, h)
                for h in range(2):
                    for i in range(DB):
                        dve.wait_ge(z_act[0], b * DB + (i + 1))
                        yi, zi = Y0[:, i, h * HALF:(h + 1) * HALF], Z0[:, i, h * HALF:(h + 1) * HALF]
                        ins = v.scalar_tensor_tensor(yi, yi, SMALL0[:, 4, i:i + 1], zi, ALU.add, ALU.mult)
                    ins.then_inc(gated[0], 1)

                def residual(layer, first=2):
                    for c in range(CB):
                        dve.wait_ge(layer_out[layer], b + 1 if layer == 0 else b * CB + (c + 1))
                        ins = v.tensor_tensor(X[:, c, :], X[:, c, :], banks(first + 2 * c, 2, CP), ALU.add)
                        if c == CB - 1 and layer < 3:
                            st.done(ins)
                    return ins

                residual(0)
                stage_end(dve, b, 3)
                dve.wait_ge(pads_clear, b * 4 + 2)
                group_norm(1, [inner(PAD1[:, c], K1) for c in range(CB)])
                dve.wait_ge(xn_ready[1], b + 1)
                for c in range(CB):
                    conv(Y1[:, c, :], PAD1[:, c], DW1[:, c, :], K1, SMALL1[:, 0, c:c + 1], None, len(TAPS_DVE))
                dve.wait_ge(pool_conv_done[1], b * CB + CB)
                for c in range(CB):
                    st.done(v.tensor_tensor(Y1[:, c, :], Y1[:, c, :], YP1[:, c, :], ALU.add))
                dve.wait_ge(pe_conv_done[1], b + 1)
                for c in range(CB):
                    ins = v.tensor_tensor(Y1[:, c, :], Y1[:, c, :], banks(4 + 2 * c, 2, CP), ALU.add)
                ins.then_inc(ln1_ready, 1)
                dve.wait_ge(ln1_ready, b * 3 + 1)
                for h in range(2):
                    center(1, Y1, 0, C, h)
                for h in range(2):
                    normalize(1, Y1, SMALL1[:, 1, :], R1, h)
                    for c in range(CB):
                        yc = Y1[:, c, h * HALF:(h + 1) * HALF]
                        ins = v.tensor_scalar(yc, yc, SMALL1[:, 2, c:c + 1], None, ALU.add)
                    ins.then_inc(ln1_ready, 1)
                for c in range(CB):
                    dve.wait_ge(layer_out[1], b * CB + (c + 1))
                    st.done(v.tensor_scalar(O1[:, c, :], banks(2 * c, 2, CP), SMALL1[:, 3, c:c + 1], SMALL1[:, 4, c:c + 1],
                                            ALU.add, ALU.mult))
                    st.done(v.tensor_tensor(X[:, c, :], X[:, c, :], O1[:, c, :], ALU.add))
                stage_end(dve, b, 4)
                dve.wait_ge(pads_clear, b * 4 + 3)
                group_norm(2, [inner(PAD2[:, c], 3) for c in range(CB)])
                residual(2)
                stage_end(dve, b, 5)
                group_norm(3, [grid(XN[:, c, :]) for c in range(CB)])
                dve.wait_ge(dt3_ready, b + 1)
                v.tensor_tensor(SPB[5].rearrange("p (j s) -> p s j", j=HD), banks(0, 1)[:, 0:HD * SB].rearrange("p (s j) -> p s j", j=HD),
                                SMALL3[:, 5:8].unsqueeze(1).to_broadcast([128, SB, HD]), ALU.add).then_inc(dtv_ready, 1)
                st.done(softplus(SPB, DTS, softplus_exps3, softplus_logs3))
                by_block = "p (s q) -> p s q"
                eye = IDENT[:, :].unsqueeze(1).to_broadcast([128, SB, 128])
                for j in range(HD):
                    v.tensor_tensor(SPREAD[:, j, :].rearrange(by_block, s=SB), eye,
                                    DTS[:, j * SB:(j + 1) * SB].unsqueeze(2).to_broadcast([128, SB, 128]),
                                    ALU.mult).then_inc(spread_ready, 1)
                for i in range(2):
                    dve.wait_ge(pad3_filled, b * 5 + (i + 1))
                    conv(XC[:, i, :], PAD3[:, i], CONV3[:, i, :], 3, None, conv3_done)
                dve.wait_ge(pad3_filled, b * 5 + 5)
                conv(C3, PAD3[:, 4], CONV3[:, 4, :], 3, None, None, len(TAPS3_DVE))
                for j in range(HD):
                    if j == HD - 1:
                        dve.wait_ge(pe_conv_done[2], b * 2 + 2)
                        v.tensor_tensor(C3, C3, banks(BANK3[4]), ALU.add).then_inc(c3_ready, 1)
                    dve.wait_ge(row_ready, b * HD + (j + 1))
                    v.tensor_tensor_scan(CUM[:, j, :], banks(0), SPREAD[:, j, :], 0.0, ALU.add, ALU.max).then_inc(cum_ready, 1)
                    dve.wait_ge(cum_ready, b * HD + (j + 1))
                    diag = SPREAD[:, j, :].rearrange(by_block, s=SB)
                    st.done(v.tensor_tensor(diag, CUM[:, j, :].rearrange(by_block, s=SB), eye, ALU.mult))
                    st.done(v.tensor_reduce(CUMS[:, j * SB:(j + 1) * SB], diag, AX_X, ALU.add))
                stage_end(dve, b, 6)
                for s in range(SB):
                    dve.wait_ge(g_kept, b * SB + (s + 1))
                    diag = GT[:, TRI[s]:TRI[s] + 128]
                    v.tensor_tensor(diag, diag, TRIM[:, :], ALU.mult)
                stage_end(dve, b, 7)

                def differences(j):
                    for s in range(SB):
                        cum = CUMX[:, bass.ds(j, 1), 128 * s:T].rearrange("p o t -> p (o t)")
                        ins = v.tensor_scalar(DIFF[:, TRI[s]:TRI[s + 1]], cum, CUMS[:, bass.ds(j * SB + s, 1)], 0.0,
                                              ALU.subtract, ALU.max)
                    ins.then_inc(diff_ready, 1)

                differences(0)
                with dve.Fori(0, HD) as j:

                    def collect(k):
                        dve.wait_ge(y3_ready, b * 12 + j * 4 + (k + 3))
                        ya = YACC[:, bass.ds(j, 1), :].rearrange("p o t -> p (o t)")
                        xc = XC[:, bass.ds(j, 1), :].rearrange("p o t -> p (o t)")
                        y = banks(2 * (k % 2)).rearrange("p (a c) -> p a c", a=SIDE)
                        if k >= 2:
                            y = y[:, ::-1, ::-1]
                        if k == 0:
                            ins = v.scalar_tensor_tensor(grid(ya), grid(xc), DSUM[:, bass.ds(j, 1)], y, ALU.mult, ALU.add)
                        else:
                            dve.wait_ge(yacc_added, b * 12 + j * 4 + (k + 2))
                            to = (grid, turned)[k % 2](ya)
                            ins = v.tensor_tensor(to, to, y, ALU.add)
                        ins.then_inc(yacc_added, 1)

                    for k in range(ND):
                        h = b * 12 + j * 4
                        dve.wait_ge(xt_ps, h + (k + 1))
                        dve.wait_ge(y3_ready, h + (k + 1))
                        v.tensor_tensor(XT[:, k % 2, :].rearrange("p (s q) -> p s q", s=SB),
                                        banks(4 + 2 * (k % 2)).rearrange("p (s q) -> p s q", s=SB),
                                        DTS[:, bass.ds(j * SB, SB)].unsqueeze(2).to_broadcast([128, SB, 128]),
                                        ALU.mult).then_inc(xt_ready, 1)
                        dve.wait_ge(e_ready, h + (k + 1))
                        v.tensor_tensor(EE[:, k % 2, :], EE[:, k % 2, :], GT, ALU.mult).then_inc(m_ready, 1)
                        if k == ND - 1:
                            differences(j + 1)
                        if k >= 1:
                            collect(k - 1)
                    collect(ND - 1)
                stage_end(dve, b, 8)
                for i in range(DB):
                    dve.wait_ge(z_act[1], b * DB + (i + 1))
                    v.tensor_tensor(YACC[:, i, :], YACC[:, i, :], Z3[:, i, :], ALU.mult).then_inc(gated[1], 1)
                for i in range(DB):
                    dve.wait_ge(gated[1], b * (2 * DB) + (DB + i))
                    v.tensor_scalar(Z3[:, i, :], YACC[:, i, :], SMALL3[:, 32 + i:33 + i], None, ALU.mult).then_inc(gated[1], 1)
                dve.wait_ge(std_ready[2], b * 2 + 2)
                for c in range(CB):
                    dve.wait_ge(layer_out[3], b * CB + (c + 1))
                    st.done(v.tensor_tensor(O3[:, c, :], banks(2 + 2 * c, 2, CP), R3[0:CP, :], ALU.mult))
                    v.tensor_tensor(X[:, c, :], X[:, c, :], O3[:, c, :], ALU.add).then_inc(x_final, 1)
                stage_end(dve, b, STAGES)
                st.end()

        @block.tensor
        def _(pe):
            pe.wait_ge(weights_in, 16 * len(WEIGHTS))
            pe.wait_ge(consts_ready, 9)
            pe.drain().then_inc(decay_free, 4)
            pe.drain().then_inc(ring_free, 8)
            pe.drain().then_inc(drive_ready, 6)
            pe.drain().then_inc(ch_ready, 2)
            pe.drain().then_inc(xj_used, 1)
            pe.drain().then_inc(y3_ready, 2)
            pe.drain().then_inc(xt_ready, 2)
            pe.drain().then_inc(prod_used, 2)
            pe.drain().then_inc(y_ready, 1)
            pe.drain().then_inc(yacc_added, 2)
            with pe.Fori(0, NB) as b:
                def mm(to, w, x, start=True, stop=True):
                    return nc.tensor.matmul(to, w, x, start=start, stop=stop)

                def project(first, p, w, x, kb):
                    for h in range(2):
                        for i in range(kb):
                            ins = mm(PS[0:p, first + h, :], w(i), x(i, h), i == 0, i == kb - 1)
                    return ins

                def cols(ap, h):
                    return ap[:, h * HALF:(h + 1) * HALF]

                def group_sums(layer):
                    pe.wait_ge(gn_stats, b * 4 + (layer + 1))
                    mm(PS[0:CP, 0, 0:2 * CB], GROUP[:, :], GS[:, :, :].rearrange("p c s -> p (c s)")).then_inc(gn_sums, 1)

                def sums(first, p, of, kb):
                    return project(first, p, lambda i: ONES[0:p, 0:p], lambda i, h: cols(of(i), h), kb)

                def diagonal_conv(first, p, diag, pad, taps, k):
                    for h in range(2):
                        for i, t in enumerate(taps):
                            view = pad[:, 16 * h + t // k:16 * h + t // k + 16, t % k:t % k + SIDE]
                            ins = mm(PS[0:p, first + h, :], diag[:, i, :], view, i == 0, i == len(taps) - 1)
                    return ins

                group_sums(0)
                pe.wait_ge(xn_ready[0], b + 1)
                for d in range(DB):
                    project(2 * d, 128, lambda i: WIN[:, i, 128 * d:128 * d + 128],
                            lambda i, h: cols(XN[:, i, :], h), CB).then_inc(xval_ready, 1)
                pe.wait_ge(diags_ready[0], b + 1)
                pe.wait_ge(pad_filled, b * DB + 2)
                diagonal_conv(6, 128, DIAG0[:, 0], PADX[:, 1], range(9), 3).then_inc(pe_conv_done[0], 1)
                pe.wait_ge(u_ready, b * DB + DB)
                pe.wait_ge(step_weights_in, b * 32 + 32)
                project(6, RANK, lambda i: WX[:, i, 0:RANK], lambda i, h: cols(U[:, i, :], h), DB).then_inc(dtr_ready, 1)
                project(0, 2 * NS, lambda i: WX[:, i, RANK:RANK + 2 * NS], lambda i, h: cols(U[:, i, :], h), DB).then_inc(bc_ready, 1)
                pe.wait_ge(dtr_copied, b + 1)
                for d in range(DB):
                    ins = project(2 + 2 * d, 128, lambda i: WDT[:, 128 * d:128 * d + 128], lambda i, h: cols(DTR, h), 1)
                ins.then_inc(dtp_ready, 1)
                pe.wait_ge(bc_split, b + 1)
                stage_end(pe, b, 1)

                def row(first, r):
                    return project(first, 128, lambda i: ONEHOT[:, r, :], lambda i, h: cols(BCS, h), 1)

                row(4, 0).then_inc(b_row, 1)
                pe.wait_ge(num_ready, b * (DB * NS + 1) + 1)
                row(4, 1).then_inc(b_row, 1)
                with pe.Fori(0, DB) as d:
                    u0 = b * (DB * NS) + d * NS

                    for n in range(NS):
                        pe.wait_ge(ch_ready, u0 + (n + 1))
                        for i, k in enumerate(ORDER):
                            pe.wait_ge(h_ready, u0 * 4 + (4 * n + i + 1))
                            state = RING[:, (4 * n + k) % 8, :]
                            for h in range(2):
                                if k < 2:
                                    src = cols(state, h)
                                else:
                                    src = state.rearrange("p (w h) -> p h w", w=SIDE)[:, 16 * h:16 * h + 16, :]
                                ins = mm(PS[:, 2 * (n % 2) + h, :], IDENT[:, :], src, i == 0, i == 3)
                            ins.then_inc(ring_free, 1)
                            if i == 0:
                                pe.wait_ge(num_ready, u0 + b + (n + 2))
                                row(4, (n + 2) % NS).then_inc(b_row, 1)
                        if n >= 2 and n % 2 == 0:
                            if n == 2:
                                pe.wait_ge(y_ready, b * DB + d + 1)
                            if n == 8:
                                pe.wait_ge(skips_ready, b * DB + d + 1)
                                for h in range(2):
                                    mm(PS[:, 6 + h, :], IDENT[:, :], cols(YD, h), False, False)
                            pe.wait_ge(products_merged, (b * DB + d) * (NS // 2) + n // 2)
                            for h in range(2):
                                ins = mm(PS[:, 6 + h, :], IDENT[:, :], cols(CM, h), n == 2, n == NS - 2)
                            ins.then_inc(ch_added, 1)
                        pe.wait_ge(ring_free, u0 * 4 + (4 * n + 12))
                        pe.sem_inc(hsum_ready, 1)
                stage_end(pe, b, 2)
                def half_sums(first, p, of, kb, h):
                    for i in range(kb):
                        ins = mm(PS[0:p, first + h, :], ONES[0:p, 0:p], cols(of[:, i, :], h), i == 0, i == kb - 1)
                    return ins

                def means_and_squares(n, p, of, squared, kb, between):
                    for h in range(2):
                        half_sums(0, p, of, kb, h).then_inc(mean_sum[n], 1)
                    between()
                    for h in range(2):
                        pe.wait_ge(squares[n], b * 2 + (h + 1))
                        half_sums(2, p, squared, kb, h).then_inc(square_sum[n], 1)

                def gate(d):
                    return project((4, 6, 0)[d], 128, lambda i: WIN[:, i, DI + 128 * d:DI + 128 * d + 128],
                                   lambda i, h: cols(XN[:, i, :], h), CB).then_inc(z_ready[0], 1)

                def first_gate():
                    pe.wait_ge(xn_again, b + 1)
                    gate(0)

                means_and_squares(0, 128, Y0, SQ0, DB, first_gate)
                for d in range(1, DB):
                    gate(d)

                pe.wait_ge(wout_in, b * 16 + 16)
                for h in range(2):
                    pe.wait_ge(gated[0], b * 2 + (h + 1))
                    for c in range(CB):
                        for i in range(DB):
                            ins = mm(PS[0:CP, 2 + 2 * c + h, :], WOUT[:, i, CP * c:CP * c + CP], cols(Y0[:, i, :], h),
                                     i == 0, i == DB - 1)
                ins.then_inc(layer_out[0], 1)
                stage_end(pe, b, 3)
                pe.wait_ge(late_weights_in, b * (16 * len(LATE)) + 16 * len(LATE))
                group_sums(1)
                pe.wait_ge(xn_ready[1], b + 1)
                pe.wait_ge(diags_ready[1], b + 1)
                for c in range(CB):
                    ins = diagonal_conv(4 + 2 * c, CP, DIAG1[:, c], PAD1[:, c], TAPS_PE, K1)
                ins.then_inc(pe_conv_done[1], 1)
                pe.wait_ge(ln1_ready, b * 3 + 1)
                means_and_squares(1, CP, Y1, SQ1, CB, lambda: None)
                for m in range(MB):
                    if m >= 2:
                        pe.wait_ge(gelu_done, b * MB + (m - 1))
                    for h in range(2):
                        if m == 0:
                            pe.wait_ge(ln1_ready, b * 3 + (h + 2))
                        for i in range(CB):
                            ins = mm(PS[:, 4 + 2 * (m % 2) + h, :], W0[:, i, 128 * m:128 * m + 128], cols(Y1[:, i, :], h),
                                     i == 0, i == CB - 1)
                    ins.then_inc(hidden_ready, 1)
                for c in range(CB):
                    for h in range(2):
                        for m in range(MB):
                            if c == 0 and h == 0:
                                pe.wait_ge(gelu_done, b * MB + (m + 1))
                            ins = mm(PS[0:CP, 2 * c + h, :], W1[:, m, CP * c:CP * c + CP], cols(G1[:, m, :], h),
                                     m == 0, m == MB - 1)
                    ins.then_inc(layer_out[1], 1)
                stage_end(pe, b, 4)
                group_sums(2)
                pe.wait_ge(xn_ready[2], b + 1)
                for c in range(CB):
                    for h in range(2):
                        for i in range(CB):
                            for t, (y, xx) in enumerate(TAPS2):
                                ins = mm(PS[0:CP, 2 + 2 * c + h, :], KE[:, i, t, CP * c:CP * c + CP],
                                         PAD2[:, i, 16 * h + y:16 * h + y + 16, xx:xx + SIDE],
                                         i == 0 and t == 0, i == CB - 1 and t == len(TAPS2) - 1)
                    ins.then_inc(layer_out[2], 1)
                stage_end(pe, b, 5)
                group_sums(3)
                pe.wait_ge(xn_ready[3], b + 1)

                def in3(first, blk):
                    return project(first, 128, lambda i: WIN3[:, i, 128 * blk:128 * blk + 128],
                                   lambda i, h: cols(XN[:, i, :], h), CB)

                for i in range(SB):
                    for c in range(CB):
                        ins = mm(PS[:, 0, HD * i:HD * i + HD], XN[:, c, 128 * i:128 * i + 128], WDT3[:, c, :], c == 0, c == CB - 1)
                ins.then_inc(dt3_ready, 1)
                for i in range(5):
                    if i >= 3:
                        pe.wait_ge(pad3_filled, b * 5 + (i - 2))
                    in3(BANK3[i], i).then_inc(xbc_ready, 1)

                def spread_row(j):
                    pe.wait_ge(spread_ready, b * HD + (j + 1))
                    if j >= 1:
                        pe.wait_ge(cum_ready, b * HD + j)
                    sums(0, 128, lambda i: SPREAD[:, j, :], 1).then_inc(row_ready, 1)

                pe.wait_ge(diags_ready[2], b + 1)
                spread_row(0)
                pe.wait_ge(pad3_filled, b * 5 + 5)
                for i in (3, 4):
                    taps = range(9) if i == 3 else TAPS3_PE
                    diagonal_conv(BANK3[i], 128, DIAG3[:, i - 3, taps[0]:9], PAD3[:, i], taps, 3).then_inc(pe_conv_done[2], 1)
                    spread_row(i - 2)
                pe.wait_ge(xbc_act, b * 11 + 11)
                stage_end(pe, b, 6)
                for s in range(SB):
                    if s >= 4:
                        pe.wait_ge(g_kept, b * SB + (s - 3))
                    for h in range(2):
                        lo, hi = max(HALF * h, 128 * s), HALF * (h + 1)
                        if lo >= hi:
                            continue
                        for c in range(2):
                            ins = mm(PS[:, 2 * (s % 4) + h, lo - HALF * h:HALF], BCAT[:, c, 128 * s:128 * s + 128],
                                     CCAT[:, c, lo:hi], c == 0, c == 1)
                    ins.then_inc(g_ready, 1)
                stage_end(pe, b, 7)
                with pe.Fori(0, HD) as j:
                    def outputs(k):
                        h0 = b * 12 + j * 4
                        pe.wait_ge(m_ready, h0 + (k + 1))
                        pe.wait_ge(xt_ready, h0 + (k + 3))
                        pe.wait_ge(yacc_added, h0 + (k + 1))
                        for h in range(2):
                            for s in range(4 * h + 4):
                                lo = max(HALF * h, 128 * s)
                                at = TRI[s] + lo - 128 * s
                                ins = mm(PS[:, 2 * (k % 2) + h, lo - HALF * h:HALF], XT[:, k % 2, 128 * s:128 * s + 128],
                                         EE[:, k % 2, at:at + HALF * (h + 1) - lo], s == 0, s == 4 * h + 3)
                        ins.then_inc(y3_ready, 1)

                    for k in range(ND):
                        pe.wait_ge(xj_ready, (b * HD + j) * ND + (k + 1))
                        pe.wait_ge(xt_ready, b * 12 + j * 4 + (k + 1))
                        for s in range(SB):
                            src = XJ[:, k, 128 * s:128 * s + 128]
                            ins = nc.tensor.transpose(banks(4 + 2 * (k % 2))[:, 128 * s:128 * s + 128], src, IDENT[:, :])
                        ins.then_inc(xt_ps, 1)
                        if k == ND - 1:
                            pe.wait_ge(xt_ps, b * 12 + j * 4 + 4)
                            pe.sem_inc(xj_used, 1)
                        if k >= 1:
                            outputs(k - 1)
                    outputs(ND - 1)
                stage_end(pe, b, 8)
                for d in range(DB):
                    project((4, 6, 0)[d], 128, lambda i: WZ3[:, i, 128 * d:128 * d + 128],
                            lambda i, h: cols(XN[:, i, :], h), CB).then_inc(z_ready[1], 1)
                pe.wait_ge(squares[2], b * DB + DB)
                for h in range(2):
                    half_sums(6, 128, SQ3.rearrange("p (d t) -> p d t", d=DB), DB, h).then_inc(square_sum[2], 1)
                pe.wait_ge(gated[1], b * (2 * DB) + 2 * DB)
                for c in range(CB):
                    project(2 + 2 * c, CP, lambda i: WOUT3[:, i, CP * c:CP * c + CP],
                            lambda i, h: cols(Z3[:, i, :], h), DB).then_inc(layer_out[3], 1)
                stage_end(pe, b, STAGES)


def kernel(**inputs):
    import ml_dtypes
    import numpy as np
    import concourse.bacc as bacc
    from concourse import mybir as mb
    from concourse.bass_utils import run_bass_kernel_spmd as run

    a = {k: np.asarray(v) for k, v in inputs.items()}

    def cols(v, p):
        return np.ascontiguousarray(v.reshape(-1, p).T)

    def rows(w, p):
        return w.reshape(-1, p, w.shape[1]).transpose(1, 0, 2)

    def on_all(v):
        return np.broadcast_to(v.reshape(1, -1), (128, v.size))

    h = {}
    h["x"] = a["x"].reshape(NB, T, CB, CP).transpose(0, 3, 2, 1)
    h["win"] = rows(a["L0_conv_W_in"], CP)
    h["conv0"] = rows(a["L0_conv_conv_w"].reshape(DI, 9), 128)
    h["small0"] = np.stack([cols(a["L0_conv_" + n], 128) for n in ("conv_b", "b_dt", "D_param", "gamma", "beta")], 1)
    h["alog0"] = rows(a["L0_conv_A_log"], 128).reshape(128, DB * NS)
    h["wx"] = rows(a["L0_conv_W_x"], 128)
    h["wdt"] = a["L0_conv_W_dt"]
    h["wout"] = rows(a["L0_conv_W_out"], 128)
    h["dw1"] = rows(a["L1_conv_dw_kernel"].reshape(K1 * K1, C).T, CP)
    h["small1"] = np.stack([cols(a["L1_conv_" + n], CP) for n in ("dw_bias", "ln_gamma", "ln_beta", "b1", "gamma")], 1)
    h["w0"] = rows(a["L1_conv_w0"], CP)
    h["b0"] = cols(a["L1_conv_b0"], 128)
    h["w1"] = rows(a["L1_conv_w1"], 128)
    k2 = a["L2_conv_kernel"]
    grp = 12
    near = np.array([[2, 1], [1, 2], [0, 2], [0, 1], [1, 0], [2, 0]])
    k6, s6 = np.arange(grp) % 6, np.arange(grp) // 6
    sign = np.where(s6 == 0, 1, -1)
    act = (k6[:, None] + sign[:, None] * np.arange(6)[None, :]) % 6
    mult = (k6[:, None] + sign[:, None] * k6[None, :]) % 6 + 6 * (s6[:, None] ^ s6[None, :])
    py, px = np.ones((grp, 7), int), np.ones((grp, 7), int)
    py[:, 1:], px[:, 1:] = near[act][:, :, 0], near[act][:, :, 1]
    gg, tt, hh = np.meshgrid(np.arange(grp), np.arange(7), np.arange(grp), indexing="ij")
    full = np.zeros((3, 3, grp, 16, grp, 16), k2.dtype)
    full[py[gg, tt], px[gg, tt], mult[gg, hh], :, gg, :] = k2[tt, hh]
    full = full.reshape(3, 3, C, C)
    h["ke"] = np.stack([full[y, x].reshape(CB, CP, C) for y, x in TAPS2], 0).transpose(2, 1, 0, 3)
    w3 = a["L3_conv_in_proj_w"].T
    xs, bs, cs, dts = w3[:, DI:2 * DI], w3[:, 2 * DI:2 * DI + 64], w3[:, 2 * DI + 64:2 * DI + 128], w3[:, 2 * DI + 128:]
    h["win3"] = rows(np.concatenate([xs, bs, bs, cs, cs], 1), CP)
    h["wdt3"] = rows(dts, CP)
    h["wz3"] = rows(w3[:, :DI], CP)

    def doubled(v):
        return np.concatenate([v[:DI], v[DI:DI + 64], v[DI:DI + 64], v[DI + 64:], v[DI + 64:]], 0)

    h["conv3"] = rows(doubled(a["L3_conv_conv_w"].reshape(DI + 128, 9)), 128)
    h["small3"] = np.concatenate([cols(doubled(a["L3_conv_conv_b"]), 128), on_all(a["L3_conv_dt_bias"]), on_all(a["L3_conv_A_log"]),
                                  on_all(a["L3_conv_Ds"]), cols(a["L3_conv_norm_w"], 128)], 1)
    h["wout3"] = rows(a["L3_conv_out_proj_w"].T, 128)
    h["ident"] = np.eye(128, dtype=np.float32)
    h["group"] = (np.kron(np.eye(CP // 6), np.ones((6, 6))) / 6).astype(np.float32)
    h["tri"] = np.triu(np.ones((128, 128), np.float32))
    pick = np.tile(np.eye(2 * NS, NS, dtype=np.float32), (3, 1))
    h["onehot"] = np.repeat(pick[:, :, None], 128, 2).astype(ml_dtypes.bfloat16)

    nc = bacc.Bacc("TRN2", target_bir_lowering=False, num_devices=1)
    arrays, args = {}, []
    for name in ("x", "win", "conv0", "small0", "alog0", "wx", "wdt", "wout", "dw1", "small1", "w0", "b0", "w1", "ke",
                 "win3", "conv3", "small3", "wz3", "wout3", "wdt3", "ident", "group", "tri", "onehot"):
        v = np.ascontiguousarray(h[name])
        arrays[f"in_{name}"] = v
        args.append(nc.dram_tensor(f"in_{name}", v.shape, mb.dt.from_np(v.dtype), kind="ExternalInput").ap())
    args.append(nc.dram_tensor("out_x", (NB, CP, CB, T), F32, kind="ExternalOutput").ap())
    args.append(nc.dram_tensor("c_rows", (NS, T), F32, kind="Internal").ap())
    build(nc, *args)
    r = run(nc, [arrays], core_ids=[0])
    got = r.results[0]["out_x"]
    return got.transpose(0, 3, 2, 1).reshape(NB, SIDE, SIDE, C)
```
